# Optimizing a Trainium2 kernel written in Bass

```python
import numpy as np
import jax
import jax.numpy as jnp

def _softmax(x, axis=-1):
    return jax.nn.softmax(x, axis=axis)

def _gelu(x):
    return jax.nn.gelu(x, approximate=True)

def _silu(x):
    return jax.nn.silu(x)

def _sigmoid(x):
    return jax.nn.sigmoid(x)

def _layernorm(x, axis=-1, eps=1e-05):
    m = jnp.mean(x, axis=axis, keepdims=True)
    v = jnp.var(x, axis=axis, keepdims=True)
    return (x - m) / jnp.sqrt(v + eps)

def _scatter_add(tgt, idx, src, axis=0):
    return tgt.at[idx].add(src)

def _segment_sum(src, seg, n):
    return jax.ops.segment_sum(src, seg, n)
kernel_name = 'mk_decoder_postln_d4_seqx_r8_ed93b0'

def setup_inputs(seed: int=0):
    np.random.seed(seed)
    _w = jnp.asarray

    def _rec_inputs():
        import jax
        import jax.numpy as jnp
        _rk = jax.random.key(seed)
        x = 7.22e-05 + 1 * jax.random.normal(jax.random.fold_in(_rk, 1), (4, 512, 128), jnp.float32)
        _lenS = 512 - jax.random.randint(jax.random.fold_in(_rk, 7), (4,), 0, max(1, 512 // 4) + 1, jnp.int32)
        _lenS2 = 77 - jax.random.randint(jax.random.fold_in(_rk, 8), (4,), 0, max(1, 77 // 4) + 1, jnp.int32)
        _ctx_768P = jax.random.normal(jax.random.fold_in(_rk, 11), (4, 16, 96), jnp.float32)
        _ctx_768c = jax.random.dirichlet(jax.random.fold_in(_rk, 511), 0.3 * jnp.ones((16,), jnp.float32), (4, 77))
        _ctx_768t = jnp.einsum('bsk,bkd->bsd', _ctx_768c, _ctx_768P)
        _ctx_768t = _ctx_768t * jax.lax.rsqrt(jnp.mean(jnp.square(_ctx_768t)) + 1e-12) * 0.953939
        ctx_768 = -0.000191848 + 0.999787 * (_ctx_768t + 0.3 * jax.random.normal(jax.random.fold_in(_rk, 611), (4, 77, 96), jnp.float32))
        return (x, ctx_768)
    x, ctx_768 = _rec_inputs()

    def _L0_attn_setup():
        import jax, jax.numpy as jnp
        import numpy as np
        DIM = 128
        NUM_HEADS = 16
        HEAD_DIM = DIM // NUM_HEADS
        TAU = 2.0
        V_TH = 1.0
        BN_EPS = 1e-05

        def _branch(x, W, gamma, beta):
            B, N, D = x.shape
            h = jnp.einsum('bnd,ed->bne', x, W)
            hf = h.reshape(B * N, D)
            mean = jnp.mean(hf, axis=0)
            var = jnp.var(hf, axis=0)
            hn = (hf - mean) * jax.lax.rsqrt(var + BN_EPS) * gamma + beta
            hn = hn.reshape(B, N, D)
            return jax.nn.sigmoid(4.0 * (hn - V_TH))

        def _heads(x):
            B, N, D = x.shape
            return x.reshape(B, N, NUM_HEADS, HEAD_DIM).transpose(0, 2, 1, 3)
        key = jax.random.key(seed)
        ks = jax.random.split(key, 12)
        B, N, D = (8, 512, DIM)
        s = 0.02
        return {'x': jax.random.normal(ks[0], (B, N, D), dtype=jnp.float32), 'Wq': jax.random.normal(ks[1], (D, D), dtype=jnp.float32) * s, 'gq': jnp.ones((D,), jnp.float32), 'bq': jnp.zeros((D,), jnp.float32), 'Wk': jax.random.normal(ks[2], (D, D), dtype=jnp.float32) * s, 'gk': jnp.ones((D,), jnp.float32), 'bk': jnp.zeros((D,), jnp.float32), 'Wv': jax.random.normal(ks[3], (D, D), dtype=jnp.float32) * s, 'gv': jnp.ones((D,), jnp.float32), 'bv': jnp.zeros((D,), jnp.float32), 'Wp': jax.random.normal(ks[4], (D, D), dtype=jnp.float32) * s, 'bp': jnp.zeros((D,), jnp.float32)}
    _L0_attn_all = _L0_attn_setup()
    _L0_attn_in = {k: v for k, v in _L0_attn_all.items() if k in ('Wq', 'gq', 'bq', 'Wk', 'gk', 'bk', 'Wv', 'gv', 'bv', 'Wp', 'bp')}
    del _L0_attn_all

    def _L0_xattn_setup():
        import jax, jax.numpy as jnp
        import numpy as np
        N_HEADS = 16
        key = jax.random.key(seed)
        ks = jax.random.split(key, 8)
        b, l, m = (8, 128, 128)
        d_embed, d_cross = (128, 96)
        s_q = 1.0 / np.sqrt(d_embed)
        s_kv = 1.0 / np.sqrt(d_cross)
        return {'x': jax.random.normal(ks[0], (b, l, d_embed), jnp.float32), 'y': jax.random.normal(ks[1], (b, m, d_cross), jnp.float32), 'Wq': jax.random.normal(ks[2], (d_embed, d_embed), jnp.float32) * s_q, 'bq': jax.random.normal(ks[3], (d_embed,), jnp.float32) * 0.01, 'Wkv': jax.random.normal(ks[4], (2 * d_embed, d_cross), jnp.float32) * s_kv, 'bkv': jax.random.normal(ks[5], (2 * d_embed,), jnp.float32) * 0.01, 'Wo': jax.random.normal(ks[6], (d_embed, d_embed), jnp.float32) * s_q, 'bo': jax.random.normal(ks[7], (d_embed,), jnp.float32) * 0.01}
    _L0_xattn_all = _L0_xattn_setup()
    _L0_xattn_in = {k: v for k, v in _L0_xattn_all.items() if k in ('Wq', 'bq', 'Wkv', 'bkv', 'Wo', 'bo')}
    del _L0_xattn_all

    def _L0_ffn_setup():
        import jax, jax.numpy as jnp
        import numpy as np
        EPS = 1e-05
        NUM_HEADS = 16
        NUM_KV_HEADS = 4
        NUM_EXPERTS = 8
        TOP_K = 2

        def _layernorm(x, w, b):
            mu = jnp.mean(x, axis=-1, keepdims=True)
            var = jnp.mean((x - mu) ** 2, axis=-1, keepdims=True)
            return (x - mu) * jax.lax.rsqrt(var + EPS) * w + b
        key = jax.random.key(seed)
        ks = jax.random.split(key, 8)
        S, B, H = (128, 4, 128)
        F = 256
        hd = H // NUM_HEADS
        qkv_out = (NUM_HEADS + 2 * NUM_KV_HEADS) * hd
        w_scale = 0.02
        return {'hidden_states': jax.random.normal(ks[0], (S, B, H), jnp.float32), 'ln1_weight': jnp.ones((H,), jnp.float32), 'ln1_bias': jnp.zeros((H,), jnp.float32), 'ln2_weight': jnp.ones((H,), jnp.float32), 'ln2_bias': jnp.zeros((H,), jnp.float32), 'qkv_weight': jax.random.normal(ks[1], (qkv_out, H), jnp.float32) * w_scale, 'proj_weight': jax.random.normal(ks[2], (H, H), jnp.float32) * w_scale, 'router_weight': jax.random.normal(ks[3], (NUM_EXPERTS, H), jnp.float32) * w_scale, 'moe_w1': jax.random.normal(ks[4], (NUM_EXPERTS, H, F), jnp.float32) * w_scale, 'moe_w2': jax.random.normal(ks[5], (NUM_EXPERTS, F, H), jnp.float32) * w_scale}
    _L0_ffn_all = _L0_ffn_setup()
    _L0_ffn_in = {k: v for k, v in _L0_ffn_all.items() if k in ('ln1_weight', 'ln1_bias', 'ln2_weight', 'ln2_bias', 'qkv_weight', 'proj_weight', 'router_weight', 'moe_w1', 'moe_w2')}
    del _L0_ffn_all

    def _L1_attn_setup():
        import jax, jax.numpy as jnp
        import numpy as np
        B, T, D, N = (4, 128, 128, 16)

        def _depthwise_conv3_same(x, w, b):
            xp = jnp.pad(x, ((0, 0), (1, 1), (0, 0)))
            return xp[:, :-2] * w[:, 0] + xp[:, 1:-1] * w[:, 1] + xp[:, 2:] * w[:, 2] + b

        def _selective_scan(x, A, Wb, bb, Wc, bc, Wdt, bdt):
            dt = jax.nn.softplus(x @ Wdt + bdt)
            Bm = x @ Wb + bb
            Cm = x @ Wc + bc
            dA = jnp.exp(dt[..., None] * A)
            dBx = dt[..., None] * Bm[:, :, None, :] * x[..., None]

            def step(h, ins):
                dA_t, dBx_t, C_t = ins
                h = dA_t * h + dBx_t
                y = jnp.einsum('bdn,bn->bd', h, C_t)
                return (h, y)
            h0 = jnp.zeros((x.shape[0], x.shape[2], A.shape[1]), x.dtype)
            _, ys = jax.lax.scan(step, h0, (dA.transpose(1, 0, 2, 3), dBx.transpose(1, 0, 2, 3), Cm.transpose(1, 0, 2)))
            return ys.transpose(1, 0, 2)
        key = jax.random.key(seed)
        ks = jax.random.split(key, 16)
        s = 1.0 / np.sqrt(D)
        inp = {'u': jax.random.normal(ks[0], (B, T, D), jnp.float32), 'Win': jax.random.normal(ks[1], (D, D), jnp.float32) * s, 'b_in': jnp.zeros((D,), jnp.float32), 'Wg': jax.random.normal(ks[2], (D, D), jnp.float32) * s, 'bg': jnp.zeros((D,), jnp.float32), 'Wout': jax.random.normal(ks[3], (D, D), jnp.float32) * s, 'bout': jnp.zeros((D,), jnp.float32), 'convw': jax.random.normal(ks[4], (D, 3), jnp.float32) * 0.5, 'convb': jnp.zeros((D,), jnp.float32), 'A': -jnp.exp(jax.random.normal(ks[5], (D, N), jnp.float32) * 0.5), 'Wb': jax.random.normal(ks[6], (D, N), jnp.float32) * s, 'bb': jnp.zeros((N,), jnp.float32), 'Wc': jax.random.normal(ks[7], (D, N), jnp.float32) * s, 'bc': jnp.zeros((N,), jnp.float32), 'Wdt': jax.random.normal(ks[8], (D, D), jnp.float32) * s, 'bdt': jnp.full((D,), -2.0, jnp.float32)}
        return inp
    _L1_attn_all = _L1_attn_setup()
    _L1_attn_in = {k: v for k, v in _L1_attn_all.items() if k in ('Win', 'b_in', 'Wg', 'bg', 'Wout', 'bout', 'convw', 'convb', 'A', 'Wb', 'bb', 'Wc', 'bc', 'Wdt', 'bdt')}
    del _L1_attn_all

    def _L1_xattn_setup():
        import jax, jax.numpy as jnp
        import numpy as np
        NUM_HEADS = 16
        CLAMP = 10000.0
        key = jax.random.key(seed)
        ks = jax.random.split(key, 8)
        B, Nq, Nkv, Cq, Ckv = (4, 256, 256, 128, 96)
        s_q = 1.0 / np.sqrt(Cq)
        s_kv = 1.0 / np.sqrt(Ckv)
        return {'query': jax.random.normal(ks[0], (B, Nq, Cq), jnp.float32), 'key_value': jax.random.normal(ks[1], (B, Nkv, Ckv), jnp.float32), 'Wq': jax.random.normal(ks[2], (Cq, Cq), jnp.float32) * s_q, 'bq': jnp.zeros((Cq,), jnp.float32), 'Wk': jax.random.normal(ks[3], (Ckv, Cq), jnp.float32) * s_kv, 'bk': jnp.zeros((Cq,), jnp.float32), 'Wv': jax.random.normal(ks[4], (Ckv, Cq), jnp.float32) * s_kv, 'bv': jnp.zeros((Cq,), jnp.float32), 'Wo': jax.random.normal(ks[5], (Cq, Cq), jnp.float32) * s_q, 'bo': jnp.zeros((Cq,), jnp.float32)}
    _L1_xattn_all = _L1_xattn_setup()
    _L1_xattn_in = {k: v for k, v in _L1_xattn_all.items() if k in ('Wq', 'bq', 'Wk', 'bk', 'Wv', 'bv', 'Wo', 'bo')}
    del _L1_xattn_all

    def _L1_ffn_setup():
        import jax, jax.numpy as jnp
        import numpy as np
        EPS = 1e-05
        TOP_K = 2

        def _rmsnorm(x, w):
            xf = x.astype(jnp.float32)
            rms = jax.lax.rsqrt(jnp.mean(xf * xf, axis=-1, keepdims=True) + EPS)
            return (xf * rms).astype(x.dtype) * w

        def _attention(x, wq, wk, wv, wo, num_heads=16):
            B, S, H = x.shape
            D = H // num_heads
            q = (x @ wq.T).reshape(B, S, num_heads, D)
            k = (x @ wk.T).reshape(B, S, num_heads, D)
            v = (x @ wv.T).reshape(B, S, num_heads, D)
            scale = 1.0 / jnp.sqrt(jnp.float32(D)).astype(x.dtype)
            scores = jnp.einsum('bqhd,bkhd->bhqk', q, k) * scale
            probs = jax.nn.softmax(scores, axis=-1)
            out = jnp.einsum('bhqk,bkhd->bqhd', probs, v).reshape(B, S, H)
            return out @ wo.T

        def _moe(x, gate_w, w1, w2, w3):
            B, S, H = x.shape
            xf = x.reshape(-1, H)
            logits = xf @ gate_w.T
            rw, sel = jax.lax.top_k(logits, TOP_K)
            rw = jax.nn.softmax(rw.astype(jnp.float32), axis=-1).astype(x.dtype)
            E = gate_w.shape[0]
            out = jnp.zeros_like(xf)
            for e in range(E):
                we = jnp.sum(jnp.where(sel == e, rw, 0.0), axis=-1)
                h = jax.nn.silu(xf @ w1[e].T) * (xf @ w3[e].T)
                out = out + h @ w2[e].T * we[:, None]
            return out.reshape(B, S, H)
        key = jax.random.key(seed)
        ks = jax.random.split(key, 10)
        H, I, E, NH = (128, 256, 8, 16)
        B, S = (2, 256)
        s = 0.02
        return {'x': jax.random.normal(ks[0], (B, S, H), jnp.float32), 'ln1_w': jnp.ones((H,), jnp.float32), 'ln2_w': jnp.ones((H,), jnp.float32), 'wq': jax.random.normal(ks[1], (H, H), jnp.float32) * s, 'wk': jax.random.normal(ks[2], (H, H), jnp.float32) * s, 'wv': jax.random.normal(ks[3], (H, H), jnp.float32) * s, 'wo': jax.random.normal(ks[4], (H, H), jnp.float32) * s, 'gate_w': jax.random.normal(ks[5], (E, H), jnp.float32) * s, 'w1': jax.random.normal(ks[6], (E, I, H), jnp.float32) * s, 'w2': jax.random.normal(ks[7], (E, H, I), jnp.float32) * s, 'w3': jax.random.normal(ks[8], (E, I, H), jnp.float32) * s}
    _L1_ffn_all = _L1_ffn_setup()
    _L1_ffn_in = {k: v for k, v in _L1_ffn_all.items() if k in ('ln1_w', 'ln2_w', 'wq', 'wk', 'wv', 'wo', 'gate_w', 'w1', 'w2', 'w3')}
    del _L1_ffn_all

    def _L2_attn_setup():
        import jax, jax.numpy as jnp
        import numpy as np
        import math
        B, S, DM, H, F = (2, 256, 128, 16, 192)
        DH = F // 3
        MAX_BIAS = 8.0

        def _get_slopes(n):

            def pow2(n):
                start = 2.0 ** (-2.0 ** (-(math.log2(n) - 3)))
                return [start * start ** i for i in range(n)]
            if math.log2(n).is_integer():
                return pow2(n)
            cp2 = 2 ** math.floor(math.log2(n))
            return pow2(cp2) + _get_slopes(2 * cp2)[0::2][:n - cp2]

        def _rope_sin_cos(seq_len, dim):
            inv_freq = 1.0 / 10000.0 ** (jnp.arange(0, dim, 2, dtype=jnp.float32) / dim)
            freqs = jnp.outer(jnp.arange(seq_len, dtype=jnp.float32), inv_freq)
            sin = jnp.concatenate([jnp.sin(freqs), jnp.sin(freqs)], axis=-1)
            cos = jnp.concatenate([jnp.cos(freqs), jnp.cos(freqs)], axis=-1)
            return (sin, cos)

        def _rotate_half(x):
            x1, x2 = jnp.split(x, 2, axis=-1)
            return jnp.concatenate([-x2, x1], axis=-1)
        key = jax.random.key(seed)
        kx, kq, ko = jax.random.split(key, 3)
        x = jax.random.normal(kx, (B, S, DM), dtype=jnp.float32)
        w_qkv = jax.random.normal(kq, (DM, H, F), dtype=jnp.float32) * (1.0 / math.sqrt(DM))
        b_qkv = jnp.zeros((H, F), dtype=jnp.float32)
        w_out = jax.random.normal(ko, (H, DH, DM), dtype=jnp.float32) * (1.0 / math.sqrt(H * DH))
        b_out = jnp.zeros((DM,), dtype=jnp.float32)
        return {'x': x, 'w_qkv': w_qkv, 'b_qkv': b_qkv, 'w_out': w_out, 'b_out': b_out}
    _L2_attn_all = _L2_attn_setup()
    _L2_attn_in = {k: v for k, v in _L2_attn_all.items() if k in ('w_qkv', 'b_qkv', 'w_out', 'b_out')}
    del _L2_attn_all

    def _L2_xattn_setup():
        import jax, jax.numpy as jnp
        import numpy as np
        HEADS = 8
        DIM_HEAD = 64
        SCALE = DIM_HEAD ** (-0.5)
        key = jax.random.key(seed)
        ks = jax.random.split(key, 7)
        b, n, m = (4, 256, 128)
        qd, cd, inner = (128, 96, HEADS * DIM_HEAD)
        s = lambda fan_in: 1.0 / np.sqrt(fan_in)
        return {'x': jax.random.normal(ks[0], (b, n, qd), jnp.float32), 'context': jax.random.normal(ks[1], (b, m, cd), jnp.float32), 'Wq': jax.random.normal(ks[2], (qd, inner), jnp.float32) * s(qd), 'Wk': jax.random.normal(ks[3], (cd, inner), jnp.float32) * s(cd), 'Wv': jax.random.normal(ks[4], (cd, inner), jnp.float32) * s(cd), 'Wout': jax.random.normal(ks[5], (inner, qd), jnp.float32) * s(inner), 'bout': jax.random.normal(ks[6], (qd,), jnp.float32) * 0.01}
    _L2_xattn_all = _L2_xattn_setup()
    _L2_xattn_in = {k: v for k, v in _L2_xattn_all.items() if k in ('Wq', 'Wk', 'Wv', 'Wout', 'bout')}
    del _L2_xattn_all

    def _L2_ffn_setup():
        import jax, jax.numpy as jnp
        import numpy as np
        DIM = 128
        N_HEADS = 16
        N_KV_HEADS = 4
        HEAD_DIM = DIM // N_HEADS
        N_REP = N_HEADS // N_KV_HEADS
        N_EXPERTS = 4
        TOP_K = 2
        HIDDEN = 3 * DIM
        EPS = 1.1920928955078125e-07

        def _rmsnorm(x, g):
            var = jnp.mean(jnp.square(x), axis=-1, keepdims=True)
            return x * jax.lax.rsqrt(var + EPS) * g

        def _rotate_half(x):
            x1, x2 = jnp.split(x, 2, axis=-1)
            return jnp.concatenate([-x2, x1], axis=-1)

        def _rope_tables(S):
            inv_freq = 1.0 / 10000.0 ** (jnp.arange(0, HEAD_DIM, 2, dtype=jnp.float32) / HEAD_DIM)
            freqs = jnp.arange(S, dtype=jnp.float32)[:, None] * inv_freq[None, :]
            emb = jnp.concatenate([freqs, freqs], axis=-1)
            return (jnp.cos(emb), jnp.sin(emb))

        def _attention(x, wq, wk, wv, wo):
            B, S, D = x.shape
            q = (x @ wq).reshape(B, S, N_HEADS, HEAD_DIM).transpose(0, 2, 1, 3)
            k = (x @ wk).reshape(B, S, N_KV_HEADS, HEAD_DIM).transpose(0, 2, 1, 3)
            v = (x @ wv).reshape(B, S, N_KV_HEADS, HEAD_DIM).transpose(0, 2, 1, 3)
            cos, sin = _rope_tables(S)
            q = q * cos + _rotate_half(q) * sin
            k = k * cos + _rotate_half(k) * sin
            k = jnp.repeat(k, N_REP, axis=1)
            v = jnp.repeat(v, N_REP, axis=1)
            scores = jnp.einsum('bhqd,bhkd->bhqk', q, k) / jnp.sqrt(jnp.float32(HEAD_DIM))
            causal = jnp.tril(jnp.ones((S, S), dtype=bool))
            scores = jnp.where(causal, scores, -jnp.inf)
            attn = jax.nn.softmax(scores, axis=-1)
            out = jnp.einsum('bhqk,bhkd->bhqd', attn, v)
            return out.transpose(0, 2, 1, 3).reshape(B, S, D) @ wo

        def _moe(x, gate, w1, w2, w3):
            B, S, D = x.shape
            xf = x.reshape(-1, D)
            probs = jax.nn.softmax(xf @ gate, axis=-1)
            w, idx = jax.lax.top_k(probs, TOP_K)
            w = w / jnp.sum(w, axis=-1, keepdims=True)
            oh = jax.nn.one_hot(idx, N_EXPERTS, dtype=xf.dtype)
            comb = jnp.einsum('nk,nke->ne', w, oh)
            out = jnp.zeros_like(xf)
            for e in range(N_EXPERTS):
                h = jax.nn.silu(xf @ w1[e]) * (xf @ w3[e])
                out = out + comb[:, e:e + 1] * (h @ w2[e])
            return out.reshape(B, S, D)
        key = jax.random.key(seed)
        ks = jax.random.split(key, 12)
        s = 0.02
        B, S = (2, 256)
        return {'x': jax.random.normal(ks[0], (B, S, DIM), jnp.float32), 'g1': jnp.ones((DIM,), jnp.float32), 'g2': jnp.ones((DIM,), jnp.float32), 'wq': jax.random.normal(ks[1], (DIM, N_HEADS * HEAD_DIM), jnp.float32) * s, 'wk': jax.random.normal(ks[2], (DIM, N_KV_HEADS * HEAD_DIM), jnp.float32) * s, 'wv': jax.random.normal(ks[3], (DIM, N_KV_HEADS * HEAD_DIM), jnp.float32) * s, 'wo': jax.random.normal(ks[4], (N_HEADS * HEAD_DIM, DIM), jnp.float32) * s, 'gate': jax.random.normal(ks[5], (DIM, N_EXPERTS), jnp.float32) * s, 'w1': jax.random.normal(ks[6], (N_EXPERTS, DIM, HIDDEN), jnp.float32) * s, 'w2': jax.random.normal(ks[7], (N_EXPERTS, HIDDEN, DIM), jnp.float32) * s, 'w3': jax.random.normal(ks[8], (N_EXPERTS, DIM, HIDDEN), jnp.float32) * s}
    _L2_ffn_all = _L2_ffn_setup()
    _L2_ffn_in = {k: v for k, v in _L2_ffn_all.items() if k in ('g1', 'g2', 'wq', 'wk', 'wv', 'wo', 'gate', 'w1', 'w2', 'w3')}
    del _L2_ffn_all

    def _L3_attn_setup():
        import jax, jax.numpy as jnp
        import numpy as np
        SCALE = 128 ** (-0.5)
        key = jax.random.key(seed)
        ks = jax.random.split(key, 5)
        b, s, d = (4, 512, 128)
        x = jax.random.normal(ks[0], (b, s, d), dtype=jnp.float32)
        w_std = (2.0 / (d + d)) ** 0.5
        Wq = jax.random.normal(ks[1], (d, d), dtype=jnp.float32) * w_std
        Wk = jax.random.normal(ks[2], (d, d), dtype=jnp.float32) * w_std
        Wv = jax.random.normal(ks[3], (d, d), dtype=jnp.float32) * w_std
        Wr = jax.random.normal(ks[4], (d, d), dtype=jnp.float32) * w_std
        return {'x': x, 'Wq': Wq, 'Wk': Wk, 'Wv': Wv, 'Wr': Wr}
    _L3_attn_all = _L3_attn_setup()
    _L3_attn_in = {k: v for k, v in _L3_attn_all.items() if k in ('Wq', 'Wk', 'Wv', 'Wr')}
    del _L3_attn_all

    def _L3_xattn_setup():
        import jax, jax.numpy as jnp
        import numpy as np
        HEADS = 16
        DIM_HEAD = 64
        RANK = 32
        LORA_W = 1.0
        IPA_SCALE = 1.0
        IPA_TOKENS = 4
        SCALE = DIM_HEAD ** (-0.5)

        def _split_heads(t):
            b, n, _ = t.shape
            return t.reshape(b, n, HEADS, DIM_HEAD).transpose(0, 2, 1, 3)

        def _merge_heads(t):
            b, h, n, d = t.shape
            return t.transpose(0, 2, 1, 3).reshape(b, n, h * d)

        def _attention(q_in, k_in, v_in):
            q = _split_heads(q_in)
            k = _split_heads(k_in)
            v = _split_heads(v_in)
            s = jnp.einsum('bhid,bhjd->bhij', q, k) * SCALE
            p = jax.nn.softmax(s, axis=-1)
            o = jnp.einsum('bhij,bhjd->bhid', p, v)
            return _merge_heads(o)

        def _lora(t, down, up, alpha):
            return t @ down @ up * (LORA_W * alpha[0] / RANK)
        key = jax.random.key(seed)
        ks = jax.random.split(key, 20)
        B, N, QD, CD, ID = (8, 512, 128, 96, HEADS * DIM_HEAD)
        CTX = 77 + IPA_TOKENS
        s = 0.02
        return {'x': jax.random.normal(ks[0], (B, N, QD), jnp.float32), 'context': jax.random.normal(ks[1], (B, CTX, CD), jnp.float32), 'Wq': jax.random.normal(ks[2], (QD, ID), jnp.float32) * s, 'Wk': jax.random.normal(ks[3], (CD, ID), jnp.float32) * s, 'Wv': jax.random.normal(ks[4], (CD, ID), jnp.float32) * s, 'Wo': jax.random.normal(ks[5], (ID, QD), jnp.float32) * s, 'bo': jnp.zeros((QD,), jnp.float32), 'q_down': jax.random.normal(ks[6], (QD, RANK), jnp.float32) * s, 'q_up': jax.random.normal(ks[7], (RANK, ID), jnp.float32) * s, 'q_alpha': jnp.ones((1,), jnp.float32) * RANK, 'k_down': jax.random.normal(ks[8], (CD, RANK), jnp.float32) * s, 'k_up': jax.random.normal(ks[9], (RANK, ID), jnp.float32) * s, 'k_alpha': jnp.ones((1,), jnp.float32) * RANK, 'v_down': jax.random.normal(ks[10], (CD, RANK), jnp.float32) * s, 'v_up': jax.random.normal(ks[11], (RANK, ID), jnp.float32) * s, 'v_alpha': jnp.ones((1,), jnp.float32) * RANK, 'o_down': jax.random.normal(ks[12], (ID, RANK), jnp.float32) * s, 'o_up': jax.random.normal(ks[13], (RANK, QD), jnp.float32) * s, 'o_alpha': jnp.ones((1,), jnp.float32) * RANK, 'Wk_ipa': jax.random.normal(ks[14], (CD, ID), jnp.float32) * s, 'Wv_ipa': jax.random.normal(ks[15], (CD, ID), jnp.float32) * s}
    _L3_xattn_all = _L3_xattn_setup()
    _L3_xattn_in = {k: v for k, v in _L3_xattn_all.items() if k in ('Wq', 'Wk', 'Wv', 'Wo', 'bo', 'q_down', 'q_up', 'q_alpha', 'k_down', 'k_up', 'k_alpha', 'v_down', 'v_up', 'v_alpha', 'o_down', 'o_up', 'o_alpha', 'Wk_ipa', 'Wv_ipa')}
    del _L3_xattn_all

    def _L3_ffn_setup():
        import jax, jax.numpy as jnp
        import numpy as np
        B, S, H = (1, 256, 128)
        E, K = (16, 4)
        G, TG = (4, 2)
        I_MOE = 64
        N_SH = 2
        SCALE = 2.5

        def _mlp(x, gw, uw, dw):
            return jax.nn.silu(x @ gw.T) * (x @ uw.T) @ dw.T

        def _route(x2d, router_weight, e_bias):
            T = x2d.shape[0]
            scores = jax.nn.sigmoid(x2d @ router_weight.T)
            sc = scores + e_bias[None, :]
            group_scores = jnp.sum(jax.lax.top_k(sc.reshape(T, G, E // G), 2)[0], axis=-1)
            _, gidx = jax.lax.top_k(group_scores, TG)
            gmask = jnp.zeros((T, G), sc.dtype).at[jnp.arange(T)[:, None], gidx].set(1.0)
            smask = jnp.repeat(gmask, E // G, axis=1)
            masked = jnp.where(smask > 0, sc, 0.0)
            _, tidx = jax.lax.top_k(masked, K)
            tw = jnp.take_along_axis(scores, tidx, axis=1)
            tw = tw / (jnp.sum(tw, axis=-1, keepdims=True) + 1e-20)
            tw = tw * SCALE
            return (tidx, tw)

        def _moe_forward(hidden_states, router_weight, e_bias, gate_w, up_w, down_w, sh_gate_w, sh_up_w, sh_down_w):
            orig_shape = hidden_states.shape
            x = hidden_states.reshape(-1, H)
            T = x.shape[0]
            tidx, tw = _route(x, router_weight, e_bias)
            g = jnp.einsum('th,eih->tei', x, gate_w)
            u = jnp.einsum('th,eih->tei', x, up_w)
            h = jax.nn.silu(g) * u
            yo = jnp.einsum('tei,ehi->teh', h, down_w)
            combine = jnp.zeros((T, E), tw.dtype).at[jnp.arange(T)[:, None], tidx].add(tw)
            routed = jnp.einsum('te,teh->th', combine, yo)
            shared = _mlp(hidden_states.reshape(-1, H), sh_gate_w, sh_up_w, sh_down_w)
            return (routed + shared).reshape(orig_shape)
        key = jax.random.key(seed)
        ks = jax.random.split(key, 9)
        s = 0.02
        return {'hidden_states': jax.random.normal(ks[0], (B, S, H), jnp.float32), 'router_weight': jax.random.normal(ks[1], (E, H), jnp.float32) * s, 'e_bias': jnp.zeros((E,), jnp.float32), 'gate_w': jax.random.normal(ks[2], (E, I_MOE, H), jnp.float32) * s, 'up_w': jax.random.normal(ks[3], (E, I_MOE, H), jnp.float32) * s, 'down_w': jax.random.normal(ks[4], (E, H, I_MOE), jnp.float32) * s, 'sh_gate_w': jax.random.normal(ks[5], (N_SH * I_MOE, H), jnp.float32) * s, 'sh_up_w': jax.random.normal(ks[6], (N_SH * I_MOE, H), jnp.float32) * s, 'sh_down_w': jax.random.normal(ks[7], (H, N_SH * I_MOE), jnp.float32) * s}
    _L3_ffn_all = _L3_ffn_setup()
    _L3_ffn_in = {k: v for k, v in _L3_ffn_all.items() if k in ('router_weight', 'e_bias', 'gate_w', 'up_w', 'down_w', 'sh_gate_w', 'sh_up_w', 'sh_down_w')}
    del _L3_ffn_all
    return {'x': x, 'ctx_768': ctx_768, 'L0_attn_Wq': _L0_attn_in['Wq'], 'L0_attn_gq': _L0_attn_in['gq'], 'L0_attn_bq': _L0_attn_in['bq'], 'L0_attn_Wk': _L0_attn_in['Wk'], 'L0_attn_gk': _L0_attn_in['gk'], 'L0_attn_bk': _L0_attn_in['bk'], 'L0_attn_Wv': _L0_attn_in['Wv'], 'L0_attn_gv': _L0_attn_in['gv'], 'L0_attn_bv': _L0_attn_in['bv'], 'L0_attn_Wp': _L0_attn_in['Wp'], 'L0_attn_bp': _L0_attn_in['bp'], 'L0_xattn_Wq': _L0_xattn_in['Wq'], 'L0_xattn_bq': _L0_xattn_in['bq'], 'L0_xattn_Wkv': _L0_xattn_in['Wkv'], 'L0_xattn_bkv': _L0_xattn_in['bkv'], 'L0_xattn_Wo': _L0_xattn_in['Wo'], 'L0_xattn_bo': _L0_xattn_in['bo'], 'L0_ffn_ln1_weight': _L0_ffn_in['ln1_weight'], 'L0_ffn_ln1_bias': _L0_ffn_in['ln1_bias'], 'L0_ffn_ln2_weight': _L0_ffn_in['ln2_weight'], 'L0_ffn_ln2_bias': _L0_ffn_in['ln2_bias'], 'L0_ffn_qkv_weight': _L0_ffn_in['qkv_weight'], 'L0_ffn_proj_weight': _L0_ffn_in['proj_weight'], 'L0_ffn_router_weight': _L0_ffn_in['router_weight'], 'L0_ffn_moe_w1': _L0_ffn_in['moe_w1'], 'L0_ffn_moe_w2': _L0_ffn_in['moe_w2'], 'L1_attn_Win': _L1_attn_in['Win'], 'L1_attn_b_in': _L1_attn_in['b_in'], 'L1_attn_Wg': _L1_attn_in['Wg'], 'L1_attn_bg': _L1_attn_in['bg'], 'L1_attn_Wout': _L1_attn_in['Wout'], 'L1_attn_bout': _L1_attn_in['bout'], 'L1_attn_convw': _L1_attn_in['convw'], 'L1_attn_convb': _L1_attn_in['convb'], 'L1_attn_A': _L1_attn_in['A'], 'L1_attn_Wb': _L1_attn_in['Wb'], 'L1_attn_bb': _L1_attn_in['bb'], 'L1_attn_Wc': _L1_attn_in['Wc'], 'L1_attn_bc': _L1_attn_in['bc'], 'L1_attn_Wdt': _L1_attn_in['Wdt'], 'L1_attn_bdt': _L1_attn_in['bdt'], 'L1_xattn_Wq': _L1_xattn_in['Wq'], 'L1_xattn_bq': _L1_xattn_in['bq'], 'L1_xattn_Wk': _L1_xattn_in['Wk'], 'L1_xattn_bk': _L1_xattn_in['bk'], 'L1_xattn_Wv': _L1_xattn_in['Wv'], 'L1_xattn_bv': _L1_xattn_in['bv'], 'L1_xattn_Wo': _L1_xattn_in['Wo'], 'L1_xattn_bo': _L1_xattn_in['bo'], 'L1_ffn_ln1_w': _L1_ffn_in['ln1_w'], 'L1_ffn_ln2_w': _L1_ffn_in['ln2_w'], 'L1_ffn_wq': _L1_ffn_in['wq'], 'L1_ffn_wk': _L1_ffn_in['wk'], 'L1_ffn_wv': _L1_ffn_in['wv'], 'L1_ffn_wo': _L1_ffn_in['wo'], 'L1_ffn_gate_w': _L1_ffn_in['gate_w'], 'L1_ffn_w1': _L1_ffn_in['w1'], 'L1_ffn_w2': _L1_ffn_in['w2'], 'L1_ffn_w3': _L1_ffn_in['w3'], 'L2_attn_w_qkv': _L2_attn_in['w_qkv'], 'L2_attn_b_qkv': _L2_attn_in['b_qkv'], 'L2_attn_w_out': _L2_attn_in['w_out'], 'L2_attn_b_out': _L2_attn_in['b_out'], 'L2_xattn_Wq': _L2_xattn_in['Wq'], 'L2_xattn_Wk': _L2_xattn_in['Wk'], 'L2_xattn_Wv': _L2_xattn_in['Wv'], 'L2_xattn_Wout': _L2_xattn_in['Wout'], 'L2_xattn_bout': _L2_xattn_in['bout'], 'L2_ffn_g1': _L2_ffn_in['g1'], 'L2_ffn_g2': _L2_ffn_in['g2'], 'L2_ffn_wq': _L2_ffn_in['wq'], 'L2_ffn_wk': _L2_ffn_in['wk'], 'L2_ffn_wv': _L2_ffn_in['wv'], 'L2_ffn_wo': _L2_ffn_in['wo'], 'L2_ffn_gate': _L2_ffn_in['gate'], 'L2_ffn_w1': _L2_ffn_in['w1'], 'L2_ffn_w2': _L2_ffn_in['w2'], 'L2_ffn_w3': _L2_ffn_in['w3'], 'L3_attn_Wq': _L3_attn_in['Wq'], 'L3_attn_Wk': _L3_attn_in['Wk'], 'L3_attn_Wv': _L3_attn_in['Wv'], 'L3_attn_Wr': _L3_attn_in['Wr'], 'L3_xattn_Wq': _L3_xattn_in['Wq'], 'L3_xattn_Wk': _L3_xattn_in['Wk'], 'L3_xattn_Wv': _L3_xattn_in['Wv'], 'L3_xattn_Wo': _L3_xattn_in['Wo'], 'L3_xattn_bo': _L3_xattn_in['bo'], 'L3_xattn_q_down': _L3_xattn_in['q_down'], 'L3_xattn_q_up': _L3_xattn_in['q_up'], 'L3_xattn_q_alpha': _L3_xattn_in['q_alpha'], 'L3_xattn_k_down': _L3_xattn_in['k_down'], 'L3_xattn_k_up': _L3_xattn_in['k_up'], 'L3_xattn_k_alpha': _L3_xattn_in['k_alpha'], 'L3_xattn_v_down': _L3_xattn_in['v_down'], 'L3_xattn_v_up': _L3_xattn_in['v_up'], 'L3_xattn_v_alpha': _L3_xattn_in['v_alpha'], 'L3_xattn_o_down': _L3_xattn_in['o_down'], 'L3_xattn_o_up': _L3_xattn_in['o_up'], 'L3_xattn_o_alpha': _L3_xattn_in['o_alpha'], 'L3_xattn_Wk_ipa': _L3_xattn_in['Wk_ipa'], 'L3_xattn_Wv_ipa': _L3_xattn_in['Wv_ipa'], 'L3_ffn_router_weight': _L3_ffn_in['router_weight'], 'L3_ffn_e_bias': _L3_ffn_in['e_bias'], 'L3_ffn_gate_w': _L3_ffn_in['gate_w'], 'L3_ffn_up_w': _L3_ffn_in['up_w'], 'L3_ffn_down_w': _L3_ffn_in['down_w'], 'L3_ffn_sh_gate_w': _L3_ffn_in['sh_gate_w'], 'L3_ffn_sh_up_w': _L3_ffn_in['sh_up_w'], 'L3_ffn_sh_down_w': _L3_ffn_in['sh_down_w']}

def reference(x, ctx_768, L0_attn_Wq, L0_attn_gq, L0_attn_bq, L0_attn_Wk, L0_attn_gk, L0_attn_bk, L0_attn_Wv, L0_attn_gv, L0_attn_bv, L0_attn_Wp, L0_attn_bp, L0_xattn_Wq, L0_xattn_bq, L0_xattn_Wkv, L0_xattn_bkv, L0_xattn_Wo, L0_xattn_bo, L0_ffn_ln1_weight, L0_ffn_ln1_bias, L0_ffn_ln2_weight, L0_ffn_ln2_bias, L0_ffn_qkv_weight, L0_ffn_proj_weight, L0_ffn_router_weight, L0_ffn_moe_w1, L0_ffn_moe_w2, L1_attn_Win, L1_attn_b_in, L1_attn_Wg, L1_attn_bg, L1_attn_Wout, L1_attn_bout, L1_attn_convw, L1_attn_convb, L1_attn_A, L1_attn_Wb, L1_attn_bb, L1_attn_Wc, L1_attn_bc, L1_attn_Wdt, L1_attn_bdt, L1_xattn_Wq, L1_xattn_bq, L1_xattn_Wk, L1_xattn_bk, L1_xattn_Wv, L1_xattn_bv, L1_xattn_Wo, L1_xattn_bo, L1_ffn_ln1_w, L1_ffn_ln2_w, L1_ffn_wq, L1_ffn_wk, L1_ffn_wv, L1_ffn_wo, L1_ffn_gate_w, L1_ffn_w1, L1_ffn_w2, L1_ffn_w3, L2_attn_w_qkv, L2_attn_b_qkv, L2_attn_w_out, L2_attn_b_out, L2_xattn_Wq, L2_xattn_Wk, L2_xattn_Wv, L2_xattn_Wout, L2_xattn_bout, L2_ffn_g1, L2_ffn_g2, L2_ffn_wq, L2_ffn_wk, L2_ffn_wv, L2_ffn_wo, L2_ffn_gate, L2_ffn_w1, L2_ffn_w2, L2_ffn_w3, L3_attn_Wq, L3_attn_Wk, L3_attn_Wv, L3_attn_Wr, L3_xattn_Wq, L3_xattn_Wk, L3_xattn_Wv, L3_xattn_Wo, L3_xattn_bo, L3_xattn_q_down, L3_xattn_q_up, L3_xattn_q_alpha, L3_xattn_k_down, L3_xattn_k_up, L3_xattn_k_alpha, L3_xattn_v_down, L3_xattn_v_up, L3_xattn_v_alpha, L3_xattn_o_down, L3_xattn_o_up, L3_xattn_o_alpha, L3_xattn_Wk_ipa, L3_xattn_Wv_ipa, L3_ffn_router_weight, L3_ffn_e_bias, L3_ffn_gate_w, L3_ffn_up_w, L3_ffn_down_w, L3_ffn_sh_gate_w, L3_ffn_sh_up_w, L3_ffn_sh_down_w):
    import jax
    import jax.numpy as jnp

    def _L0_attn_ref(x, Wq, gq, bq, Wk, gk, bk, Wv, gv, bv, Wp, bp):
        import jax, jax.numpy as jnp
        import numpy as np
        DIM = 128
        NUM_HEADS = 16
        HEAD_DIM = DIM // NUM_HEADS
        TAU = 2.0
        V_TH = 1.0
        BN_EPS = 1e-05

        def _branch(x, W, gamma, beta):
            B, N, D = x.shape
            h = jnp.einsum('bnd,ed->bne', x, W)
            hf = h.reshape(B * N, D)
            mean = jnp.mean(hf, axis=0)
            var = jnp.var(hf, axis=0)
            hn = (hf - mean) * jax.lax.rsqrt(var + BN_EPS) * gamma + beta
            hn = hn.reshape(B, N, D)
            return jax.nn.sigmoid(4.0 * (hn - V_TH))

        def _heads(x):
            B, N, D = x.shape
            return x.reshape(B, N, NUM_HEADS, HEAD_DIM).transpose(0, 2, 1, 3)
        B, N, D = x.shape
        scale = HEAD_DIM ** (-0.5)
        q = _branch(x, Wq, gq, bq)
        k = _branch(x, Wk, gk, bk)
        v = _branch(x, Wv, gv, bv)
        qk = _heads(q * k) * scale
        v_h = _heads(v)
        vv = jnp.einsum('bhnd,bhne->bhde', v_h, v_h)
        out = jnp.einsum('bhnd,bhde->bhne', qk, vv)
        out = out.transpose(0, 2, 1, 3).reshape(B, N, D)
        return jnp.einsum('bnd,ed->bne', out, Wp) + bp

    def _L0_xattn_ref(x, y, Wq, bq, Wkv, bkv, Wo, bo):
        import jax, jax.numpy as jnp
        import numpy as np
        N_HEADS = 16
        b, l, d = x.shape
        m = y.shape[1]
        h = N_HEADS
        dh = d // h
        q = (jnp.einsum('bld,ed->ble', x, Wq) + bq).reshape(b, l, h, dh)
        kv = (jnp.einsum('bmc,ec->bme', y, Wkv) + bkv).reshape(b, m, h, 2 * dh)
        k, v = (kv[..., :dh], kv[..., dh:])
        scale = 1.0 / jnp.sqrt(jnp.asarray(dh, x.dtype))
        att = jax.nn.softmax(jnp.einsum('blhd,bmhd->blmh', q, k) * scale, axis=2)
        out = jnp.einsum('blmh,bmhd->blhd', att, v).reshape(b, l, d)
        return jnp.einsum('bld,ed->ble', out, Wo) + bo

    def _L0_ffn_ref(hidden_states, ln1_weight, ln1_bias, ln2_weight, ln2_bias, qkv_weight, proj_weight, router_weight, moe_w1, moe_w2):
        import jax, jax.numpy as jnp
        import numpy as np
        EPS = 1e-05
        NUM_HEADS = 16
        NUM_KV_HEADS = 4
        NUM_EXPERTS = 8
        TOP_K = 2

        def _layernorm(x, w, b):
            mu = jnp.mean(x, axis=-1, keepdims=True)
            var = jnp.mean((x - mu) ** 2, axis=-1, keepdims=True)
            return (x - mu) * jax.lax.rsqrt(var + EPS) * w + b
        S, B, H = hidden_states.shape
        hd = H // NUM_HEADS
        rep = NUM_HEADS // NUM_KV_HEADS
        scale = 1.0 / hd ** 0.5
        ln1_out = _layernorm(hidden_states, ln1_weight, ln1_bias)
        qkv = jnp.einsum('sbh,oh->sbo', ln1_out, qkv_weight)
        q = qkv[..., :NUM_HEADS * hd].reshape(S, B, NUM_HEADS, hd)
        k = qkv[..., NUM_HEADS * hd:(NUM_HEADS + NUM_KV_HEADS) * hd].reshape(S, B, NUM_KV_HEADS, hd)
        v = qkv[..., (NUM_HEADS + NUM_KV_HEADS) * hd:].reshape(S, B, NUM_KV_HEADS, hd)
        k = jnp.repeat(k, rep, axis=2)
        v = jnp.repeat(v, rep, axis=2)
        scores = jnp.einsum('sbhd,tbhd->bhst', q, k) * scale
        causal = jnp.tril(jnp.ones((S, S), bool))
        scores = jnp.where(causal, scores, jnp.finfo(scores.dtype).min)
        probs = jax.nn.softmax(scores, axis=-1)
        attn = jnp.einsum('bhst,tbhd->sbhd', probs, v).reshape(S, B, H)
        proj_out = jnp.einsum('sbh,oh->sbo', attn, proj_weight)
        hidden_after_attn = hidden_states + proj_out
        ln2_out = _layernorm(hidden_after_attn, ln2_weight, ln2_bias)
        x = ln2_out.reshape(-1, H)
        logits = jnp.einsum('th,eh->te', x, router_weight)
        gate = jax.nn.softmax(logits, axis=-1)
        top_probs, top_idx = jax.lax.top_k(gate, TOP_K)
        h_mid = jax.nn.gelu(jnp.einsum('th,ehf->etf', x, moe_w1))
        expert_out = jnp.einsum('etf,efh->eth', h_mid, moe_w2)
        e_ids = jnp.arange(NUM_EXPERTS)[:, None, None]
        weights = jnp.sum(jnp.where(top_idx[None] == e_ids, top_probs[None], 0.0), axis=-1)
        moe_out = jnp.einsum('eth,et->th', expert_out, weights).reshape(S, B, H)
        return hidden_after_attn + moe_out

    def _L1_attn_ref(u, Win, b_in, Wg, bg, Wout, bout, convw, convb, A, Wb, bb, Wc, bc, Wdt, bdt):
        import jax, jax.numpy as jnp
        import numpy as np
        B, T, D, N = (4, 128, 128, 16)

        def _depthwise_conv3_same(x, w, b):
            xp = jnp.pad(x, ((0, 0), (1, 1), (0, 0)))
            return xp[:, :-2] * w[:, 0] + xp[:, 1:-1] * w[:, 1] + xp[:, 2:] * w[:, 2] + b

        def _selective_scan(x, A, Wb, bb, Wc, bc, Wdt, bdt):
            dt = jax.nn.softplus(x @ Wdt + bdt)
            Bm = x @ Wb + bb
            Cm = x @ Wc + bc
            dA = jnp.exp(dt[..., None] * A)
            dBx = dt[..., None] * Bm[:, :, None, :] * x[..., None]

            def step(h, ins):
                dA_t, dBx_t, C_t = ins
                h = dA_t * h + dBx_t
                y = jnp.einsum('bdn,bn->bd', h, C_t)
                return (h, y)
            h0 = jnp.zeros((x.shape[0], x.shape[2], A.shape[1]), x.dtype)
            _, ys = jax.lax.scan(step, h0, (dA.transpose(1, 0, 2, 3), dBx.transpose(1, 0, 2, 3), Cm.transpose(1, 0, 2)))
            return ys.transpose(1, 0, 2)
        x = u @ Win + b_in
        x = _depthwise_conv3_same(x, convw, convb)
        x = jax.nn.silu(x)
        x_ssm = _selective_scan(x, A, Wb, bb, Wc, bc, Wdt, bdt)
        z = jax.nn.silu(u @ Wg + bg)
        return x_ssm * z @ Wout + bout

    def _L1_xattn_ref(query, key_value, Wq, bq, Wk, bk, Wv, bv, Wo, bo):
        import jax, jax.numpy as jnp
        import numpy as np
        NUM_HEADS = 16
        CLAMP = 10000.0
        B, Nq, Cq = query.shape
        Nkv = key_value.shape[1]
        H = NUM_HEADS
        D = Cq // H
        scale = D ** (-0.5)
        q = (query @ Wq + bq).reshape(B, Nq, H, D).transpose(0, 2, 1, 3)
        k = (key_value @ Wk + bk).reshape(B, Nkv, H, D).transpose(0, 2, 1, 3)
        v = (key_value @ Wv + bv).reshape(B, Nkv, H, D).transpose(0, 2, 1, 3)
        attn = jnp.einsum('bhqd,bhkd->bhqk', q, k) * scale
        attn = jnp.clip(attn, -CLAMP, CLAMP)
        attn = jax.nn.softmax(attn, axis=-1)
        attn = jnp.where(jnp.any(jnp.isnan(attn)), jnp.asarray(1.0 / Nkv, attn.dtype), attn)
        x = jnp.einsum('bhqk,bhkd->bqhd', attn, v).reshape(B, Nq, Cq)
        return x @ Wo + bo

    def _L1_ffn_ref(x, ln1_w, ln2_w, wq, wk, wv, wo, gate_w, w1, w2, w3):
        import jax, jax.numpy as jnp
        import numpy as np
        EPS = 1e-05
        TOP_K = 2

        def _rmsnorm(x, w):
            xf = x.astype(jnp.float32)
            rms = jax.lax.rsqrt(jnp.mean(xf * xf, axis=-1, keepdims=True) + EPS)
            return (xf * rms).astype(x.dtype) * w

        def _attention(x, wq, wk, wv, wo, num_heads=16):
            B, S, H = x.shape
            D = H // num_heads
            q = (x @ wq.T).reshape(B, S, num_heads, D)
            k = (x @ wk.T).reshape(B, S, num_heads, D)
            v = (x @ wv.T).reshape(B, S, num_heads, D)
            scale = 1.0 / jnp.sqrt(jnp.float32(D)).astype(x.dtype)
            scores = jnp.einsum('bqhd,bkhd->bhqk', q, k) * scale
            probs = jax.nn.softmax(scores, axis=-1)
            out = jnp.einsum('bhqk,bkhd->bqhd', probs, v).reshape(B, S, H)
            return out @ wo.T

        def _moe(x, gate_w, w1, w2, w3):
            B, S, H = x.shape
            xf = x.reshape(-1, H)
            logits = xf @ gate_w.T
            rw, sel = jax.lax.top_k(logits, TOP_K)
            rw = jax.nn.softmax(rw.astype(jnp.float32), axis=-1).astype(x.dtype)
            E = gate_w.shape[0]
            out = jnp.zeros_like(xf)
            for e in range(E):
                we = jnp.sum(jnp.where(sel == e, rw, 0.0), axis=-1)
                h = jax.nn.silu(xf @ w1[e].T) * (xf @ w3[e].T)
                out = out + h @ w2[e].T * we[:, None]
            return out.reshape(B, S, H)
        h = x + _attention(_rmsnorm(x, ln1_w), wq, wk, wv, wo)
        h = h + _moe(_rmsnorm(h, ln2_w), gate_w, w1, w2, w3)
        return h

    def _L2_attn_ref(x, w_qkv, b_qkv, w_out, b_out):
        import jax, jax.numpy as jnp
        import numpy as np
        import math
        B, S, DM, H, F = (2, 256, 128, 16, 192)
        DH = F // 3
        MAX_BIAS = 8.0

        def _get_slopes(n):

            def pow2(n):
                start = 2.0 ** (-2.0 ** (-(math.log2(n) - 3)))
                return [start * start ** i for i in range(n)]
            if math.log2(n).is_integer():
                return pow2(n)
            cp2 = 2 ** math.floor(math.log2(n))
            return pow2(cp2) + _get_slopes(2 * cp2)[0::2][:n - cp2]

        def _rope_sin_cos(seq_len, dim):
            inv_freq = 1.0 / 10000.0 ** (jnp.arange(0, dim, 2, dtype=jnp.float32) / dim)
            freqs = jnp.outer(jnp.arange(seq_len, dtype=jnp.float32), inv_freq)
            sin = jnp.concatenate([jnp.sin(freqs), jnp.sin(freqs)], axis=-1)
            cos = jnp.concatenate([jnp.cos(freqs), jnp.cos(freqs)], axis=-1)
            return (sin, cos)

        def _rotate_half(x):
            x1, x2 = jnp.split(x, 2, axis=-1)
            return jnp.concatenate([-x2, x1], axis=-1)
        b, s, dm = x.shape
        h, f = (w_qkv.shape[1], w_qkv.shape[2])
        dh = f // 3
        qkv = jnp.einsum('bsd,dhf->bshf', x, w_qkv) + b_qkv
        q, k, v = jnp.split(qkv, 3, axis=-1)
        sin, cos = _rope_sin_cos(s, dh)
        sin, cos = (sin[:, None, :], cos[:, None, :])
        q = q * cos + _rotate_half(q) * sin
        k = k * cos + _rotate_half(k) * sin
        q = q.transpose(0, 2, 1, 3)
        k = k.transpose(0, 2, 1, 3)
        v = v.transpose(0, 2, 1, 3)
        scores = jnp.einsum('bhqd,bhkd->bhqk', q, k) / jnp.sqrt(jnp.float32(f))
        slopes = jnp.asarray(_get_slopes(h), dtype=jnp.float32)
        pos = jnp.arange(s, dtype=jnp.float32)
        rel = pos[None, :] - pos[:, None]
        rel = jnp.where(rel > 0, 0.0, rel)
        alibi = rel[None, :, :] * slopes[:, None, None] * MAX_BIAS
        scores = scores + alibi[None]
        causal = jnp.tril(jnp.ones((s, s), dtype=jnp.float32))
        scores = jnp.where(causal == 0, -1000000000.0, scores)
        weights = jax.nn.softmax(scores, axis=-1)
        attn = jnp.einsum('bhqk,bhkd->bhqd', weights, v).transpose(0, 2, 1, 3)
        return jnp.einsum('bshd,hdm->bsm', attn, w_out) + b_out

    def _L2_xattn_ref(x, context, Wq, Wk, Wv, Wout, bout):
        import jax, jax.numpy as jnp
        import numpy as np
        HEADS = 8
        DIM_HEAD = 64
        SCALE = DIM_HEAD ** (-0.5)
        b, n, _ = x.shape
        m = context.shape[1]
        q = (x @ Wq).reshape(b, n, HEADS, DIM_HEAD)
        k = (context @ Wk).reshape(b, m, HEADS, DIM_HEAD)
        v = (context @ Wv).reshape(b, m, HEADS, DIM_HEAD)
        sim = jnp.einsum('bihd,bjhd->bhij', q, k) * SCALE
        attn = jax.nn.softmax(sim, axis=-1)
        out = jnp.einsum('bhij,bjhd->bihd', attn, v).reshape(b, n, HEADS * DIM_HEAD)
        return out @ Wout + bout

    def _L2_ffn_ref(x, g1, g2, wq, wk, wv, wo, gate, w1, w2, w3):
        import jax, jax.numpy as jnp
        import numpy as np
        DIM = 128
        N_HEADS = 16
        N_KV_HEADS = 4
        HEAD_DIM = DIM // N_HEADS
        N_REP = N_HEADS // N_KV_HEADS
        N_EXPERTS = 4
        TOP_K = 2
        HIDDEN = 3 * DIM
        EPS = 1.1920928955078125e-07

        def _rmsnorm(x, g):
            var = jnp.mean(jnp.square(x), axis=-1, keepdims=True)
            return x * jax.lax.rsqrt(var + EPS) * g

        def _rotate_half(x):
            x1, x2 = jnp.split(x, 2, axis=-1)
            return jnp.concatenate([-x2, x1], axis=-1)

        def _rope_tables(S):
            inv_freq = 1.0 / 10000.0 ** (jnp.arange(0, HEAD_DIM, 2, dtype=jnp.float32) / HEAD_DIM)
            freqs = jnp.arange(S, dtype=jnp.float32)[:, None] * inv_freq[None, :]
            emb = jnp.concatenate([freqs, freqs], axis=-1)
            return (jnp.cos(emb), jnp.sin(emb))

        def _attention(x, wq, wk, wv, wo):
            B, S, D = x.shape
            q = (x @ wq).reshape(B, S, N_HEADS, HEAD_DIM).transpose(0, 2, 1, 3)
            k = (x @ wk).reshape(B, S, N_KV_HEADS, HEAD_DIM).transpose(0, 2, 1, 3)
            v = (x @ wv).reshape(B, S, N_KV_HEADS, HEAD_DIM).transpose(0, 2, 1, 3)
            cos, sin = _rope_tables(S)
            q = q * cos + _rotate_half(q) * sin
            k = k * cos + _rotate_half(k) * sin
            k = jnp.repeat(k, N_REP, axis=1)
            v = jnp.repeat(v, N_REP, axis=1)
            scores = jnp.einsum('bhqd,bhkd->bhqk', q, k) / jnp.sqrt(jnp.float32(HEAD_DIM))
            causal = jnp.tril(jnp.ones((S, S), dtype=bool))
            scores = jnp.where(causal, scores, -jnp.inf)
            attn = jax.nn.softmax(scores, axis=-1)
            out = jnp.einsum('bhqk,bhkd->bhqd', attn, v)
            return out.transpose(0, 2, 1, 3).reshape(B, S, D) @ wo

        def _moe(x, gate, w1, w2, w3):
            B, S, D = x.shape
            xf = x.reshape(-1, D)
            probs = jax.nn.softmax(xf @ gate, axis=-1)
            w, idx = jax.lax.top_k(probs, TOP_K)
            w = w / jnp.sum(w, axis=-1, keepdims=True)
            oh = jax.nn.one_hot(idx, N_EXPERTS, dtype=xf.dtype)
            comb = jnp.einsum('nk,nke->ne', w, oh)
            out = jnp.zeros_like(xf)
            for e in range(N_EXPERTS):
                h = jax.nn.silu(xf @ w1[e]) * (xf @ w3[e])
                out = out + comb[:, e:e + 1] * (h @ w2[e])
            return out.reshape(B, S, D)
        x = x + _attention(_rmsnorm(x, g1), wq, wk, wv, wo)
        x = x + _moe(_rmsnorm(x, g2), gate, w1, w2, w3)
        return x

    def _L3_attn_ref(x, Wq, Wk, Wv, Wr):
        import jax, jax.numpy as jnp
        import numpy as np
        SCALE = 128 ** (-0.5)
        query = jnp.einsum('bsd,de->bse', x, Wq)
        key_ = jnp.einsum('bsd,de->bse', x, Wk)
        value = jnp.einsum('bsd,de->bse', x, Wv)
        alpha = jax.nn.softmax(query * SCALE, axis=-1)
        global_query = jnp.sum(query * alpha, axis=1)
        p = global_query[:, None, :] * key_
        beta = jax.nn.softmax(p * SCALE, axis=-1)
        global_key = jnp.sum(p * beta, axis=1)
        u = global_key[:, None, :] * value
        r = jnp.einsum('bsd,de->bse', u, Wr)
        return query + r

    def _L3_xattn_ref(x, context, Wq, Wk, Wv, Wo, bo, q_down, q_up, q_alpha, k_down, k_up, k_alpha, v_down, v_up, v_alpha, o_down, o_up, o_alpha, Wk_ipa, Wv_ipa):
        import jax, jax.numpy as jnp
        import numpy as np
        HEADS = 16
        DIM_HEAD = 64
        RANK = 32
        LORA_W = 1.0
        IPA_SCALE = 1.0
        IPA_TOKENS = 4
        SCALE = DIM_HEAD ** (-0.5)

        def _split_heads(t):
            b, n, _ = t.shape
            return t.reshape(b, n, HEADS, DIM_HEAD).transpose(0, 2, 1, 3)

        def _merge_heads(t):
            b, h, n, d = t.shape
            return t.transpose(0, 2, 1, 3).reshape(b, n, h * d)

        def _attention(q_in, k_in, v_in):
            q = _split_heads(q_in)
            k = _split_heads(k_in)
            v = _split_heads(v_in)
            s = jnp.einsum('bhid,bhjd->bhij', q, k) * SCALE
            p = jax.nn.softmax(s, axis=-1)
            o = jnp.einsum('bhij,bhjd->bhid', p, v)
            return _merge_heads(o)

        def _lora(t, down, up, alpha):
            return t @ down @ up * (LORA_W * alpha[0] / RANK)
        q_in = x @ Wq + _lora(x, q_down, q_up, q_alpha)
        end = context.shape[1] - IPA_TOKENS
        org_ctx = context[:, :end, :]
        ipa_ctx = context[:, end:, :]
        k_in = org_ctx @ Wk + _lora(org_ctx, k_down, k_up, k_alpha)
        v_in = org_ctx @ Wv + _lora(org_ctx, v_down, v_up, v_alpha)
        out = _attention(q_in, k_in, v_in)
        ipa_k = ipa_ctx @ Wk_ipa
        ipa_v = ipa_ctx @ Wv_ipa
        out_ipa = _attention(q_in, ipa_k, ipa_v)
        out = out + IPA_SCALE * out_ipa
        return out @ Wo + bo + _lora(out, o_down, o_up, o_alpha)

    def _L3_ffn_ref(hidden_states, router_weight, e_bias, gate_w, up_w, down_w, sh_gate_w, sh_up_w, sh_down_w):
        import jax, jax.numpy as jnp
        import numpy as np
        B, S, H = (1, 256, 128)
        E, K = (16, 4)
        G, TG = (4, 2)
        I_MOE = 64
        N_SH = 2
        SCALE = 2.5

        def _mlp(x, gw, uw, dw):
            return jax.nn.silu(x @ gw.T) * (x @ uw.T) @ dw.T

        def _route(x2d, router_weight, e_bias):
            T = x2d.shape[0]
            scores = jax.nn.sigmoid(x2d @ router_weight.T)
            sc = scores + e_bias[None, :]
            group_scores = jnp.sum(jax.lax.top_k(sc.reshape(T, G, E // G), 2)[0], axis=-1)
            _, gidx = jax.lax.top_k(group_scores, TG)
            gmask = jnp.zeros((T, G), sc.dtype).at[jnp.arange(T)[:, None], gidx].set(1.0)
            smask = jnp.repeat(gmask, E // G, axis=1)
            masked = jnp.where(smask > 0, sc, 0.0)
            _, tidx = jax.lax.top_k(masked, K)
            tw = jnp.take_along_axis(scores, tidx, axis=1)
            tw = tw / (jnp.sum(tw, axis=-1, keepdims=True) + 1e-20)
            tw = tw * SCALE
            return (tidx, tw)

        def _moe_forward(hidden_states, router_weight, e_bias, gate_w, up_w, down_w, sh_gate_w, sh_up_w, sh_down_w):
            orig_shape = hidden_states.shape
            x = hidden_states.reshape(-1, H)
            T = x.shape[0]
            tidx, tw = _route(x, router_weight, e_bias)
            g = jnp.einsum('th,eih->tei', x, gate_w)
            u = jnp.einsum('th,eih->tei', x, up_w)
            h = jax.nn.silu(g) * u
            yo = jnp.einsum('tei,ehi->teh', h, down_w)
            combine = jnp.zeros((T, E), tw.dtype).at[jnp.arange(T)[:, None], tidx].add(tw)
            routed = jnp.einsum('te,teh->th', combine, yo)
            shared = _mlp(hidden_states.reshape(-1, H), sh_gate_w, sh_up_w, sh_down_w)
            return (routed + shared).reshape(orig_shape)
        return _moe_forward(hidden_states, router_weight, e_bias, gate_w, up_w, down_w, sh_gate_w, sh_up_w, sh_down_w)
    x = _layernorm(x + _L0_attn_ref(x, L0_attn_Wq, L0_attn_gq, L0_attn_bq, L0_attn_Wk, L0_attn_gk, L0_attn_bk, L0_attn_Wv, L0_attn_gv, L0_attn_bv, L0_attn_Wp, L0_attn_bp), axis=-1)
    x = _layernorm(x + _L0_xattn_ref(x, ctx_768, L0_xattn_Wq, L0_xattn_bq, L0_xattn_Wkv, L0_xattn_bkv, L0_xattn_Wo, L0_xattn_bo), axis=-1)
    x = _layernorm(x + _L0_ffn_ref(x, L0_ffn_ln1_weight, L0_ffn_ln1_bias, L0_ffn_ln2_weight, L0_ffn_ln2_bias, L0_ffn_qkv_weight, L0_ffn_proj_weight, L0_ffn_router_weight, L0_ffn_moe_w1, L0_ffn_moe_w2), axis=-1)
    x = _layernorm(x + _L1_attn_ref(x, L1_attn_Win, L1_attn_b_in, L1_attn_Wg, L1_attn_bg, L1_attn_Wout, L1_attn_bout, L1_attn_convw, L1_attn_convb, L1_attn_A, L1_attn_Wb, L1_attn_bb, L1_attn_Wc, L1_attn_bc, L1_attn_Wdt, L1_attn_bdt), axis=-1)
    x = _layernorm(x + _L1_xattn_ref(x, ctx_768, L1_xattn_Wq, L1_xattn_bq, L1_xattn_Wk, L1_xattn_bk, L1_xattn_Wv, L1_xattn_bv, L1_xattn_Wo, L1_xattn_bo), axis=-1)
    x = _layernorm(x + _L1_ffn_ref(x, L1_ffn_ln1_w, L1_ffn_ln2_w, L1_ffn_wq, L1_ffn_wk, L1_ffn_wv, L1_ffn_wo, L1_ffn_gate_w, L1_ffn_w1, L1_ffn_w2, L1_ffn_w3), axis=-1)
    x = _layernorm(x + _L2_attn_ref(x, L2_attn_w_qkv, L2_attn_b_qkv, L2_attn_w_out, L2_attn_b_out), axis=-1)
    x = _layernorm(x + _L2_xattn_ref(x, ctx_768, L2_xattn_Wq, L2_xattn_Wk, L2_xattn_Wv, L2_xattn_Wout, L2_xattn_bout), axis=-1)
    x = _layernorm(x + _L2_ffn_ref(x, L2_ffn_g1, L2_ffn_g2, L2_ffn_wq, L2_ffn_wk, L2_ffn_wv, L2_ffn_wo, L2_ffn_gate, L2_ffn_w1, L2_ffn_w2, L2_ffn_w3), axis=-1)
    x = _layernorm(x + _L3_attn_ref(x, L3_attn_Wq, L3_attn_Wk, L3_attn_Wv, L3_attn_Wr), axis=-1)
    x = _layernorm(x + _L3_xattn_ref(x, ctx_768, L3_xattn_Wq, L3_xattn_Wk, L3_xattn_Wv, L3_xattn_Wo, L3_xattn_bo, L3_xattn_q_down, L3_xattn_q_up, L3_xattn_q_alpha, L3_xattn_k_down, L3_xattn_k_up, L3_xattn_k_alpha, L3_xattn_v_down, L3_xattn_v_up, L3_xattn_v_alpha, L3_xattn_o_down, L3_xattn_o_up, L3_xattn_o_alpha, L3_xattn_Wk_ipa, L3_xattn_Wv_ipa), axis=-1)
    x = _layernorm(x + _L3_ffn_ref(x, L3_ffn_router_weight, L3_ffn_e_bias, L3_ffn_gate_w, L3_ffn_up_w, L3_ffn_down_w, L3_ffn_sh_gate_w, L3_ffn_sh_up_w, L3_ffn_sh_down_w), axis=-1)
    return x

_drawn_inputs = setup_inputs


def setup_inputs(seed=0):
    import zlib

    import numpy as np

    out = dict(_drawn_inputs(seed))
    spreads = {'L0_attn_gq': (1.0, 0.2),
     'L0_attn_bq': (0.0, 0.1),
     'L0_attn_gk': (1.0, 0.2),
     'L0_attn_bk': (0.0, 0.1),
     'L0_attn_gv': (1.0, 0.2),
     'L0_attn_bv': (0.0, 0.1),
     'L0_attn_bp': (0.0, 0.1),
     'L0_ffn_ln1_weight': (1.0, 0.6),
     'L0_ffn_ln1_bias': (0.0, 0.8),
     'L0_ffn_ln2_weight': (1.0, 0.6),
     'L0_ffn_ln2_bias': (0.0, 0.8),
     'L1_attn_b_in': (0.0, 0.1),
     'L1_attn_bg': (0.0, 0.341),
     'L1_attn_bout': (0.0, 0.1),
     'L1_attn_convb': (0.0, 0.1),
     'L1_attn_bb': (0.0, 0.1),
     'L1_attn_bc': (0.0, 0.1),
     'L1_attn_bdt': (-2.0, 0.6),
     'L1_xattn_bq': (0.0, 0.1),
     'L1_xattn_bk': (0.0, 0.8),
     'L1_xattn_bv': (0.0, 0.1),
     'L1_xattn_bo': (0.0, 0.1),
     'L1_ffn_ln1_w': (1.0, 0.6),
     'L1_ffn_ln2_w': (1.0, 0.6),
     'L2_attn_b_qkv': (0.0, 0.1),
     'L2_attn_b_out': (0.0, 0.1),
     'L2_ffn_g1': (1.0, 0.6),
     'L2_ffn_g2': (1.0, 0.6),
     'L3_xattn_bo': (0.0, 0.1),
     'L3_ffn_e_bias': (0.0, 0.8)}
    factors = {'L0_xattn_bq': 8.0,
     'L0_xattn_bkv': 3.168,
     'L0_xattn_bo': 3.387,
     'L0_ffn_router_weight': 8.0,
     'L0_ffn_moe_w1': 8.0,
     'L0_ffn_moe_w2': 8.0,
     'L1_ffn_wq': 8.0,
     'L1_ffn_wk': 8.0,
     'L1_ffn_gate_w': 8.0,
     'L1_ffn_w1': 8.0,
     'L1_ffn_w2': 8.0,
     'L1_ffn_w3': 8.0,
     'L2_ffn_wq': 8.0,
     'L2_ffn_wk': 8.0,
     'L2_ffn_gate': 8.0,
     'L2_ffn_w1': 8.0,
     'L2_ffn_w2': 8.0,
     'L2_ffn_w3': 8.0,
     'L3_xattn_Wq': 8.0,
     'L3_xattn_Wk': 8.0,
     'L3_xattn_q_down': 8.0,
     'L3_xattn_q_up': 8.0,
     'L3_xattn_k_down': 8.0,
     'L3_xattn_k_up': 8.0,
     'L3_xattn_v_down': 7.383,
     'L3_xattn_v_up': 7.922,
     'L3_xattn_o_down': 4.783,
     'L3_xattn_o_up': 5.104,
     'L3_xattn_Wk_ipa': 8.0,
     'L3_ffn_router_weight': 8.0,
     'L3_ffn_gate_w': 8.0,
     'L3_ffn_up_w': 8.0,
     'L3_ffn_down_w': 8.0,
     'L3_ffn_sh_gate_w': 8.0,
     'L3_ffn_sh_up_w': 8.0,
     'L3_ffn_sh_down_w': 8.0}
    for name, (base, spread) in spreads.items():
        noise = np.random.default_rng([zlib.crc32(name.encode()), seed]).standard_normal(out[name].shape)
        drawn = base * np.exp(spread * noise) if base else spread * noise
        out[name] = jnp.asarray(drawn.astype(out[name].dtype))
    for name, factor in factors.items():
        out[name] = (out[name] * factor).astype(out[name].dtype)
    return out
```

```python
import math
from contextlib import ExitStack, contextmanager

import numpy as np
import concourse.bass as bass
from concourse import mybir

F32 = mybir.dt.float32
BF16 = mybir.dt.bfloat16
ALU = mybir.AluOpType
ACT = mybir.ActivationFunctionType
AX = mybir.AxisListType

FIRST, LAST = 0, 12

B, N, D = 4, 512, 128
TOK = B * N
TILES = TOK // 128
QT = N // 128
CTX, CD = 77, 96
IPA = 4
NH = 16
GROUP = 4
RANK = 32
NEG = -1e30
BANK_S, BANK_ST, BANK_PV, BANK_V, BANK_A = 0, 2, 4, 6, 7

STAGES = ["L0_attn", "L0_xattn", "L0_ffn", "L1_attn", "L1_xattn", "L1_ffn",
          "L2_attn", "L2_xattn", "L2_ffn", "L3_attn", "L3_xattn", "L3_ffn"]


def spread_heads(w, heads, dh, rep=1):
    out = np.zeros((w.shape[0], heads * rep * 32), np.float32)
    for h in range(heads * rep):
        out[:, 32 * h:32 * h + dh] = w[:, (h // rep) * dh:(h // rep + 1) * dh]
    return out


def spread_bias(b, heads, dh, aug, rep=1):
    v = np.zeros((heads * rep, 32), np.float32)
    if b is not None:
        v[:, :dh] = np.repeat(b.reshape(heads, dh), rep, axis=0)
    v[:, dh] = aug
    return v.reshape(-1, 128).T


def half_turn(w, dh):
    v = w.reshape(w.shape[0], -1, 2, dh // 2)
    return v[:, :, ::-1].reshape(w.shape)


def rope_tables(dh, period, aug):
    inv = 1.0 / 10000.0 ** (np.arange(0, dh, 2, dtype=np.float32) / np.float32(dh))
    ang = np.outer(np.arange(N, dtype=np.float32), inv.astype(np.float32)).astype(np.float32)
    ang = np.concatenate([ang, ang], axis=1).T
    cos, sin = np.zeros((128, N), np.float32), np.zeros((128, N), np.float32)
    for r0 in range(0, 128, period):
        cos[r0:r0 + dh] = np.cos(ang)
        sin[r0:r0 + dh] = np.sin(ang)
        sin[r0:r0 + dh // 2] = -np.sin(ang[:dh // 2])
        if aug:
            cos[r0 + dh] = 1.0
    return cos, sin


def slopes():
    start = 2.0 ** (-2.0 ** (-(math.log2(NH) - 3)))
    return [8.0 * start * start ** i for i in range(NH)]


def kv_cols(w, out):
    return w.transpose(1, 0, 2).reshape(w.shape[1], -1)


def rows_tiled(w, tile=128):
    return w.reshape(-1, tile, w.shape[1]).transpose(1, 0, 2).reshape(tile, -1)


def row(v):
    return v.reshape(1, -1)


def pieces(stage, a):
    g = lambda n: a[f"{stage}_{n}"]
    if stage == "L0_attn":
        return dict(wq=g("Wq").T, wk=g("Wk").T, wv=g("Wv").T, wp=g("Wp").T, bp=row(g("bp")),
                    gam=np.stack([g("gq"), g("gk"), g("gv")], 1), bet=np.stack([g("bq"), g("bk"), g("bv")], 1),
                    blocks=np.kron(np.eye(16), np.ones((8, 8))))
    if stage == "L0_xattn":
        wkv, bkv = g("Wkv").reshape(NH, 2, 8, CD), g("bkv").reshape(NH, 2, 8)
        return dict(wq=spread_heads(g("Wq").T, NH, 8), wk=spread_heads(wkv[:, 0].reshape(128, CD).T, NH, 8),
                    wv=wkv[:, 1].reshape(128, CD).T, wo=g("Wo").T,
                    bq=spread_bias(g("bq"), NH, 8, 0), bk=spread_bias(bkv[:, 0], NH, 8, 1),
                    bv=row(bkv[:, 1]), bo=row(g("bo")))
    if stage == "L0_ffn":
        qkv = g("qkv_weight")
        k, v = (np.repeat(qkv[128 + 32 * i:160 + 32 * i].reshape(4, 8, 128), 4, axis=0).reshape(128, 128).T for i in (0, 1))
        return dict(n1w=g("ln1_weight").reshape(-1, 1), n1b=g("ln1_bias").reshape(-1, 1),
                    n2w=g("ln2_weight").reshape(-1, 1), n2b=g("ln2_bias").reshape(-1, 1),
                    wqkv=np.concatenate([qkv[:128].T, k, v], 1), wo=g("proj_weight").T, router=g("router_weight").T,
                    w1=kv_cols(g("moe_w1"), 256), w2=rows_tiled(g("moe_w2").reshape(-1, 128)))
    if stage == "L1_attn":
        return dict(win=g("Win"), wg=g("Wg"), wout=g("Wout"), wdt=g("Wdt"), wb=g("Wb"), wc=g("Wc"), a=g("A"),
                    bin=g("b_in").reshape(-1, 1), bg=g("bg").reshape(-1, 1), convw=g("convw"),
                    convb=g("convb").reshape(-1, 1), bdt=g("bdt").reshape(-1, 1),
                    bb=np.broadcast_to(g("bb"), (128, 16)), bc=np.broadcast_to(g("bc"), (128, 16)), bout=row(g("bout")))
    if stage == "L1_xattn":
        pick = np.zeros((128, CTX), np.float32)
        pick[8::32] = 1.0
        return dict(wq=spread_heads(g("Wq"), NH, 8), wk=spread_heads(g("Wk"), NH, 8), wv=g("Wv"), wo=g("Wo"),
                    bq=spread_bias(g("bq"), NH, 8, 0), bk=spread_bias(g("bk"), NH, 8, 1),
                    bv=row(g("bv")), bo=row(g("bo")), pick=pick)
    if stage == "L1_ffn":
        return dict(n1w=g("ln1_w").reshape(-1, 1), n2w=g("ln2_w").reshape(-1, 1),
                    wq=spread_heads(g("wq").T, NH, 8), wk=spread_heads(g("wk").T, NH, 8), wv=g("wv").T, wo=g("wo").T,
                    bq=spread_bias(None, NH, 8, 0), bk=spread_bias(None, NH, 8, 1), router=g("gate_w").T,
                    w1=kv_cols(g("w1").transpose(0, 2, 1), 256), w3=kv_cols(g("w3").transpose(0, 2, 1), 256),
                    w2=rows_tiled(g("w2").transpose(0, 2, 1).reshape(-1, 128)))
    if stage == "L2_attn":
        w, b = g("w_qkv").reshape(128, NH, 3, 64), g("b_qkv").reshape(NH, 3, 64)
        q, k, v = (w[:, :, i].reshape(128, 1024) for i in range(3))
        bq, bk, bv = (b[:, i].reshape(1, 1024) for i in range(3))
        cos, sin = rope_tables(64, 64, False)
        cols = lambda r: r.reshape(8, 128).T
        return dict(wq=q, wqt=half_turn(q, 64), wk=k, wkt=half_turn(k, 64), wv=v,
                    bq=cols(bq), bqt=cols(half_turn(bq, 64)), bk=cols(bk), bkt=cols(half_turn(bk, 64)), bv=bv,
                    wo=rows_tiled(g("w_out").reshape(1024, 128)), bo=row(g("b_out")), cos=cos, sin=sin)
    if stage == "L2_xattn":
        return dict(wq=g("Wq"), wk=g("Wk"), wv=g("Wv"), wo=rows_tiled(g("Wout")), bo=row(g("bout")))
    if stage == "L2_ffn":
        cos, sin = rope_tables(8, 32, True)
        return dict(n1w=g("g1").reshape(-1, 1), n2w=g("g2").reshape(-1, 1),
                    wq=spread_heads(g("wq"), NH, 8), wqt=spread_heads(half_turn(g("wq"), 8), NH, 8),
                    wk=spread_heads(g("wk"), 4, 8, 4), wkt=spread_heads(half_turn(g("wk"), 8), 4, 8, 4),
                    wv=g("wv"), wo=g("wo"), bq=spread_bias(None, NH, 8, 0), bk=spread_bias(None, NH, 8, 1),
                    router=g("gate"), w1=kv_cols(g("w1"), 384), w3=kv_cols(g("w3"), 384),
                    w2=rows_tiled(g("w2").reshape(-1, 128)), cos=cos, sin=sin)
    if stage == "L3_attn":
        return dict(wq=g("Wq"), wk=g("Wk"), wvt=g("Wv").T, wr=g("Wr"))
    if stage == "L3_xattn":
        seg = np.zeros((CTX, 2), np.float32)
        seg[:CTX - IPA, 0] = 1.0
        seg[CTX - IPA:, 1] = 1.0
        alpha = np.concatenate([np.broadcast_to(g(f"{n}_alpha"), (RANK, 1)) for n in "qkvo"], 1)
        return dict(wq=g("Wq"), wk=g("Wk"), wki=g("Wk_ipa"), wv=g("Wv"), wvi=g("Wv_ipa"), wo=rows_tiled(g("Wo")),
                    qd=g("q_down"), kd=g("k_down"), vd=g("v_down"), qu=g("q_up"), ku=g("k_up"), vu=g("v_up"),
                    od=rows_tiled(g("o_down")), ou=g("o_up"), bo=row(g("bo")), seg=seg, alpha=alpha)
    gate, up = (g(n).reshape(8, 128, 128).transpose(2, 0, 1).reshape(128, 1024) for n in ("gate_w", "up_w"))
    return dict(router=g("router_weight").T, ebias=np.broadcast_to(g("e_bias"), (128, 16)),
                w1=np.concatenate([gate, g("sh_gate_w").T], 1), w3=np.concatenate([up, g("sh_up_w").T], 1),
                w2=np.concatenate([rows_tiled(g("down_w").transpose(0, 2, 1).reshape(1024, 128)), g("sh_down_w").T], 1))


def pack(stage, a):
    ps = pieces(stage, a)
    where, at = {}, 0
    for n, p in ps.items():
        where[n] = (p.shape[0], at, p.shape[1])
        at += p.shape[1]
    out = np.zeros((128, at), np.float32)
    for n, p in ps.items():
        r, c, w = where[n]
        out[:r, c:c + w] = p
    return out, where


def constants():
    i = np.arange(128)
    ident = np.eye(128, dtype=np.float32)
    over = np.where(i[None, :] > i[:, None], np.float32(NEG), np.float32(0))
    before = np.broadcast_to((np.arange(16)[None, :] < np.arange(16)[:, None]).astype(np.float32).reshape(1, 256), (128, 256))
    return np.concatenate([ident, over, over.T, before], 1)


def key_rows():
    s = np.array(slopes(), np.float32)
    sc = np.float32(1.0 / math.sqrt(192.0))
    alibi = (s[:, None] * (np.arange(N, dtype=np.float32) - N // 2)[None, :] / sc).astype(np.float32)
    l2a = np.stack([alibi, np.ones_like(alibi)], 0).reshape(2, -1)
    l2x = np.ones((1, 8 * CTX), np.float32)
    seg = np.zeros((2, NH, CTX), np.float32)
    seg[0, :, :CTX - IPA] = 1.0
    seg[1, :, CTX - IPA:] = 1.0
    return l2a, l2x, seg.reshape(2, -1)


class Sems:

    def __init__(self, pool):
        self.pool, self.names = pool, {}

    def __call__(self, name):
        if name not in self.names:
            self.names[name] = self.pool[len(self.names)]
        return self.names[name]


class Ctx:
    pass


@contextmanager
def phase(k):
    s = Sems(k.pool)
    with k.nc.Block() as block:
        yield block, s
    for sem in s.names.values():
        k.nc.gpsimd.sem_clear(sem)
    k.nc.all_engine_barrier()


def weights(k, i):
    where, tile = k.where[i], k.W[i % 2]
    get = {n: tile[0:r, c:c + w] for n, (r, c, w) in where.items()}

    def ready(eng):
        eng.wait_ge(k.w_loaded[i], 16)
    return get, ready


def load_weights(k, i):
    if i >= LAST:
        return
    cols = k.wd[i].shape[1]
    k.nc.sync.dma_start(k.W[i % 2][:, 0:cols], k.wd[i]).then_inc(k.w_loaded[i], 16)


def normalise(k, i, src, dst, eps, rms=False, scale=None, shift=None, store=False, prefetch=None):
    nc = k.nc
    w, w_ready = weights(k, i)
    stats, mv, inv, rstd, nmr, sq = k.stats, k.mv, k.inv, k.rstd, k.nmr, k.sq
    P = k.P
    half = TILES // 2
    with phase(k) as (block, s):
        @block.sync
        def _(sp):
            if prefetch is not None:
                load_weights(k, prefetch)
            if store:
                sp.wait_ge(s("norm_v"), half)
                sp.wait_ge(s("norm_a"), half)
                sp.dma_start(k.out, dst[:]).then_inc(k.stored, 16)
                sp.wait_ge(k.stored, 16)

        @block.vector
        def _(v):
            for t in range(TILES):
                v.bn_stats(stats[:, t, :], src[:, t, :]).then_inc(s("stats"), 1)
            v.wait_ge(s("stats"), TILES)
            for t in range(TILES):
                v.bn_aggr(mv[:, t, :], stats[:, t, :]).then_inc(s("aggr"), 1)
            v.wait_ge(s("aggr"), TILES)
            if rms:
                v.tensor_tensor(sq[:], mv[:, :, 0], mv[:, :, 0], ALU.mult).then_inc(s("small"), 1)
                v.wait_ge(s("small"), 1)
                v.scalar_tensor_tensor(inv[:], sq[:], eps, mv[:, :, 1], ALU.add, ALU.add).then_inc(s("small"), 1)
            else:
                v.tensor_scalar(sq[:], mv[:, :, 0], -1.0, None, ALU.mult).then_inc(s("small"), 1)
                v.tensor_scalar(inv[:], mv[:, :, 1], eps, None, ALU.add).then_inc(s("small"), 1)
            v.wait_ge(s("small"), 2)
            v.reciprocal(inv[:], inv[:]).then_inc(s("inv"), 1)
            v.wait_ge(s("rstd"), 1)
            if not rms:
                v.tensor_tensor(nmr[:], sq[:], rstd[:], ALU.mult).then_inc(s("nmr"), 1)
            for t in range(0, TILES, 2):
                if rms:
                    v.tensor_scalar(dst[:, t, :], src[:, t, :], rstd[:, t:t + 1], None, ALU.mult).then_inc(s("norm_v"), 1)
                else:
                    v.tensor_scalar(dst[:, t, :], src[:, t, :], mv[:, t, 0:1], rstd[:, t:t + 1],
                                    ALU.subtract, ALU.mult).then_inc(s("norm_v"), 1)
            if not store:
                if scale is not None:
                    w_ready(v)
                for c in (1, 3):
                    v.wait_ge(s("turned"), c + 1)
                    o = k.XT[:, N * c:N * (c + 1)]
                    if scale is not None and shift is not None:
                        v.tensor_scalar(o, P[:, c, :], w[scale], w[shift], ALU.mult, ALU.add)
                    elif scale is not None:
                        v.tensor_scalar(o, P[:, c, :], w[scale], None, ALU.mult)
                    else:
                        v.tensor_copy(o, P[:, c, :])

        @block.scalar
        def _(a):
            a.wait_ge(s("inv"), 1)
            a.activation(rstd[:], inv[:], ACT.Sqrt).then_inc(s("rstd"), 1)
            a.wait_ge(s("rstd"), 1)
            if not rms:
                a.wait_ge(s("nmr"), 1)
            for t in range(1, TILES, 2):
                a.activation(dst[:, t, :], src[:, t, :], ACT.Identity, scale=rstd[:, t:t + 1],
                             bias=0.0 if rms else nmr[:, t:t + 1]).then_inc(s("norm_a"), 1)
            if not store:
                if scale is not None:
                    w_ready(a)
                for c in (0, 2):
                    a.wait_ge(s("turned"), c + 1)
                    a.activation(k.XT[:, N * c:N * (c + 1)], P[:, c, :], ACT.Identity,
                                 scale=1.0 if scale is None else w[scale], bias=0.0 if shift is None else w[shift])

        @block.tensor
        def _(pe):
            if not store:
                for c in range(4):
                    pe.wait_ge(s("norm_v"), 2 * (c + 1))
                    pe.wait_ge(s("norm_a"), 2 * (c + 1))
                    for t in range(4):
                        last = pe.transpose(P[:, c, 128 * t:128 * (t + 1)], dst[:, 4 * c + t, :], k.ident[:])
                    last.then_inc(s("turned"), 1)


class Attention:

    def __init__(self, k, heads, dh, nk, scale, causal=False, aug=1, segs=((0, None),), clip=None, vrep=1,
                 jobs=(), bo=None, wo=None, src=None, dst=None, lora=None, static=()):
        self.k, self.H, self.dh, self.nk, self.scale, self.causal, self.aug = k, heads, dh, nk, scale, causal, aug
        self.segs, self.clip, self.vrep, self.jobs, self.bo, self.wo = segs, clip, vrep, jobs, bo, wo
        self.src, self.dst, self.lora, self.static = src, dst, lora, static
        self.narrow = dh == 8
        self.gs = GROUP if self.narrow else 1
        self.kt = -(-nk // 128)
        self.kp = min(nk, 128)
        self.units = QT if nk == N else 1
        self.vc = (dh + 1) * len(segs)
        self.pv_units = 1 if QT * self.vc <= 512 else 2
        self.pv_ring = 1 if clip else 2
        self.groups = heads // self.gs
        self.nf = heads * dh // 128
        self.lag = self.gs + 1
        self.ot_ch = ["VA"[c % 2] for c in range(self.nf)]
        self.n_v = sum(j["ch"] == "V" for j in jobs) + self.groups + self.ot_ch.count("V") + 1
        self.n_a = sum(j["ch"] == "A" for j in jobs) + self.ot_ch.count("A") + (1 if lora else 0)
        self.n_rope = sum(j["kind"] == "rope2" for j in jobs)

    def rows(self, h, n):
        p = 32 * (h % GROUP) if self.narrow else 0
        return slice(p, p + n)

    def width(self, t):
        return N - 128 * t if self.causal else N

    def pe(self, pe, s, b):
        k, H, nk, kp = self.k, self.H, self.nk, self.kp
        P, QA, KA, VA, PT = k.P, k.QA, k.KA, k.VA, k.PT
        cnt = {"V": 0, "A": 0}
        per = {"V": self.n_v, "A": self.n_a}
        free = {"V": "v_free", "A": "a_free"}
        bank = {"V": BANK_V, "A": BANK_A}

        def evacuated(ch):
            pe.wait_ge(s(free[ch]), b * per[ch] + cnt[ch] + 1)

        def done(ins, ch):
            cnt[ch] += 1
            ins.then_inc(s("v_full" if ch == "V" else "a_full"), 1)

        pe.wait_ge(s("static"), (b + 1) * len(self.static))
        for j in self.jobs:
            if j.get("after"):
                evacuated("V")
                evacuated("A")
            evacuated(j["ch"])
            mms = j["mms"](b)
            for n, (l, r) in enumerate(mms):
                last = pe.matmul(P[0:j["m"], bank[j["ch"]], 0:j["n"]], l, r, start=n == 0, stop=n == len(mms) - 1)
            done(last, j["ch"])
        evacuated("V")
        evacuated("A")
        R0 = self.dh + (self.aug - 1 if not self.narrow and self.aug > len(self.segs) else 0)
        R = self.dh + self.aug
        sb, tb = [0], [0]

        def scores(h, u):
            pe.wait_ge(s("max_done"), b * H * self.units + sb[0] + 1)
            bk = BANK_S + sb[0] % 2
            sb[0] += 1
            q, kk = QA[self.rows(h, R0 if not self.narrow else R), h // self.gs, :], KA[self.rows(h, R0 if not self.narrow else R), h // self.gs, :]
            if self.units == 1:
                for t in range(QT):
                    last = pe.matmul(P[:, bk, nk * t:nk * (t + 1)], q[:, 128 * t:128 * (t + 1)], kk[:, 0:nk],
                                     start=True, stop=True)
            else:
                w = 128 * (u + 1) if self.causal else nk
                last = pe.matmul(P[:, bk, 0:w], q[:, 128 * u:128 * (u + 1)], kk[:, 0:w], start=True, stop=not self.causal)
                if self.causal:
                    last = pe.matmul(P[:, bk, w - 128:w], k.identb[:], k.maskq[:], start=False, stop=True)
            last.then_inc(s("score"), 1)

        def transposed(h, t):
            n = b * H * self.kt + tb[0]
            bk = BANK_ST + tb[0] % 2
            q, kk = QA[self.rows(h, R), h // self.gs, :], KA[self.rows(h, R), h // self.gs, :]
            if self.clip:
                pe.wait_ge(s("clipped"), n + 1)
                r = self.rows(h, self.dh)
                pe.matmul(P[0:kp, bk, :], KA[r, h // self.gs, 0:nk], QA[r, h // self.gs, :], start=True, stop=True)
                last = pe.matmul(P[0:kp, BANK_PV + 1, :], self.clip[self.rows(h, R), :], q, start=True, stop=True)
            else:
                pe.wait_ge(s("exp_done"), n + 1)
                w = self.width(t)
                last = pe.matmul(P[0:kp, bk, 0:w], kk[:, 128 * t:128 * t + kp], q[:, N - w:N], start=True, stop=not self.causal)
                if self.causal:
                    last = pe.matmul(P[0:kp, bk, 0:128], k.identb[:], k.maskk[:], start=False, stop=True)
            tb[0] += 1
            last.then_inc(s("score_t"), 1)

        def turn_max(g):
            pe.wait_ge(s("max_done"), b * H * self.units + (g + 1) * self.gs * self.units + 2)
            evacuated("V")
            for t in range(QT):
                if self.narrow:
                    last = pe.transpose(P[:, BANK_V, 128 * t:128 * (t + 1)], k.M8[:, t, 4 * g:4 * g + 4, :].rearrange("p h c -> p (h c)"), k.ident[:])
                else:
                    last = pe.transpose(P[0:self.aug, BANK_V, 128 * t:128 * (t + 1)], k.M64[:, t, g, 0:self.aug], k.ident[:])
            done(last, "V")

        def values(h):
            pe.wait_ge(s("exp_done"), (b * H + h + 1) * self.kt + 2)
            for u in range(self.pv_units):
                n = (b * H + h) * self.pv_units + u
                pe.wait_ge(s("norm_done"), n + 1)
                bk = BANK_PV + (h * self.pv_units + u) % self.pv_ring
                for ti in range(QT // self.pv_units):
                    t = u * (QT // self.pv_units) + ti
                    kts = range(t + 1) if self.causal else range(self.kt)
                    for kt in kts:
                        last = pe.matmul(P[:, bk, self.vc * ti:self.vc * (ti + 1)], PT[0:kp, h % 2, kt, 128 * t:128 * (t + 1)],
                                         VA[0:kp, kt, h // self.vrep, 0:self.vc], start=kt == 0, stop=kt == kts[-1])
                last.then_inc(s("value"), 1)

        for i in range(H + self.lag + 1):
            for u in range(QT):
                if i < H and u < self.units:
                    scores(i, u)
                if 0 <= i - self.lag < H:
                    if i - self.lag == (i - self.lag) // self.gs * self.gs and u == 0:
                        evacuated("V")
                    if u < self.kt:
                        transposed(i - self.lag, u)
            if i and i % self.gs == 0 and i // self.gs <= self.groups:
                turn_max(i // self.gs - 1)
            if i - self.lag - 1 >= 0:
                values(i - self.lag - 1)
        pe.wait_ge(s("norm_done"), (b + 1) * H * self.pv_units + self.pv_ring)
        for c in range(self.nf):
            ch = self.ot_ch[c]
            evacuated(ch)
            for t in range(QT):
                last = pe.transpose(P[:, bank[ch], 128 * t:128 * (t + 1)], k.O[:, t, 128 * c:128 * (c + 1)], k.ident[:])
            done(last, ch)
        evacuated("V")
        evacuated("A")
        if self.lora:
            for c in range(self.nf):
                last = pe.matmul(P[0:RANK, BANK_A, :], self.lora[0][:, RANK * c:RANK * (c + 1)], k.OT[:, c, :],
                                 start=c == 0, stop=c == self.nf - 1)
            done(last, "A")
            evacuated("A")
        for t in range(QT):
            mms = [(k.OT[:, c, 128 * t:128 * (t + 1)], self.wo[:, 128 * c:128 * (c + 1)]) for c in range(self.nf)]
            if self.lora:
                mms.append((k.TL[0:RANK, 3, 128 * t:128 * (t + 1)], self.lora[1]))
            if self.bo is not None:
                mms.append((k.ones[0:1, 0:128], self.bo))
            for n, (l, r) in enumerate(mms):
                last = pe.matmul(P[:, BANK_V, 128 * t:128 * (t + 1)], l, r, start=n == 0, stop=n == len(mms) - 1)
        done(last, "V")
        assert cnt == per, (cnt, per)

    def dve_start(self, v, s):
        v.sem_inc(s("v_free"), 1)
        v.sem_inc(s("max_done"), 2)
        v.sem_inc(s("norm_done"), self.pv_ring)
        if self.clip:
            v.sem_inc(s("clipped"), 1)

    def act_start(self, a, s):
        a.sem_inc(s("a_free"), 1)
        a.sem_inc(s("exp_done"), 2)

    def dve(self, v, s, b):
        k, H = self.k, self.H
        P = k.P
        cnt, ropes, nm, sb, tb, cl = [0], [0], [0], [0], [0], [0]

        def full():
            cnt[0] += 1
            v.wait_ge(s("v_full"), b * self.n_v + cnt[0])

        for j in self.jobs:
            if j["ch"] != "V":
                continue
            full()
            ps = P[0:j["m"], BANK_V, 0:j["n"]]
            if j["kind"] == "cols":
                v.tensor_scalar(j["dst"], ps, j["bias"], None, ALU.add).then_inc(s("v_free"), 1)
            elif j["kind"] == "scaled":
                v.tensor_scalar(j["dst"], ps, j["bias"], None, ALU.mult).then_inc(s("v_free"), 1)
            elif j["kind"] == "pair":
                v.tensor_copy(j["dst"][0], P[0:64, BANK_V, 0:j["n"]])
                v.tensor_copy(j["dst"][1], P[64:128, BANK_V, 0:j["n"]]).then_inc(s("v_free"), 1)
            elif j["kind"] == "rows":
                v.tensor_copy(j["dst"], ps.rearrange("p (h d) -> p h d", d=self.dh)).then_inc(s("v_free"), 1)
            elif j["kind"] == "rope1":
                v.scalar_tensor_tensor(k.R1, ps, j["bias"], j["tab"], ALU.add, ALU.mult).then_inc(s("v_free"), 1)
            elif j["kind"] == "rope2":
                ropes[0] += 1
                v.scalar_tensor_tensor(k.R2, ps, j["bias"], j["tab"], ALU.add, ALU.mult).then_inc(s("turned"), 1)
                v.wait_ge(s("turned"), b * self.n_rope + ropes[0])
                for d, r in j["dst"]:
                    last = v.tensor_tensor(d, k.R1[r, :], k.R2[r, :], ALU.add)
                last.then_inc(s("v_free"), 1)

        def maxima(h, u):
            sb[0] += 1
            v.wait_ge(s("score"), b * H * self.units + sb[0])
            bk = BANK_S + (sb[0] - 1) % 2
            ts = slice(0, QT) if self.units == 1 else slice(u, u + 1)
            w = self.nk if self.units == 1 or not self.causal else 128 * (u + 1)
            for n, (k0, k1) in enumerate(self.segs):
                k1 = w if k1 is None else k1
                src = P[:, bk, 0:w * (ts.stop - ts.start)].rearrange("p (t k) -> p t k", k=w)[:, :, k0:k1]
                col = k.M8[:, ts, h, 8] if self.narrow else k.M64[:, ts, h, self.aug - len(self.segs) + n]
                last = v.tensor_reduce(col, src, AX.X, ALU.max, negate=True)
                if self.clip:
                    cl[0] += 1
                    last.then_inc(s("raw_max"), 1)
                    v.wait_ge(s("raw_max"), b * H + cl[0])
                    lim = k.clip_at
                    last = v.tensor_scalar(col, col, lim, -lim, ALU.min, ALU.max)
            last.then_inc(s("max_done"), 1)

        def place_max(g):
            full()
            if self.narrow:
                v.tensor_tensor(k.QA[:, g, :], k.QA[:, g, :], P[:, BANK_V, :], ALU.add).then_inc(s("v_free"), 1)
            else:
                v.tensor_copy(k.QA[64:64 + self.aug, g, :], P[0:self.aug, BANK_V, :]).then_inc(s("v_free"), 1)

        def clip_scores(h):
            n = b * H + h
            kp = self.kp
            v.wait_ge(s("score_t"), n + 1)
            lim = k.clip_at
            v.tensor_scalar(k.C1[0:kp, :], P[0:kp, BANK_ST + h % 2, :], lim, -lim, ALU.min, ALU.max).then_inc(s("raw_clip"), 1)
            v.wait_ge(s("raw_clip"), n + 1)
            v.wait_ge(s("exp_done"), n + 1)
            v.tensor_tensor(k.C2[0:kp, h % 2, :], k.C1[0:kp, :], P[0:kp, BANK_PV + 1, :], ALU.add).then_inc(s("clipped"), 1)

        def divide(h):
            dh, vc = self.dh, self.vc
            for u in range(self.pv_units):
                n = (b * H + h) * self.pv_units + u
                v.wait_ge(s("value"), n + 1)
                nt = QT // self.pv_units
                bk = BANK_PV + (h * self.pv_units + u) % self.pv_ring
                ps = P[:, bk, 0:nt * vc].rearrange("p (t c) -> p t c", c=vc)
                o = k.O[:, u * nt:(u + 1) * nt, dh * h:dh * (h + 1)]
                v.wait_ge(s("norm_done"), n + self.pv_ring)
                if len(self.segs) == 1:
                    r = k.rc[:, 0:nt]
                    v.reciprocal(r, ps[:, :, dh]).then_inc(s("recip"), 1)
                    v.wait_ge(s("recip"), n + 1)
                    v.tensor_tensor(o, ps[:, :, 0:dh], r.unsqueeze(2).to_broadcast([128, nt, dh]), ALU.mult).then_inc(s("norm_done"), 1)
                else:
                    r0, r1 = k.rc[:, 0:nt], k.rc[:, nt:2 * nt]
                    v.reciprocal(r0, ps[:, :, dh])
                    v.reciprocal(r1, ps[:, :, vc - 1]).then_inc(s("recip"), 1)
                    v.wait_ge(s("recip"), 2 * n + 1)
                    t2 = k.seg2[:, 0:nt, :]
                    v.tensor_tensor(o, ps[:, :, 0:dh], r0.unsqueeze(2).to_broadcast([128, nt, dh]), ALU.mult)
                    v.tensor_tensor(t2, ps[:, :, dh + 1:vc - 1], r1.unsqueeze(2).to_broadcast([128, nt, dh]), ALU.mult).then_inc(s("recip"), 1)
                    v.wait_ge(s("recip"), 2 * n + 2)
                    v.tensor_tensor(o, o, t2, ALU.add).then_inc(s("norm_done"), 1)

        for i in range(H + self.lag + 1):
            if i < H:
                for u in range(self.units):
                    maxima(i, u)
            if self.clip and 0 <= i - self.lag < H:
                clip_scores(i - self.lag)
            if i and i % self.gs == 0 and i // self.gs <= self.groups:
                place_max(i // self.gs - 1)
            if i - self.lag - 1 >= 0:
                divide(i - self.lag - 1)
        for c in range(self.nf):
            if self.ot_ch[c] == "V":
                full()
                v.tensor_copy(k.OT[:, c, :], P[:, BANK_V, :]).then_inc(s("v_free"), 1)
        full()
        y = P[:, BANK_V, :].rearrange("p (t d) -> p t d", d=D)
        v.tensor_tensor(self.dst[:, bass.ds(b * QT, QT), :], self.src[:, bass.ds(b * QT, QT), :], y, ALU.add).then_inc(s("v_free"), 1)
        assert cnt[0] == self.n_v

    def act(self, a, s, b):
        k, H = self.k, self.H
        P = k.P
        cnt = [0]

        def full():
            cnt[0] += 1
            a.wait_ge(s("a_full"), b * self.n_a + cnt[0])

        for j in self.jobs:
            if j["ch"] != "A":
                continue
            full()
            ps = P[0:j["m"], BANK_A, 0:j["n"]]
            if j["kind"] == "cols":
                a.activation(j["dst"], ps, ACT.Identity, bias=j["bias"]).then_inc(s("a_free"), 1)
            elif j["kind"] == "scaled":
                a.activation(j["dst"], ps, ACT.Identity, scale=j["bias"]).then_inc(s("a_free"), 1)
            elif j["kind"] == "pair":
                a.activation(j["dst"][0], P[0:64, BANK_A, 0:j["n"]], ACT.Copy)
                a.activation(j["dst"][1], P[64:128, BANK_A, 0:j["n"]], ACT.Copy).then_inc(s("a_free"), 1)
            else:
                a.activation(j["dst"], ps.rearrange("p (h d) -> p h d", d=self.dh), ACT.Copy).then_inc(s("a_free"), 1)
        tb = 0
        for h in range(H):
            for t in range(self.kt):
                tb += 1
                w = self.width(t)
                a.wait_ge(s("clipped" if self.clip else "score_t"), b * H * self.kt + tb + (1 if self.clip else 0))
                if t == 0 and h >= 2:
                    a.wait_ge(s("value"), (b * H + h - 1) * self.pv_units)
                elif t == 0:
                    a.wait_ge(s("value_all"), b + 1)
                src = k.C2[0:self.kp, h % 2, :] if self.clip else P[0:self.kp, BANK_ST + (tb - 1) % 2, 0:w]
                a.activation(k.PT[0:self.kp, h % 2, t, N - w:N], src, ACT.Exp, scale=self.scale).then_inc(s("exp_done"), 1)
        for c in range(self.nf):
            if self.ot_ch[c] == "A":
                full()
                a.activation(k.OT[:, c, :], P[:, BANK_A, :], ACT.Copy).then_inc(s("a_free"), 1)
        if self.lora:
            full()
            a.activation(k.TL[0:RANK, 3, :], P[0:RANK, BANK_A, :], ACT.Identity, scale=self.lora[2]).then_inc(s("a_free"), 1)
        assert cnt[0] == self.n_a

    def pool(self, g, s, b):
        for n, (dst, src) in enumerate(self.static):
            g.tensor_copy(dst, src(b)).then_inc(s("static"), 1)
        g.wait_ge(s("norm_done"), (b + 1) * self.H * self.pv_units + self.pv_ring)
        g.sem_inc(s("value_all"), 1)

    def run(self, i, prefetch=None, once=None, kaug=None):
        k, nc = self.k, self.k.nc
        w, w_ready = weights(k, i)
        with phase(k) as (block, s):
            @block.sync
            def _(sp):
                if prefetch is not None:
                    load_weights(k, prefetch)
                if kaug is not None:
                    sp.dma_start(k.KA[64:64 + self.aug, 0:self.H, 0:self.nk], kaug).then_inc(s("kaug"), 16)

            @block.gpsimd
            def _(g):
                w_ready(g)
                g.memset(k.M8[:] if self.narrow else k.M64[:], 0.0 if self.narrow else 1.0).then_inc(s("consts"), 1)
                if len(self.segs) == 1:
                    g.memset(k.VA[:, :, :, self.dh:self.dh + 1], 1.0).then_inc(s("consts"), 1)
                else:
                    for n in range(2):
                        g.tensor_copy(k.VA[0:self.nk, 0, :, (self.dh + 1) * (n + 1) - 1],
                                      w["seg"][:, n:n + 1].to_broadcast([self.nk, self.H])).then_inc(s("consts"), 1)
                g.sem_inc(s("value_all"), 1)
                with g.Fori(0, B) as b:
                    self.pool(g, s, b)

            @block.vector
            def _(v):
                w_ready(v)
                self.dve_start(v, s)
                if once:
                    once(v, s)
                v.wait_ge(s("consts"), 1 + len(self.segs))
                with v.Fori(0, B) as b:
                    self.dve(v, s, b)

            @block.scalar
            def _(a):
                w_ready(a)
                self.act_start(a, s)
                if once:
                    a.wait_ge(s("once"), 1)
                with a.Fori(0, B) as b:
                    self.act(a, s, b)

            @block.tensor
            def _(pe):
                w_ready(pe)
                pe.wait_ge(s("consts"), 1 + len(self.segs))
                if kaug is not None:
                    pe.wait_ge(s("kaug"), 16)
                with pe.Fori(0, B) as b:
                    self.pe(pe, s, b)


def batch_cols(t, b, n=N):
    return t[:, bass.ds(b * n, n)]


def narrow_jobs(k, w, kv, nk, vcols, rope=False):
    jobs = []
    ch = 0
    for name, dst, x, n in (("q", k.QA, "x", N), ("k", k.KA, kv, nk)):
        for g in range(NH // GROUP):
            cols = slice(128 * g, 128 * (g + 1))
            m = 128
            o = dst[:, g, 0:n]
            xin = (lambda b: k.XB[:]) if x == "x" and kv == "x" else ((lambda b: batch_cols(k.XT, b)) if x == "x" else (lambda b: k.CB[:, :]))
            bias = w["b" + name][:, g:g + 1]
            mk = lambda wt, xin=xin, cols=cols: (lambda b: [(w[wt][:, cols], xin(b))])
            if rope:
                jobs.append(dict(ch="V", kind="rope1", m=m, n=n, mms=mk("w" + name), bias=bias, tab=w["cos"]))
                jobs.append(dict(ch="V", kind="rope2", m=m, n=n, mms=mk("w" + name + "t"), bias=0.0, tab=w["sin"],
                                 dst=[(o, slice(0, 128))]))
            else:
                jobs.append(dict(ch="VA"[ch % 2], kind="cols", m=m, n=n, mms=mk("w" + name), bias=bias, dst=o))
                ch += 1
    kp = min(nk, 128)
    for t in range(-(-nk // 128)):
        x = k.XB if kv == "x" else k.CB
        def mms(b, t=t, x=x):
            r = [(x[:, kp * t:kp * (t + 1)], w["wv"])]
            if "bv" in w:
                r.append((k.ones[0:1, 0:kp], w["bv"]))
            return r
        jobs.append(dict(ch="VA"[t % 2], kind="rows", m=kp, n=vcols, mms=mms, dst=k.VA[0:kp, t, 0:vcols // 8, 0:8]))
    return jobs


@contextmanager
def attention_buffers(k, narrow, nk, heads, vheads, vc, clip=False, rope=False, lora=False):
    kt = -(-nk // 128)
    with ExitStack() as st:
        def sb(name, shape, dt=F32):
            k.serial += 1
            return st.enter_context(k.nc.sbuf_tensor(f"{name}_{k.serial}", shape, dt))
        g = heads // GROUP if narrow else heads
        k.QA = sb("QA", [128, g, N])
        k.KA = sb("KA", [128, g, nk])
        k.VA = sb("VA", [128, kt, vheads, vc])
        k.PT = sb("PT", [128, 2, kt, N])
        nf = heads * (8 if narrow else 64) // 128
        k.O = sb("O", [128, QT, nf * 128])
        k.OT = k.PT[:].rearrange("p a t n -> p (a t) n") if nf == 2 * kt else sb("OT", [128, nf, N])
        if narrow:
            k.M8 = sb("M8", [128, QT, NH, 32])
        else:
            k.M64 = sb("M64", [128, QT, heads, 2])
        k.rc = sb("rc", [128, 2 * QT])
        if clip:
            k.C1, k.C2 = sb("C1", [128, N]), sb("C2", [128, 2, N])
        if rope:
            k.R1, k.R2 = k.PT[:, 0, 0, :], k.PT[:, 0, 1, :]
        if lora:
            k.TL, k.seg2, k.al = sb("TL", [RANK, 4, N]), sb("seg2", [128, QT, 64]), sb("al", [RANK, 4])
        yield sb


def self_static(k):
    return [(k.XB[:], lambda b: batch_cols(k.XT, b))]


def ctx_static(k):
    return [(k.CB[:, :], lambda b: k.CT[:, 0, bass.ds(b * CTX, CTX)])]


def l0_xattn(k, i):
    w, _ = weights(k, i)
    with attention_buffers(k, True, CTX, NH, NH, 9):
        Attention(k, NH, 8, CTX, 8 ** -0.5, jobs=narrow_jobs(k, w, "c", CTX, 128), bo=w["bo"], wo=w["wo"],
                  src=k.X, dst=k.X, static=ctx_static(k)).run(i, prefetch=i + 1)


def l1_xattn(k, i):
    w, _ = weights(k, i)
    k.clip_at = 10000.0 * math.sqrt(8.0)
    with attention_buffers(k, True, CTX, NH, NH, 9, clip=True):
        Attention(k, NH, 8, CTX, 8 ** -0.5, clip=w["pick"], jobs=narrow_jobs(k, w, "c", CTX, 128), bo=w["bo"], wo=w["wo"],
                  src=k.X, dst=k.X, static=ctx_static(k)).run(i, prefetch=i + 1)


def ffn_attention(k, i, causal, rope, vrep):
    w, _ = weights(k, i)
    vh = NH // vrep
    with attention_buffers(k, True, N, NH, vh, 9, rope=rope):
        Attention(k, NH, 8, N, 8 ** -0.5, causal=causal, vrep=vrep, jobs=narrow_jobs(k, w, "x", N, vh * 8, rope=rope),
                  wo=w["wo"], src=k.X, dst=k.Hs, static=self_static(k)).run(i, prefetch=i + 1)


def l2_attn(k, i):
    w, _ = weights(k, i)
    jobs = []
    with attention_buffers(k, False, N, NH, NH, 65, rope=True):
        for name, dst in (("q", k.QA), ("k", k.KA)):
            for g in range(8):
                cols = slice(128 * g, 128 * (g + 1))
                mk = lambda wt, cols=cols: (lambda b: [(w[wt][:, cols], k.XB[:])])
                jobs.append(dict(ch="V", kind="rope1", m=128, n=N, mms=mk("w" + name), bias=w["b" + name][:, g:g + 1], tab=w["cos"]))
                jobs.append(dict(ch="V", kind="rope2", m=128, n=N, mms=mk("w" + name + "t"), bias=w["b" + name + "t"][:, g:g + 1],
                                 tab=w["sin"], dst=[(dst[0:64, 2 * g, :], slice(0, 64)), (dst[0:64, 2 * g + 1, :], slice(64, 128))]))
        for t in range(QT):
            for u in range(2):
                jobs.append(dict(ch="A", kind="rows", m=128, n=512, dst=k.VA[:, t, 8 * u:8 * u + 8, 0:64],
                                 mms=lambda b, t=t, u=u: [(k.XB[:, 128 * t:128 * (t + 1)], w["wv"][:, 512 * u:512 * (u + 1)]),
                                                          (k.ones[0:1, 0:128], w["bv"][:, 512 * u:512 * (u + 1)])]))
        once = lambda v, s: (v.memset(k.QA[64:66, :, :], 1.0).then_inc(s("once"), 1), v.wait_ge(s("once"), 1))
        Attention(k, NH, 64, N, 192 ** -0.5, causal=True, aug=2, jobs=jobs, bo=w["bo"], wo=w["wo"], src=k.X, dst=k.X,
                  static=self_static(k)).run(i, prefetch=i + 1, once=once, kaug=k.kaug[0])


def l2_xattn(k, i):
    w, _ = weights(k, i)
    jobs = []
    with attention_buffers(k, False, CTX, 8, 8, 65):
        for name, dst, n in (("wq", k.QA, N), ("wk", k.KA, CTX)):
            for g in range(4):
                jobs.append(dict(ch="VA"[g % 2], kind="pair", m=128, n=n, dst=[dst[0:64, 2 * g, 0:n], dst[0:64, 2 * g + 1, 0:n]],
                                 mms=lambda b, g=g, name=name: [(w[name][:, 128 * g:128 * (g + 1)],
                                                                 batch_cols(k.XT, b) if name == "wq" else k.CB[:, :])]))
        jobs.append(dict(ch="A", kind="rows", m=CTX, n=512, dst=k.VA[0:CTX, 0, :, 0:64], mms=lambda b: [(k.CB[:, :], w["wv"])]))
        Attention(k, 8, 64, CTX, 64 ** -0.5, jobs=jobs, bo=w["bo"], wo=w["wo"], src=k.X, dst=k.X,
                  static=ctx_static(k)).run(i, prefetch=i + 1, kaug=k.kaug[1])


def l3_xattn(k, i):
    w, _ = weights(k, i)
    with attention_buffers(k, False, CTX, NH, NH, 130, lora=True):
        lo = lambda n: k.TL[0:RANK, n, :]
        x = lambda b: batch_cols(k.XT, b)
        jobs = [dict(ch="V", kind="scaled", m=RANK, n=N, dst=lo(0), bias=k.al[:, 0:1], mms=lambda b: [(w["qd"], x(b))]),
                dict(ch="V", kind="scaled", m=RANK, n=CTX, dst=lo(1)[:, 0:CTX], bias=k.al[:, 1:2], mms=lambda b: [(w["kd"], k.CB[:, :])]),
                dict(ch="V", kind="scaled", m=RANK, n=CTX, dst=lo(2)[:, 0:CTX], bias=k.al[:, 2:3], mms=lambda b: [(w["vd"], k.CB[:, :])])]
        first = True
        for g in range(8):
            c = slice(128 * g, 128 * (g + 1))
            jobs.append(dict(ch="VA"[g % 2], kind="pair", m=128, n=N, dst=[k.QA[0:64, 2 * g, :], k.QA[0:64, 2 * g + 1, :]], after=first,
                             mms=lambda b, c=c: [(w["wq"][:, c], x(b)), (w["qu"][:, c], lo(0))]))
            first = False
            jobs.append(dict(ch="AV"[g % 2], kind="pair", m=128, n=CTX, dst=[k.KA[0:64, 2 * g, :], k.KA[0:64, 2 * g + 1, :]],
                             mms=lambda b, c=c: [(w["wk"][:, c], k.CB[:, :]), (w["ku"][:, c], lo(1)[:, 0:CTX]), (w["wki"][:, c], k.CI[:, :])]))
        for u in range(2):
            c = slice(512 * u, 512 * (u + 1))
            jobs.append(dict(ch="VA"[u], kind="rows", m=CTX, n=512, dst=k.VA[0:CTX, 0, 8 * u:8 * u + 8, 0:64],
                             mms=lambda b, c=c: [(k.CB[:, :], w["wv"][:, c]), (lo(2)[:, 0:CTX], w["vu"][:, c])]))
            jobs.append(dict(ch="AV"[u], kind="rows", m=CTX, n=512, dst=k.VA[0:CTX, 0, 8 * u:8 * u + 8, 65:129],
                             mms=lambda b, c=c: [(k.CI[:, :], w["wvi"][:, c])]))
        def once(v, s):
            v.tensor_scalar(k.al[:], w["alpha"], 1.0 / RANK, None, ALU.mult).then_inc(s("once"), 1)
            v.wait_ge(s("once"), 1)
        Attention(k, NH, 64, CTX, 64 ** -0.5, aug=2, segs=((0, CTX - IPA), (CTX - IPA, CTX)), jobs=jobs, bo=w["bo"], wo=w["wo"],
                  src=k.X, dst=k.X, lora=(w["od"], w["ou"], k.al[:, 3:4]),
                  static=[(k.CB[:, :], lambda b: k.CT[:, 1, bass.ds(b * CTX, CTX)]), (k.CI[:, :], lambda b: k.CT[:, 2, bass.ds(b * CTX, CTX)])]
                  ).run(i, prefetch=i + 1, once=once, kaug=k.kaug[2])


def l0_attn(k, i):
    nc, P = k.nc, k.P
    w, w_ready = weights(k, i)
    with ExitStack() as st, phase(k) as (block, s):
        sb = lambda n, sh: st.enter_context(nc.sbuf_tensor(n, sh, F32))
        S = [sb(f"l0_{n}", [128, TOK]) for n in "qkv"]
        VT, G, M = sb("l0_vt", [128, TILES, 128]), sb("l0_g", [128, B, 128]), sb("l0_m", [128, B, 128])
        stats, mv, col = sb("l0_st", [128, 3, 4, 6]), sb("l0_mv", [128, 3, 2]), sb("l0_col", [128, 3, 6])
        bank0 = (0, 4, 0)

        @block.sync
        def _(sp):
            load_weights(k, i + 1)

        @block.tensor
        def _(pe):
            w_ready(pe)
            for j, n in enumerate(("wq", "wk", "wv")):
                if j == 2:
                    pe.wait_ge(s("sig"), 4)
                for c in range(4):
                    pe.matmul(P[:, bank0[j] + c, :], w[n], k.XT[:, N * c:N * (c + 1)], start=True, stop=True).then_inc(s("proj"), 1)
            pe.wait_ge(s("sig"), 12)
            for b in range(B):
                for t in range(QT):
                    last = pe.transpose(P[:, 4 + b, 128 * t:128 * (t + 1)], S[2][:, N * b + 128 * t:N * b + 128 * (t + 1)], k.ident[:])
                last.then_inc(s("vt"), 1)
            for b in range(B):
                pe.wait_ge(s("vt_copied"), b + 1)
                for t in range(QT):
                    last = pe.matmul(P[:, 0, 128 * b:128 * (b + 1)], VT[:, QT * b + t, :], VT[:, QT * b + t, :], start=t == 0, stop=t == QT - 1)
            last.then_inc(s("gram"), 1)
            pe.wait_ge(s("gram_masked"), 1)
            for b in range(B):
                last = pe.matmul(P[:, 1, 128 * b:128 * (b + 1)], G[:, b, :], w["wp"], start=True, stop=True)
            last.then_inc(s("m"), 1)
            pe.wait_ge(s("m_copied"), 1)
            pe.wait_ge(s("qk"), 4)
            for b in range(B):
                for t in range(QT):
                    o = P[:, 4 + b, 128 * t:128 * (t + 1)]
                    pe.matmul(o, S[0][:, N * b + 128 * t:N * b + 128 * (t + 1)], M[:, b, :], start=True, stop=False)
                    last = pe.matmul(o, k.ones[0:1, 0:128], w["bp"], start=False, stop=True)
                last.then_inc(s("y"), 1)

        @block.vector
        def _(v):
            w_ready(v)
            for j in range(3):
                for c in range(4):
                    v.wait_ge(s("proj"), 4 * j + c + 1)
                    v.bn_stats(stats[:, j, c, :], P[:, bank0[j] + c, :]).then_inc(s("stats"), 1)
                v.wait_ge(s("stats"), 4 * j + 4)
                v.bn_aggr(mv[:, j, :], stats[:, j, :, :].rearrange("p c s -> p (c s)")).then_inc(s("small"), 1)
                v.wait_ge(s("small"), 5 * j + 1)
                v.tensor_scalar(col[:, j, 0:1], mv[:, j, 1:2], 1e-5, None, ALU.add).then_inc(s("small"), 1)
                v.wait_ge(s("small"), 5 * j + 2)
                v.reciprocal(col[:, j, 1:2], col[:, j, 0:1]).then_inc(s("inv"), 1)
                v.wait_ge(s("root"), j + 1)
                v.tensor_scalar(col[:, j, 3:4], col[:, j, 2:3], w["gam"][:, j:j + 1], 4.0, ALU.mult, ALU.mult).then_inc(s("small"), 1)
                v.wait_ge(s("small"), 5 * j + 3)
                v.tensor_scalar(col[:, j, 4:5], mv[:, j, 0:1], col[:, j, 3:4], -1.0, ALU.mult, ALU.mult).then_inc(s("small"), 1)
                v.wait_ge(s("small"), 5 * j + 4)
                v.scalar_tensor_tensor(col[:, j, 5:6], w["bet"][:, j:j + 1], 4.0, col[:, j, 4:5], ALU.mult, ALU.add).then_inc(s("small"), 1)
                v.wait_ge(s("small"), 5 * j + 5)
                v.tensor_scalar(col[:, j, 5:6], col[:, j, 5:6], -4.0, None, ALU.add).then_inc(s("affine"), 1)
            for c in range(4):
                v.wait_ge(s("sig"), 8)
                cs = slice(N * c, N * (c + 1))
                v.scalar_tensor_tensor(S[0][:, cs], S[0][:, cs], 8 ** -0.5, S[1][:, cs], ALU.mult, ALU.mult).then_inc(s("qk"), 1)
            for b in range(B):
                v.wait_ge(s("vt"), b + 1)
                v.tensor_copy(VT[:, QT * b:QT * (b + 1), :].rearrange("p t d -> p (t d)"), P[:, 4 + b, :]).then_inc(s("vt_copied"), 1)
            v.wait_ge(s("gram"), 1)
            v.tensor_tensor(G[:], P[:, 0, :].rearrange("p (b d) -> p b d", b=B), w["blocks"].unsqueeze(1).to_broadcast([128, B, 128]),
                            ALU.mult).then_inc(s("gram_masked"), 1)
            v.wait_ge(s("m"), 1)
            v.tensor_copy(M[:].rearrange("p b d -> p (b d)"), P[:, 1, :]).then_inc(s("m_copied"), 1)
            for b in range(B):
                v.wait_ge(s("y"), b + 1)
                x = k.X[:, QT * b:QT * (b + 1), :].rearrange("p t d -> p (t d)")
                v.tensor_tensor(x, x, P[:, 4 + b, :], ALU.add)

        @block.scalar
        def _(a):
            for j in range(3):
                a.wait_ge(s("inv"), j + 1)
                a.activation(col[:, j, 2:3], col[:, j, 1:2], ACT.Sqrt).then_inc(s("root"), 1)
                a.wait_ge(s("affine"), j + 1)
                for c in range(4):
                    a.activation(S[j][:, N * c:N * (c + 1)], P[:, bank0[j] + c, :], ACT.Sigmoid, scale=col[:, j, 3:4],
                                 bias=col[:, j, 5:6]).then_inc(s("sig"), 1)


def l0_ffn_attention(k, i):
    nc, P = k.nc, k.P
    w, w_ready = weights(k, i)
    pairs = [(q, t) for q in range(B) for t in range(q + 1)]
    first = [q * (q + 1) // 2 for q in range(B + 1)]
    with ExitStack() as st, phase(k) as (block, s):
        sb = lambda n, sh: st.enter_context(nc.sbuf_tensor(n, sh, F32))
        QKV = sb("f_qkv", [128, 2, B, 384])
        PR, SC, RD = sb("f_pr", [128, len(pairs), 128]), sb("f_sc", [128, len(pairs), NH]), sb("f_rd", [128, B, NH])
        MX, O, OT = sb("f_mx", [128, B, NH]), sb("f_o", [128, 2, B, 128]), sb("f_ot", [128, 2, N])

        @block.sync
        def _(sp):
            load_weights(k, i + 1)

        @block.tensor
        def _(pe):
            w_ready(pe)

            def qkv(r):
                if r >= 1:
                    pe.wait_ge(s("qkv_copied"), 4 * r)
                for q in range(B):
                    t = QT * q + r
                    pe.matmul(P[:, q, 0:384], k.XT[:, 128 * t:128 * (t + 1)], w["wqkv"], start=True, stop=True).then_inc(s("qkv"), 1)

            qkv(0)
            for r in range(QT):
                if r + 1 < QT:
                    qkv(r + 1)
                pe.wait_ge(s("o"), r + 1)
                for q in range(B):
                    last = pe.transpose(P[:, 4, 128 * q:128 * (q + 1)], O[:, r % 2, q, :], k.ident[:])
                last.then_inc(s("ot"), 1)
                pe.wait_ge(s("ot_copied"), r + 1)
                if r >= 1:
                    pe.wait_ge(s("added"), r)
                for q in range(B):
                    last = pe.matmul(P[:, 5, 128 * q:128 * (q + 1)], OT[:, r % 2, 128 * q:128 * (q + 1)], w["wo"], start=True, stop=True)
                last.then_inc(s("y"), 1)

        @block.scalar
        def _(a):
            def copies(r):
                if r >= 2:
                    a.wait_ge(s("o"), r - 1)
                for q in range(B):
                    a.wait_ge(s("qkv"), 4 * r + q + 1)
                    a.activation(QKV[:, r % 2, q, :], P[:, q, 0:384], ACT.Copy).then_inc(s("qkv_copied"), 1)

            copies(0)
            for r in range(QT):
                if r + 1 < QT:
                    copies(r + 1)
                a.wait_ge(s("shifted"), r + 1)
                a.activation(SC[:], SC[:], ACT.Exp, scale=8 ** -0.5).then_inc(s("exp"), 1)
                a.wait_ge(s("ot"), r + 1)
                a.activation(OT[:, r % 2, :], P[:, 4, :], ACT.Copy).then_inc(s("ot_copied"), 1)

        @block.vector
        def _(v):
            n = [0]

            def step(ins):
                n[0] += 1
                ins.then_inc(s("step"), 1)
                v.wait_ge(s("step"), n[0])

            for r in range(QT):
                v.wait_ge(s("qkv_copied"), 4 * r + 4)
                for q in range(B):
                    m = q + 1
                    last = v.tensor_tensor(PR[:, first[q]:first[q + 1], :],
                                           QKV[:, r % 2, q:q + 1, 0:128].to_broadcast([128, m, 128]),
                                           QKV[:, r % 2, 0:m, 128:256], ALU.mult)
                step(last)
                step(v.tensor_reduce(SC[:], PR[:].rearrange("p n (h d) -> p n h d", d=8), AX.X, ALU.add))
                for q in range(B):
                    last = v.tensor_reduce(MX[:, q, :], SC[:, first[q]:first[q + 1], :].rearrange("p t h -> p h t"), AX.X, ALU.max)
                step(last)
                for q in range(B):
                    m = q + 1
                    sc = SC[:, first[q]:first[q + 1], :]
                    last = v.tensor_tensor(sc, sc, MX[:, q:q + 1, :].to_broadcast([128, m, NH]), ALU.subtract)
                last.then_inc(s("shifted"), 1)
                v.wait_ge(s("exp"), r + 1)
                for q in range(B):
                    last = v.tensor_reduce(RD[:, q, :], SC[:, first[q]:first[q + 1], :].rearrange("p t h -> p h t"), AX.X, ALU.add)
                step(last)
                v.reciprocal(RD[:], RD[:])
                for q in range(B):
                    m = q + 1
                    o = PR[:, first[q]:first[q + 1], :].rearrange("p t (h d) -> p t h d", d=8)
                    last = v.tensor_tensor(o, SC[:, first[q]:first[q + 1], :].unsqueeze(3).to_broadcast([128, m, NH, 8]),
                                           QKV[:, r % 2, 0:m, 256:384].rearrange("p t (h d) -> p t h d", d=8), ALU.mult)
                step(last)
                if r >= 2:
                    v.wait_ge(s("ot"), r - 1)
                for q in range(B):
                    last = v.tensor_reduce(O[:, r % 2, q, :], PR[:, first[q]:first[q + 1], :].rearrange("p t x -> p x t"), AX.X, ALU.add)
                step(last)
                o = O[:, r % 2, :, :].rearrange("p q (h d) -> p (q h) d", d=8)
                v.tensor_tensor(o, o, RD[:].rearrange("p q h -> p (q h)").unsqueeze(2).to_broadcast([128, B * NH, 8]), ALU.mult).then_inc(s("o"), 1)
                v.wait_ge(s("y"), r + 1)
                tiles = lambda t: t[:, r::QT, :]
                v.tensor_tensor(tiles(k.Hs), tiles(k.X), P[:, 5, :].rearrange("p (q d) -> p q d", d=128), ALU.add).then_inc(s("added"), 1)


def l1_attn(k, i):
    nc, P = k.nc, k.P
    w, w_ready = weights(k, i)
    NS = 16
    with ExitStack() as st, phase(k) as (block, s):
        sb = lambda n, sh: st.enter_context(nc.sbuf_tensor(n, sh, F32))
        XC, C1, C2, XS = sb("m_xc", [128, N + 2]), sb("m_c1", [128, N]), sb("m_c2", [128, N]), sb("m_xs", [128, N])
        AB, RE, DT, DTX, Z = (sb(f"m_{n}", [128, N]) for n in ("ab", "re", "dt", "dtx", "z"))
        DA, BX, H, HC = (sb(f"m_{n}", [128, 2, N]) for n in ("da", "bxx", "h", "hc"))
        YZ = sb("m_yz", [128, N])
        PB, PC, PY, PM = 0, 2, 4, 5

        @block.sync
        def _(sp):
            load_weights(k, i + 1)

        @block.gpsimd
        def _(g):
            g.memset(XC[:], 0.0).then_inc(s("edges"), 1)

        @block.tensor
        def _(pe):
            w_ready(pe)
            with pe.Fori(0, B) as b:
                x = k.XT[:, bass.ds(b * N, N)]
                pe.wait_ge(s("m_free"), 3 * b + 1)
                pe.matmul(P[:, PM, :], w["win"], x, start=True, stop=True).then_inc(s("m_full"), 1)
                pe.wait_ge(s("z_free"), b + 1)
                pe.matmul(P[:, PM + 1, :], w["wg"], x, start=True, stop=True).then_inc(s("z_full"), 1)
                pe.wait_ge(s("xs"), b + 1)
                pe.wait_ge(s("m_free"), 3 * b + 2)
                pe.matmul(P[:, PM, :], w["wdt"], XS[:], start=True, stop=True).then_inc(s("m_full"), 1)

                def bc(n):
                    pe.wait_ge(s("bx"), NS * b + n + 1)
                    pe.matmul(P[:, PB + n % 2, :], w["wb"][:, n:n + 1].to_broadcast([128, 128]), XS[:], start=True, stop=True).then_inc(s("b_full"), 1)
                    pe.wait_ge(s("hc"), NS * b + n + 1)
                    pe.matmul(P[:, PC + n % 2, :], w["wc"][:, n:n + 1].to_broadcast([128, 128]), XS[:], start=True, stop=True).then_inc(s("c_full"), 1)

                for n in range(NS + 2):
                    if n < NS:
                        bc(n)
                    if n >= 2:
                        m = n - 2
                        pe.wait_ge(s("hc"), NS * b + m + 3)
                        pe.matmul(P[:, PY, :], k.ident[:], HC[:, m % 2, :], start=m == 0, stop=m == NS - 1).then_inc(s("summed"), 1)
                pe.wait_ge(s("yz"), b + 1)
                pe.wait_ge(s("m_free"), 3 * b + 3)
                for t in range(QT):
                    o = P[:, PM, 128 * t:128 * (t + 1)]
                    pe.matmul(o, YZ[:, 128 * t:128 * (t + 1)], w["wout"], start=True, stop=False)
                    last = pe.matmul(o, k.ones[0:1, 0:128], w["bout"], start=False, stop=True)
                last.then_inc(s("m_full"), 1)

        @block.scalar
        def _(a):
            w_ready(a)
            a.sem_inc(s("z_free"), 1)
            with a.Fori(0, B) as b:
                a.wait_ge(s("conv"), b + 1)
                a.activation(XS[:], C1[:], ACT.Silu, bias=w["convb"]).then_inc(s("xs"), 1)
                a.wait_ge(s("z_full"), b + 1)
                a.activation(Z[:], P[:, PM + 1, :], ACT.Silu, bias=w["bg"]).then_inc(s("z_free"), 1)
                a.wait_ge(s("m_full"), 3 * b + 2)
                a.activation(AB[:], P[:, PM, :], ACT.Abs, bias=w["bdt"]).then_inc(s("abs"), 1)
                a.wait_ge(s("abs"), b + 1)
                a.activation(AB[:], AB[:], ACT.Exp, scale=-1.0).then_inc(s("ab"), 1)
                a.wait_ge(s("ab"), 2 * b + 1)
                a.activation(AB[:], AB[:], ACT.Ln, bias=1.0).then_inc(s("ab"), 1)
                a.wait_ge(s("dt"), b + 1)
                for n in range(NS):
                    a.wait_ge(s("scan"), NS * b + n + 1)
                    a.activation(DA[:, n % 2, :], DT[:], ACT.Exp, scale=w["a"][:, n:n + 1]).then_inc(s("da"), 1)

        @block.vector
        def _(v):
            w_ready(v)
            v.sem_inc(s("m_free"), 1)
            v.sem_inc(s("bx"), 2)
            v.sem_inc(s("hc"), 2)
            v.sem_inc(s("scan"), 2)
            v.sem_inc(s("summed"), 2)
            v.wait_ge(s("edges"), 1)
            with v.Fori(0, B) as b:
                v.wait_ge(s("m_full"), 3 * b + 1)
                v.tensor_scalar(XC[:, 1:N + 1], P[:, PM, :], w["bin"], None, ALU.add).then_inc(s("m_free"), 1)
                v.wait_ge(s("m_free"), 3 * b + 2)
                cw = w["convw"]
                v.tensor_scalar(C1[:], XC[:, 0:N], cw[:, 0:1], None, ALU.mult).then_inc(s("own"), 1)
                v.wait_ge(s("own"), 3 * b + 1)
                v.scalar_tensor_tensor(C2[:], XC[:, 1:N + 1], cw[:, 1:2], C1[:], ALU.mult, ALU.add).then_inc(s("own"), 1)
                v.wait_ge(s("own"), 3 * b + 2)
                v.scalar_tensor_tensor(C1[:], XC[:, 2:N + 2], cw[:, 2:3], C2[:], ALU.mult, ALU.add).then_inc(s("conv"), 1)
                v.wait_ge(s("m_full"), 3 * b + 2)
                v.wait_ge(s("abs"), b + 1)
                v.tensor_scalar(RE[:], P[:, PM, :], w["bdt"], 0.0, ALU.add, ALU.max).then_inc(s("m_free"), 1)
                v.wait_ge(s("m_free"), 3 * b + 3)
                v.wait_ge(s("ab"), 2 * b + 2)
                v.tensor_tensor(DT[:], RE[:], AB[:], ALU.add).then_inc(s("dt"), 1)
                v.wait_ge(s("dt"), b + 1)
                v.tensor_tensor(DTX[:], DT[:], XS[:], ALU.mult).then_inc(s("own"), 1)
                v.wait_ge(s("own"), 3 * b + 3)

                def inp(n):
                    v.wait_ge(s("b_full"), NS * b + n + 1)
                    v.scalar_tensor_tensor(BX[:, n % 2, :], P[:, PB + n % 2, :], w["bb"][:, n:n + 1], DTX[:], ALU.add, ALU.mult).then_inc(s("bx"), 1)

                def out(n):
                    v.wait_ge(s("c_full"), NS * b + n + 1)
                    v.wait_ge(s("scan"), NS * b + n + 3)
                    v.wait_ge(s("summed"), NS * b + n + 1)
                    v.scalar_tensor_tensor(HC[:, n % 2, :], P[:, PC + n % 2, :], w["bc"][:, n:n + 1], H[:, n % 2, :], ALU.add, ALU.mult).then_inc(s("hc"), 1)

                inp(0)
                for n in range(NS):
                    v.wait_ge(s("da"), NS * b + n + 1)
                    v.wait_ge(s("bx"), NS * b + n + 3)
                    v.wait_ge(s("hc"), NS * b + n + 1)
                    v.tensor_tensor_scan(H[:, n % 2, :], DA[:, n % 2, :], BX[:, n % 2, :], 0.0, ALU.mult, ALU.add).then_inc(s("scan"), 1)
                    if n + 1 < NS:
                        inp(n + 1)
                    if n >= 1:
                        out(n - 1)
                out(NS - 1)
                v.wait_ge(s("summed"), NS * (b + 1) + 2)
                v.tensor_tensor(YZ[:], P[:, PY, :], Z[:], ALU.mult).then_inc(s("yz"), 1)
                v.wait_ge(s("m_full"), 3 * b + 3)
                x = k.X[:, bass.ds(b * QT, QT), :]
                v.tensor_tensor(x, x, P[:, PM, :].rearrange("p (t d) -> p t d", d=D), ALU.add).then_inc(s("m_free"), 1)


def l3_attn(k, i):
    nc, P = k.nc, k.P
    w, w_ready = weights(k, i)
    SC = 128 ** -0.5
    with ExitStack() as st, phase(k) as (block, s):
        sb = lambda n, sh: st.enter_context(nc.sbuf_tensor(n, sh, F32))
        PK, E, WT = (sb(f"a_{n}", [128, B, QT, 128]) for n in ("pk", "e", "wt"))
        MX, SM, GQ, GK, WR, WM = sb("a_mx", [128, 2, B, QT]), sb("a_sm", [128, 2, B, QT]), sb("a_gq", [128, B, 128]), \
            sb("a_gk", [128, B]), sb("a_wr", [128, B, 128]), sb("a_wm", [128, B, 128])

        @block.sync
        def _(sp):
            load_weights(k, i + 1)

        @block.tensor
        def _(pe):
            w_ready(pe)
            for n, bank in (("wq", 0), ("wk", 4)):
                for b in range(B):
                    for t in range(QT):
                        last = pe.matmul(P[:, bank + b, 128 * t:128 * (t + 1)], k.XT[:, N * b + 128 * t:N * b + 128 * (t + 1)], w[n], start=True, stop=True)
                    last.then_inc(s("proj"), 1)
            for b in range(B):
                pe.wait_ge(s("weighted"), b + 1)
                for t in range(QT):
                    last = pe.matmul(P[:, b, 0:128], k.ones[:, 0:128], WT[:, b, t, :], start=t == 0, stop=t == QT - 1)
                last.then_inc(s("gq"), 1)
            for b in range(B):
                pe.wait_ge(s("weighted"), B + b + 1)
                for t in range(QT):
                    last = pe.matmul(P[:, b, 128:129], WT[:, b, t, :], k.ones[:, 0:1], start=t == 0, stop=t == QT - 1)
                last.then_inc(s("gk"), 1)
            for b in range(B):
                pe.wait_ge(s("wr"), b + 1)
                pe.matmul(P[:, b, 256:384], w["wvt"], WR[:, b, :], start=True, stop=True).then_inc(s("m"), 1)
            for b in range(B):
                pe.wait_ge(s("wm"), b + 1)
                for t in range(QT):
                    last = pe.matmul(P[:, 4 + b, 128 * t:128 * (t + 1)], k.XT[:, N * b + 128 * t:N * b + 128 * (t + 1)], WM[:, b, :], start=True, stop=True)
                last.then_inc(s("y"), 1)

        @block.scalar
        def _(a):
            for n in range(2 * B):
                a.wait_ge(s("shifted"), n + 1)
                a.activation(E[:, n % B, :, :], E[:, n % B, :, :], ACT.Exp, scale=SC).then_inc(s("exp"), 1)

        @block.vector
        def _(v):
            w_ready(v)
            own = [0]

            def step(ins):
                own[0] += 1
                ins.then_inc(s("step"), 1)
                v.wait_ge(s("step"), own[0])

            over = lambda c: c.unsqueeze(2).to_broadcast([128, QT, 128])
            for j in range(2):
                for b in range(B):
                    if j == 0:
                        v.wait_ge(s("proj"), b + 1)
                        x = P[:, b, :].rearrange("p (t d) -> p t d", d=128)
                    else:
                        v.wait_ge(s("proj"), B + b + 1)
                        v.wait_ge(s("gq"), b + 1)
                        step(v.tensor_copy(GQ[:, b, :], P[:, b, 0:128]))
                        x = PK[:, b, :, :]
                        step(v.tensor_tensor(x, P[:, 4 + b, :].rearrange("p (t d) -> p t d", d=128),
                                             GQ[:, b:b + 1, :].to_broadcast([128, QT, 128]), ALU.mult))
                    step(v.tensor_reduce(MX[:, j, b, :], x, AX.X, ALU.max, negate=True))
                    v.tensor_tensor(E[:, b, :, :], x, over(MX[:, j, b, :]), ALU.add).then_inc(s("shifted"), 1)
                for b in range(B):
                    x = P[:, b, :].rearrange("p (t d) -> p t d", d=128) if j == 0 else PK[:, b, :, :]
                    v.wait_ge(s("exp"), B * j + b + 1)
                    step(v.tensor_reduce(SM[:, j, b, :], E[:, b, :, :], AX.X, ALU.add))
                    step(v.reciprocal(SM[:, j, b, :], SM[:, j, b, :]))
                    step(v.tensor_tensor(WT[:, b, :, :], x, over(SM[:, j, b, :]), ALU.mult))
                    v.tensor_tensor(WT[:, b, :, :], WT[:, b, :, :], E[:, b, :, :], ALU.mult).then_inc(s("weighted"), 1)
            for b in range(B):
                v.wait_ge(s("gk"), b + 1)
                step(v.tensor_copy(GK[:, b:b + 1], P[:, b, 128:129]))
                v.tensor_scalar(WR[:, b, :], w["wr"], GK[:, b:b + 1], None, ALU.mult).then_inc(s("wr"), 1)
            for b in range(B):
                v.wait_ge(s("m"), b + 1)
                v.tensor_tensor(WM[:, b, :], P[:, b, 256:384], w["wq"], ALU.add).then_inc(s("wm"), 1)
            for b in range(B):
                v.wait_ge(s("y"), b + 1)
                x = k.X[:, QT * b:QT * (b + 1), :].rearrange("p t d -> p (t d)")
                v.tensor_tensor(x, x, P[:, 4 + b, :], ALU.add)


def route(k, i, E, mode):
    nc, P = k.nc, k.P
    w, w_ready = weights(k, i)
    with ExitStack() as st, phase(k) as (block, s):
        sb = lambda n, sh: st.enter_context(nc.sbuf_tensor(n, sh, F32))
        k.serial += 1
        q = k.serial
        L, SCO, SEL = (sb(f"r_{n}_{q}", [128, TILES, E]) for n in ("l", "sco", "sel"))
        c1, c2 = (sb(f"r_{n}_{q}", [128, TILES, 1]) for n in ("c1", "c2"))
        T1, T2 = (sb(f"r_{n}_{q}", [128, TILES * E * max(E, 8)]) for n in ("t1", "t2"))
        GS, GM = (sb(f"r_{n}_{q}", [128, TILES, 4]) for n in ("gs", "gm"))
        WE = k.WE[:, :, 0:E]

        @block.tensor
        def _(pe):
            w_ready(pe)
            for t in range(TILES):
                last = pe.matmul(P[:, 0, E * t:E * (t + 1)], k.XT[:, 128 * t:128 * (t + 1)], w["router"], start=True, stop=True)
            last.then_inc(s("logits"), 1)

        @block.scalar
        def _(a):
            a.wait_ge(s("shifted"), 1)
            a.activation(SCO[:], L[:], ACT.Sigmoid if mode == "groups" else ACT.Exp).then_inc(s("exp"), 1)

        @block.vector
        def _(v):
            own = [0]

            def step(ins):
                own[0] += 1
                ins.then_inc(s("step"), 1)
                v.wait_ge(s("step"), own[0])

            def choose(x, m, n, top, out):
                t1 = T1[:, 0:m * n * n].rearrange("p (m i j) -> p m i j", i=n, j=n)
                t2 = T2[:, 0:m * n * n].rearrange("p (m i j) -> p m i j", i=n, j=n)
                xj = x.unsqueeze(2).to_broadcast([128, m, n, n])
                xi = x.unsqueeze(3).to_broadcast([128, m, n, n])
                earlier = k.before[:, 0:n, 0:n].unsqueeze(1).to_broadcast([128, m, n, n])
                v.tensor_tensor(t2, xj, xi, ALU.is_gt)
                step(v.tensor_tensor(t1, xj, xi, ALU.is_ge))
                step(v.tensor_tensor(t1, t1, earlier, ALU.mult))
                step(v.tensor_tensor(t1, t1, t2, ALU.max))
                step(v.tensor_reduce(out, t1, AX.X, ALU.add))
                step(v.tensor_scalar(out, out, top - 0.5, None, ALU.is_lt))

            def per(c, n=E):
                return c.to_broadcast([128, TILES, n])

            v.wait_ge(s("logits"), 1)
            lg = P[:, 0, 0:TILES * E].rearrange("p (t e) -> p t e", e=E)
            if mode == "groups":
                v.tensor_copy(L[:], lg).then_inc(s("shifted"), 1)
                v.wait_ge(s("exp"), 1)
                w_ready(v)
                step(v.tensor_tensor(L[:], SCO[:], w["ebias"].unsqueeze(1).to_broadcast([128, TILES, E]), ALU.add))
                x4 = L[:].rearrange("p t (g e) -> p (t g) e", e=4)
                sel4 = SEL[:].rearrange("p t (g e) -> p (t g) e", e=4)
                choose(x4, TILES * 4, 4, 2, sel4)
                step(v.tensor_tensor(sel4, sel4, x4, ALU.mult))
                step(v.tensor_reduce(GS[:].rearrange("p t g -> p (t g)"), sel4, AX.X, ALU.add))
                choose(GS[:], TILES, 4, 2, GM[:])
                step(v.tensor_tensor(x4, x4, GM[:].rearrange("p t g -> p (t g)").unsqueeze(2).to_broadcast([128, TILES * 4, 4]), ALU.mult))
                choose(L[:], TILES, E, 4, SEL[:])
                step(v.tensor_tensor(SEL[:], SEL[:], SCO[:], ALU.mult))
                step(v.tensor_reduce(c1[:, :, 0], SEL[:], AX.X, ALU.add))
                step(v.tensor_scalar(c1[:], c1[:], 1e-20, None, ALU.add))
                step(v.reciprocal(c1[:], c1[:]))
                step(v.tensor_scalar(c1[:], c1[:], 2.5, None, ALU.mult))
                v.tensor_tensor(WE, SEL[:], per(c1[:]), ALU.mult)
                return
            step(v.tensor_reduce(c1[:, :, 0], lg, AX.X, ALU.max))
            v.tensor_tensor(L[:], lg, per(c1[:]), ALU.subtract).then_inc(s("shifted"), 1)
            v.wait_ge(s("exp"), 1)
            if mode == "plain":
                step(v.tensor_reduce(c1[:, :, 0], SCO[:], AX.X, ALU.add))
                choose(SCO[:], TILES, E, 2, SEL[:])
                step(v.tensor_tensor(SEL[:], SEL[:], SCO[:], ALU.mult))
            else:
                v.wait_ge(s("shifted"), 1)
                choose(L[:], TILES, E, 2, SEL[:])
                step(v.tensor_tensor(SEL[:], SEL[:], SCO[:], ALU.mult))
                step(v.tensor_reduce(c1[:, :, 0], SEL[:], AX.X, ALU.add))
            step(v.reciprocal(c2[:], c1[:]))
            v.tensor_tensor(WE, SEL[:], per(c2[:]), ALU.mult)


def experts(k, i, units, gated, func, hidden_in=None):
    nc, P = k.nc, k.P
    w, w_ready = weights(k, i)
    nb = len(units[0][0])
    n_up = sum(len(u[0]) for u in units)
    n_out = sum(len(u[1]) for u in units)
    with ExitStack() as st, phase(k) as (block, s):
        k.serial += 1
        sb = lambda n, sh: st.enter_context(nc.sbuf_tensor(f"{n}_{k.serial}", sh, F32))
        HT = sb("e_h", [128, 2, nb, N])
        SG = sb("e_g", [128, 2, N])
        PG, PU, PY = 0, 2, 4

        @block.tensor
        def _(pe):
            w_ready(pe)
            pe.sem_inc(s("down"), 2)
            with pe.Fori(0, 4) as c:
                x = k.XT[:, bass.ds(c * N, N)]
                nu, no, nh = [0], [0], [0]

                def up(u):
                    for col in units[u][0]:
                        j = nu[0]
                        nu[0] += 1
                        pe.wait_ge(s("act"), n_up * c + j + 1)
                        pe.matmul(P[:, PG + j % 2, :], w["w1"][:, col:col + 128], x, start=True, stop=True).then_inc(s("gate"), 1)
                        if gated:
                            pe.wait_ge(s("hidden"), n_up * c + j + 1)
                            pe.matmul(P[:, PU + j % 2, :], w["w3"][:, col:col + 128], x, start=True, stop=True).then_inc(s("up"), 1)

                def down(u):
                    nh[0] += len(units[u][0])
                    if gated:
                        pe.wait_ge(s("hidden"), n_up * c + nh[0] + 2)
                    else:
                        pe.wait_ge(s("act"), n_up * c + nh[0] + 2)
                    for m, (_, parts) in enumerate(units[u][1]):
                        j = no[0]
                        no[0] += 1
                        pe.wait_ge(s("added"), n_out * c + j + 1)
                        for t in range(4):
                            for n, (blk, rows, w2) in enumerate(parts):
                                last = pe.matmul(P[:, PY + j % 2, 128 * t:128 * (t + 1)], HT[rows, u % 2, blk, 128 * t:128 * (t + 1)], w2,
                                                 start=n == 0, stop=n == len(parts) - 1)
                        last.then_inc(s("y"), 1)
                    pe.sem_inc(s("down"), 1)

                for u in range(len(units) + 1):
                    if u < len(units):
                        up(u)
                    if u >= 1:
                        down(u - 1)

        def half_free(eng, c, u):
            eng.wait_ge(s("down"), len(units) * c + u + 1)

        @block.scalar
        def _(a):
            a.sem_inc(s("act"), 2)
            with a.Fori(0, 4) as c:
                j = 0
                for u in range(len(units)):
                    if not gated:
                        half_free(a, c, u)
                    for blk in range(len(units[u][0])):
                        a.wait_ge(s("gate"), n_up * c + j + 1)
                        if gated:
                            a.wait_ge(s("hidden"), n_up * c + j + 1)
                        dst = SG[:, j % 2, :] if gated else HT[:, u % 2, blk, :]
                        a.activation(dst, P[:, PG + j % 2, :], func).then_inc(s("act"), 1)
                        j += 1

        @block.vector
        def _(v):
            v.sem_inc(s("hidden"), 2)
            if hidden_in is not None:
                v.tensor_tensor(k.X[:], k.X[:], hidden_in[:], ALU.add).then_inc(s("added"), 2)
            else:
                v.sem_inc(s("added"), 2)
            with v.Fori(0, 4) as c:
                j, jo = [0], [0]

                def hidden(u):
                    half_free(v, c, u)
                    for blk in range(len(units[u][0])):
                        v.wait_ge(s("act"), n_up * c + j[0] + 3)
                        v.wait_ge(s("up"), n_up * c + j[0] + 1)
                        v.tensor_tensor(HT[:, u % 2, blk, :], SG[:, j[0] % 2, :], P[:, PU + j[0] % 2, :], ALU.mult).then_inc(s("hidden"), 1)
                        j[0] += 1

                def out(u):
                    for e, _ in units[u][1]:
                        v.wait_ge(s("y"), n_out * c + jo[0] + 1)
                        v.wait_ge(s("added"), n_out * c + jo[0] + 2)
                        for t in range(4):
                            x = k.X[:, bass.ds(c * 4 + t, 1), :].rearrange("p a d -> p (a d)")
                            y = P[:, PY + jo[0] % 2, 128 * t:128 * (t + 1)]
                            if e is None:
                                last = v.tensor_tensor(x, x, y, ALU.add)
                            else:
                                last = v.scalar_tensor_tensor(x, y, k.WE[:, bass.ds(c * 4 + t, 1), e], x, ALU.mult, ALU.add)
                        last.then_inc(s("added"), 1)
                        jo[0] += 1

                for u in range(len(units) + 1):
                    if gated and u < len(units):
                        hidden(u)
                    if u >= 1:
                        out(u - 1)


ALL = slice(0, 128)


def expert_units(k, i, n, blocks):
    w, _ = weights(k, i)
    return [([128 * (blocks * e + f) for f in range(blocks)],
             [(e, [(f, ALL, w["w2"][:, 128 * (blocks * e + f):128 * (blocks * e + f + 1)]) for f in range(blocks)])]) for e in range(n)]


def l3_units(k, i):
    w, _ = weights(k, i)
    units = [([128 * p], [(2 * p + h, [(0, slice(64 * h, 64 * h + 64), w["w2"][64 * h:64 * h + 64, 128 * p:128 * (p + 1)])]) for h in range(2)])
             for p in range(8)]
    return units + [([1024], [(None, [(0, ALL, w["w2"][:, 1024:1152])])])]


def begin(k, i):
    nc, P = k.nc, k.P
    with phase(k) as (block, s):
        @block.sync
        def _(sp):
            sp.dma_start(k.X[:], k.x_in).then_inc(s("x"), 16)
            load_weights(k, i)

        @block.scalar
        def _(a):
            a.dma_start(k.cst[:], k.const_in).then_inc(s("const"), 16)
            a.dma_start(k.CT[:], k.ctx_in).then_inc(s("ctx"), 16)
            a.wait_ge(s("ctx"), 16)

        @block.gpsimd
        def _(g):
            g.memset(k.ones[:], 1.0)

        @block.tensor
        def _(pe):
            pe.wait_ge(s("x"), 16)
            pe.wait_ge(s("const"), 16)
            for c in range(4):
                for t in range(4):
                    last = pe.transpose(P[:, c, 128 * t:128 * (t + 1)], k.X[:, 4 * c + t, :], k.ident[:])
                last.then_inc(s("turned"), 1)

        @block.vector
        def _(v):
            v.wait_ge(s("const"), 16)
            v.tensor_copy(k.identb[:], k.ident[:])
            v.tensor_copy(k.maskq[:], k.cst[:, 128:256])
            v.tensor_copy(k.maskk[:], k.cst[:, 256:384])
            for c in range(4):
                v.wait_ge(s("turned"), c + 1)
                v.tensor_copy(k.XT[:, N * c:N * (c + 1)], P[:, c, :])


def build(nc, x, const, ctx, kaug, wd, where, out):
    k = Ctx()
    k.nc, k.x_in, k.const_in, k.ctx_in, k.kaug, k.wd, k.where, k.out, k.serial = nc, x, const, ctx, kaug, wd, where, out, 0
    sb = lambda n, sh, dt=F32: nc.alloc_sbuf_tensor(n, sh, dt)
    k.X, k.XT = sb("X", [128, TILES, D]), sb("XT", [128, TOK])
    wmax = max(w.shape[1] for w in wd)
    k.W = [sb(f"W{n}", [128, max([w.shape[1] for j, w in enumerate(wd) if j % 2 == n])]) for n in range(2)]
    k.XB, k.CB, k.CI, k.CT = sb("XB", [128, N]), sb("CB", [CD, CTX]), sb("CI", [CD, CTX]), sb("CT", [CD, 3, B * CTX])
    k.cst = sb("cst", [128, 640])
    k.ident, k.before = k.cst[:, 0:128], k.cst[:, 384:640].rearrange("p (i j) -> p i j", j=16)
    k.identb, k.maskq, k.maskk = sb("identb", [128, 128], BF16), sb("maskq", [128, 128], BF16), sb("maskk", [128, 128], BF16)
    k.ones = sb("ones", [128, 128])
    k.stats, k.mv = sb("stats", [128, TILES, 6]), sb("mv", [128, TILES, 2])
    k.inv, k.rstd, k.nmr, k.sq = (sb(n, [128, TILES]) for n in ("inv", "rstd", "nmr", "sq"))
    k.P = nc.alloc_psum_tensor("P", [128, 8, 512], F32)
    k.pool = [nc.alloc_semaphore(f"count{n}") for n in range(24)]
    k.w_loaded = [nc.alloc_semaphore(f"weights_{n}") for n in STAGES]

    k.stored = nc.alloc_semaphore("stored")

    begin(k, FIRST)
    for i in range(FIRST, LAST):
        with ExitStack() as st:
            if STAGES[i] in ("L0_ffn", "L1_ffn", "L2_ffn"):
                k.Hs = st.enter_context(nc.sbuf_tensor(f"Hs{i}", [128, TILES, D], F32))
            if "ffn" in STAGES[i]:
                k.WE = st.enter_context(nc.sbuf_tensor(f"WE{i}", [128, TILES, 16], F32))
            run_stage(k, i, STAGES[i])
            normalise(k, i, k.X, k.X, 1e-5, store=i == LAST - 1)


def run_stage(k, i, name):
    nc = k.nc
    if True:
        if name == "L0_attn":
            l0_attn(k, i)
        elif name == "L0_xattn":
            l0_xattn(k, i)
        elif name == "L0_ffn":
            with nc.sbuf_tensor("NX0", [128, TILES, D], F32) as nx:
                normalise(k, i, k.X, nx, 1e-5, scale="n1w", shift="n1b")
                l0_ffn_attention(k, i)
                normalise(k, i, k.Hs, nx, 1e-5, scale="n2w", shift="n2b")
            route(k, i, 8, "plain")
            experts(k, i, expert_units(k, i, 8, 2), False, ACT.Gelu_apprx_tanh, hidden_in=k.Hs)
        elif name == "L1_attn":
            l1_attn(k, i)
        elif name == "L1_xattn":
            l1_xattn(k, i)
        elif name == "L1_ffn":
            with nc.sbuf_tensor("NX1", [128, TILES, D], F32) as nx:
                normalise(k, i, k.X, nx, 1e-5, rms=True, scale="n1w")
            ffn_attention(k, i, False, False, 1)
            with nc.sbuf_tensor("NX2", [128, TILES, D], F32) as nx:
                normalise(k, i, k.Hs, nx, 1e-5, rms=True, scale="n2w")
            route(k, i, 8, "shares")
            experts(k, i, expert_units(k, i, 8, 2), True, ACT.Silu, hidden_in=k.Hs)
        elif name == "L2_attn":
            l2_attn(k, i)
        elif name == "L2_xattn":
            l2_xattn(k, i)
        elif name == "L2_ffn":
            eps = 1.1920928955078125e-07
            with nc.sbuf_tensor("NX3", [128, TILES, D], F32) as nx:
                normalise(k, i, k.X, nx, eps, rms=True, scale="n1w")
            ffn_attention(k, i, True, True, 4)
            with nc.sbuf_tensor("NX4", [128, TILES, D], F32) as nx:
                normalise(k, i, k.Hs, nx, eps, rms=True, scale="n2w")
            route(k, i, 4, "shares")
            experts(k, i, expert_units(k, i, 4, 3), True, ACT.Silu, hidden_in=k.Hs)
        elif name == "L3_attn":
            l3_attn(k, i)
        elif name == "L3_xattn":
            l3_xattn(k, i)
        else:
            route(k, i, 16, "groups")
            experts(k, i, l3_units(k, i), True, ACT.Silu)


def tokens_down(x):
    return np.ascontiguousarray(x.reshape(TILES, 128, D).transpose(1, 0, 2).reshape(128, TILES * D))


FIRST, LAST = 0, 12


def kernel(**inputs):
    import concourse.bacc as _bacc
    from concourse.bass_utils import run_bass_kernel_spmd as _run

    a = {n: np.asarray(v) for n, v in inputs.items()}
    nc = _bacc.Bacc("TRN2", target_bir_lowering=False, num_devices=1)
    ctx = a["ctx_768"].transpose(2, 0, 1)
    org, ipa = np.zeros_like(ctx), np.zeros_like(ctx)
    org[:, :, :CTX - IPA] = ctx[:, :, :CTX - IPA]
    ipa[:, :, CTX - IPA:] = ctx[:, :, CTX - IPA:]
    arrays = {"x": tokens_down(a["x"]), "const": constants(), "ctx": np.concatenate([t.reshape(CD, B * CTX) for t in (ctx, org, ipa)], 1)}
    where = []
    for n in STAGES:
        arrays[f"w_{n}"], wh = pack(n, a)
        where.append(wh)
    for n, v in zip(("kaug_l2a", "kaug_l2x", "kaug_l3x"), key_rows()):
        arrays[n] = v
    arrays = {n: np.ascontiguousarray(v) for n, v in arrays.items()}
    d = {n: nc.dram_tensor(f"in_{n}", v.shape, F32, kind="ExternalInput").ap() for n, v in arrays.items()}
    out = nc.dram_tensor("out_0", (128, TILES * D), F32, kind="ExternalOutput").ap()
    tiled = lambda p: p.rearrange("p (t d) -> p t d", d=D)
    kaug = [d["kaug_l2a"].rearrange("a (h k) -> a h k", k=N), d["kaug_l2x"].rearrange("a (h k) -> a h k", k=CTX),
            d["kaug_l3x"].rearrange("a (h k) -> a h k", k=CTX)]
    build(nc, tiled(d["x"]), d["const"], d["ctx"].rearrange("c (s k) -> c s k", s=3), kaug, [d[f"w_{n}"] for n in STAGES], where, tiled(out))
    r = _run(nc, [{f"in_{n}": v for n, v in arrays.items()}], core_ids=[0])
    o = r.results[0]["out_0"]
    return o.reshape(128, TILES, D).transpose(1, 0, 2).reshape(B, N, D)
```

```python
import math
from contextlib import ExitStack, contextmanager

import numpy as np
import concourse.bass as bass
from concourse import mybir

F32 = mybir.dt.float32
BF16 = mybir.dt.bfloat16
ALU = mybir.AluOpType
ACT = mybir.ActivationFunctionType
AX = mybir.AxisListType

FIRST, LAST = 0, 12

B, N, D = 4, 512, 128
TOK = B * N
TILES = TOK // 128
QT = N // 128
CTX, CD = 77, 96
IPA = 4
NH = 16
GROUP = 4
PARTS = ((0, 0), (1, 0), (0, 1), (1, 1), (2, 0), (0, 2))
MAX_ROW = 8 * len(PARTS)
RANK = 32
BF16_ONE = 0x3F80
NEG = -1e30
BANK_ST, BANK_PV, BANK_V, BANK_A = 2, 4, 6, 7
RING = {"V": (6, 0, 1, 2), "A": (7, 3, 4, 5)}

STAGES = ["L0_attn", "L0_xattn", "L0_ffn", "L1_attn", "L1_xattn", "L1_ffn",
          "L2_attn", "L2_xattn", "L2_ffn", "L3_attn", "L3_xattn", "L3_ffn"]


def per_head(w):
    return np.ascontiguousarray(w).reshape(128, 1)


def stacking(side):
    out = np.zeros((128, NH // 2, 3, 128), np.float32)
    for p in range(NH // 2):
        for j in range(2):
            for c, pair in enumerate(PARTS):
                for d in range(8):
                    out[16 * p + 8 * j + d, p, pair[side], 64 * j + 8 * c + d] = 1.0
    return (out.reshape(128, -1) * BF16_ONE).astype(np.uint16)


def half_turn(w, dh):
    v = w.reshape(w.shape[0], -1, 2, dh // 2)
    return v[:, :, ::-1].reshape(w.shape)


def rope_tables(dh):
    inv = 1.0 / 10000.0 ** (np.arange(0, dh, 2, dtype=np.float32) / np.float32(dh))
    ang = np.outer(np.arange(N, dtype=np.float32), inv.astype(np.float32)).astype(np.float32)
    ang = np.concatenate([ang, ang], axis=1).T
    cos, sin = np.zeros((128, N), np.float32), np.zeros((128, N), np.float32)
    for r0 in range(0, 128, dh):
        cos[r0:r0 + dh] = np.cos(ang)
        sin[r0:r0 + dh] = np.sin(ang)
        sin[r0:r0 + dh // 2] = -np.sin(ang[:dh // 2])
    return cos, sin


def repeat_heads(w):
    return np.repeat(w.reshape(128, 4, 8), 4, axis=1).reshape(128, 128)


def slopes():
    start = 2.0 ** (-2.0 ** (-(math.log2(NH) - 3)))
    return [8.0 * start * start ** i for i in range(NH)]


def kv_cols(w, out):
    return w.transpose(1, 0, 2).reshape(w.shape[1], -1)


def rows_tiled(w, tile=128):
    return w.reshape(-1, tile, w.shape[1]).transpose(1, 0, 2).reshape(tile, -1)


def row(v):
    return v.reshape(1, -1)


def pieces(stage, a):
    g = lambda n: a[f"{stage}_{n}"]
    if stage == "L0_attn":
        return dict(wq=g("Wq").T, wk=g("Wk").T, wv=g("Wv").T, wp=g("Wp").T, bp=row(g("bp")),
                    gam=np.stack([g("gq"), g("gk"), g("gv")], 1), bet=np.stack([g("bq"), g("bk"), g("bv")], 1),
                    blocks=np.kron(np.eye(16), np.ones((8, 8))))
    if stage == "L0_xattn":
        wkv, bkv = g("Wkv").reshape(NH, 2, 8, CD), g("bkv").reshape(NH, 2, 8)
        return dict(wq=g("Wq").T, wk=wkv[:, 0].reshape(128, CD).T,
                    wv=wkv[:, 1].reshape(128, CD).T, wo=g("Wo").T,
                    bq=per_head(g("bq")), bk=per_head(bkv[:, 0]),
                    bv=row(bkv[:, 1]), bo=row(g("bo")))
    if stage == "L0_ffn":
        qkv = g("qkv_weight")
        k, v = (np.repeat(qkv[128 + 32 * i:160 + 32 * i].reshape(4, 8, 128), 4, axis=0).reshape(128, 128).T for i in (0, 1))
        return dict(n1w=g("ln1_weight").reshape(-1, 1), n1b=g("ln1_bias").reshape(-1, 1),
                    n2w=g("ln2_weight").reshape(-1, 1), n2b=g("ln2_bias").reshape(-1, 1),
                    wqkv=np.concatenate([qkv[:128].T, k, v], 1), wo=g("proj_weight").T, router=g("router_weight").T,
                    w1=kv_cols(g("moe_w1"), 256), w2=rows_tiled(g("moe_w2").reshape(-1, 128)))
    if stage == "L1_attn":
        return dict(win=g("Win"), wg=g("Wg"), wout=g("Wout"), wdt=g("Wdt"), wbc=np.concatenate([g("Wb"), g("Wc")], 1), a=g("A"),
                    bin=g("b_in").reshape(-1, 1), bg=g("bg").reshape(-1, 1), convw=g("convw"),
                    convb=g("convb").reshape(-1, 1), bdt=g("bdt").reshape(-1, 1),
                    bb=np.broadcast_to(g("bb"), (128, 16)), bc=np.broadcast_to(g("bc"), (128, 16)), bout=row(g("bout")))
    if stage == "L1_xattn":
        return dict(wq=g("Wq"), wk=g("Wk"), wv=g("Wv"), wo=g("Wo"), bq=per_head(g("bq")), bk=per_head(g("bk")),
                    bv=row(g("bv")), bo=row(g("bo")))
    if stage == "L1_ffn":
        return dict(n1w=g("ln1_w").reshape(-1, 1), n2w=g("ln2_w").reshape(-1, 1),
                    wq=g("wq").T, wk=g("wk").T, wv=g("wv").T, wo=g("wo").T, router=g("gate_w").T,
                    w1=kv_cols(g("w1").transpose(0, 2, 1), 256), w3=kv_cols(g("w3").transpose(0, 2, 1), 256),
                    w2=rows_tiled(g("w2").transpose(0, 2, 1).reshape(-1, 128)))
    if stage == "L2_attn":
        w, b = g("w_qkv").reshape(128, NH, 3, 64), g("b_qkv").reshape(NH, 3, 64)
        q, k, v = (w[:, :, i].reshape(128, 1024) for i in range(3))
        bq, bk, bv = (b[:, i].reshape(1, 1024) for i in range(3))
        cos, sin = rope_tables(64)
        cols = lambda r: r.reshape(8, 128).T
        return dict(wq=q, wqt=half_turn(q, 64), wk=k, wkt=half_turn(k, 64), wv=v,
                    bq=cols(bq), bqt=cols(half_turn(bq, 64)), bk=cols(bk), bkt=cols(half_turn(bk, 64)), bv=bv,
                    wo=rows_tiled(g("w_out").reshape(1024, 128)), bo=row(g("b_out")), cos=cos, sin=sin)
    if stage == "L2_xattn":
        return dict(wq=g("Wq"), wk=g("Wk"), wv=g("Wv"), wo=rows_tiled(g("Wout")), bo=row(g("bout")))
    if stage == "L2_ffn":
        cos, sin = rope_tables(8)
        return dict(n1w=g("g1").reshape(-1, 1), n2w=g("g2").reshape(-1, 1),
                    wq=g("wq"), wqt=half_turn(g("wq"), 8), wk=repeat_heads(g("wk")), wkt=repeat_heads(half_turn(g("wk"), 8)),
                    wv=g("wv"), wo=g("wo"),
                    router=g("gate"), w1=kv_cols(g("w1"), 384), w3=kv_cols(g("w3"), 384),
                    w2=rows_tiled(g("w2").reshape(-1, 128)), cos=cos, sin=sin)
    if stage == "L3_attn":
        return dict(wq=g("Wq"), wk=g("Wk"), wvt=g("Wv").T, wr=g("Wr"))
    if stage == "L3_xattn":
        seg = np.zeros((CTX, 2), np.float32)
        seg[:CTX - IPA, 0] = 1.0
        seg[CTX - IPA:, 1] = 1.0
        alpha = np.concatenate([np.broadcast_to(g(f"{n}_alpha"), (128, 1)) for n in "qkvo"], 1)
        ups = np.concatenate([g("q_up"), g("k_up"), g("v_up")], 0)
        downs = np.zeros((3 * RANK, 128), np.float32)
        for n, name in enumerate("qkv"):
            d = g(f"{name}_down")
            downs[RANK * n:RANK * (n + 1), :d.shape[0]] = d.T
        return dict(wq=g("Wq"), wk=g("Wk"), wki=g("Wk_ipa"), wv=g("Wv"), wvi=g("Wv_ipa"), wo=rows_tiled(g("Wo")),
                    ups=ups, downs=downs, odt=g("o_down").T, ou=g("o_up"), bo=row(g("bo")), seg=seg, alpha=alpha)
    gate, up = (g(n).reshape(8, 128, 128).transpose(2, 0, 1).reshape(128, 1024) for n in ("gate_w", "up_w"))
    return dict(router=g("router_weight").T, ebias=np.broadcast_to(g("e_bias"), (128, 16)),
                w1=np.concatenate([gate, g("sh_gate_w").T], 1), w3=np.concatenate([up, g("sh_up_w").T], 1),
                w2=np.concatenate([rows_tiled(g("down_w").transpose(0, 2, 1).reshape(1024, 128)), g("sh_down_w").T], 1))


def pack(stage, a):
    ps = pieces(stage, a)
    where, at = {}, 0
    for n, p in ps.items():
        where[n] = (p.shape[0], at, p.shape[1])
        at += p.shape[1]
    out = np.zeros((128, at), np.float32)
    for n, p in ps.items():
        r, c, w = where[n]
        out[:r, c:c + w] = p
    return out, where


def constants():
    i = np.arange(128)
    ident = np.eye(128, dtype=np.float32)
    over = np.where(i[None, :] > i[:, None], np.float32(NEG), np.float32(0))
    before = np.broadcast_to((np.arange(16)[None, :] < np.arange(16)[:, None]).astype(np.float32).reshape(1, 256), (128, 256))
    takes_off = ((i % 64 == MAX_ROW) | (i % 64 == MAX_ROW + 1)).astype(np.float32).reshape(128, 1)
    return np.concatenate([ident, over, over.T, before, takes_off], 1)


def key_rows():
    s = np.array(slopes(), np.float32)
    sc = np.float32(1.0 / math.sqrt(192.0))
    alibi = (s[:, None] * (np.arange(N, dtype=np.float32) - N // 2)[None, :] / sc).astype(np.float32)
    l2a = np.stack([alibi, np.ones_like(alibi)], 0).reshape(2, -1)
    l2x = np.ones((1, 8 * CTX), np.float32)
    seg = np.zeros((2, NH, CTX), np.float32)
    seg[0, :, :CTX - IPA] = 1.0
    seg[1, :, CTX - IPA:] = 1.0
    return l2a, l2x, seg.reshape(2, -1)


class Sems:

    def __init__(self, pool):
        self.pool, self.names = pool, {}

    def __call__(self, name):
        if name not in self.names:
            self.names[name] = self.pool[len(self.names)]
        return self.names[name]


class Ctx:
    pass


@contextmanager
def phase(k):
    s = Sems(k.pool)
    with k.nc.Block() as block:
        yield block, s
    for sem in s.names.values():
        k.nc.gpsimd.sem_clear(sem)
    k.nc.all_engine_barrier()


def weights(k, i):
    where, tile = k.where[i], k.W[i % 2]
    get = {n: tile[0:r, c:c + w] for n, (r, c, w) in where.items()}

    def ready(eng):
        eng.wait_ge(k.w_loaded[i], 16)
    return get, ready


def load_weights(k, i):
    if i >= LAST:
        return
    cols = k.wd[i].shape[1]
    k.nc.sync.dma_start(k.W[i % 2][:, 0:cols], k.wd[i]).then_inc(k.w_loaded[i], 16)


def normalise(k, i, src, dst, eps, rms=False, scale=None, shift=None, store=False, prefetch=None):
    nc = k.nc
    w, w_ready = weights(k, i)
    P = k.P
    half = TILES // 2
    on_v = ((0, 4), (8, 10, 12, 14))
    on_a = ((1, 2, 3, 5, 6, 7), (9, 11, 13, 15))
    k.serial += 1
    with ExitStack() as st, phase(k) as (block, s):
        sb = lambda n, *shape: st.enter_context(nc.sbuf_tensor(f"{n}_{k.serial}", [128, *shape], F32))
        stats, mv = sb("stats", TILES, 6), sb("mv", TILES, 2)
        inv, rstd, nmr, sq = (sb(n, TILES) for n in ("inv", "rstd", "nmr", "sq"))

        @block.sync
        def _(sp):
            if prefetch is not None:
                load_weights(k, prefetch)
            if store:
                sp.wait_ge(s("norm_v"), sum(len(t) for t in on_v))
                sp.wait_ge(s("norm_a"), sum(len(t) for t in on_a))
                sp.dma_start(k.out, dst[:]).then_inc(k.stored, 16)
                sp.wait_ge(k.stored, 16)

        def turned(eng, c):
            eng.wait_ge(s("turned"), c + 1)
            return k.XT[:, N * c:N * (c + 1)], P[:, c, :]

        @block.vector
        def _(v):
            def apply(h):
                ts = slice(half * h, half * (h + 1))
                v.wait_ge(s("rstd"), h + 1)
                if not rms:
                    v.scalar_tensor_tensor(nmr[:, ts], mv[:, ts, 0], -1.0, rstd[:, ts], ALU.mult, ALU.mult).then_inc(s("nmr"), 1)
                for t in on_v[h]:
                    if rms:
                        v.tensor_scalar(dst[:, t, :], src[:, t, :], rstd[:, t:t + 1], None, ALU.mult).then_inc(s("norm_v"), 1)
                    else:
                        v.tensor_scalar(dst[:, t, :], src[:, t, :], mv[:, t, 0:1], rstd[:, t:t + 1],
                                        ALU.subtract, ALU.mult).then_inc(s("norm_v"), 1)

            for h in range(2):
                ts = slice(half * h, half * (h + 1))
                for t in range(ts.start, ts.stop):
                    v.bn_stats(stats[:, t, :], src[:, t, :]).then_inc(s("stats"), 1)
                    if t == half + 2:
                        apply(0)
                v.wait_ge(s("stats"), ts.stop)
                for t in range(ts.start, ts.stop):
                    v.bn_aggr(mv[:, t, :], stats[:, t, :]).then_inc(s("aggr"), 1)
                v.wait_ge(s("aggr"), ts.stop)
                if rms:
                    v.tensor_tensor(sq[:, ts], mv[:, ts, 0], mv[:, ts, 0], ALU.mult).then_inc(s("small"), 1)
                    v.wait_ge(s("small"), 2 * h + 1)
                    v.scalar_tensor_tensor(inv[:, ts], sq[:, ts], eps, mv[:, ts, 1], ALU.add, ALU.add).then_inc(s("small"), 1)
                    v.wait_ge(s("small"), 2 * h + 2)
                else:
                    v.tensor_scalar(inv[:, ts], mv[:, ts, 1], eps, None, ALU.add).then_inc(s("small"), 1)
                    v.wait_ge(s("small"), h + 1)
                v.reciprocal(inv[:, ts], inv[:, ts]).then_inc(s("inv"), 1)
            apply(1)
            if not store:
                if scale is not None:
                    w_ready(v)
                for c in (1, 3):
                    o, i_ = turned(v, c)
                    if scale is not None and shift is not None:
                        v.tensor_scalar(o, i_, w[scale], w[shift], ALU.mult, ALU.add)
                    elif scale is not None:
                        v.tensor_scalar(o, i_, w[scale], None, ALU.mult)
                    else:
                        v.tensor_copy(o, i_)

        @block.scalar
        def _(a):
            if scale is not None and not store:
                w_ready(a)
            for h in range(2):
                ts = slice(half * h, half * (h + 1))
                a.wait_ge(s("inv"), h + 1)
                a.activation(rstd[:, ts], inv[:, ts], ACT.Sqrt).then_inc(s("rstd"), 1)
                a.wait_ge(s("rstd"), h + 1)
                if not rms:
                    a.wait_ge(s("nmr"), h + 1)
                for t in on_a[h]:
                    a.activation(dst[:, t, :], src[:, t, :], ACT.Identity, scale=rstd[:, t:t + 1],
                                 bias=0.0 if rms else nmr[:, t:t + 1]).then_inc(s("norm_a"), 1)
                if not store:
                    o, i_ = turned(a, 2 * h)
                    a.activation(o, i_, ACT.Identity, scale=1.0 if scale is None else w[scale], bias=0.0 if shift is None else w[shift])

        @block.tensor
        def _(pe):
            if not store:
                for c in range(4):
                    pe.wait_ge(s("norm_v"), sum(t < 4 * (c + 1) for g in on_v for t in g))
                    pe.wait_ge(s("norm_a"), sum(t < 4 * (c + 1) for g in on_a for t in g))
                    for t in range(4):
                        last = pe.transpose(P[:, c, 128 * t:128 * (t + 1)], dst[:, 4 * c + t, :], k.ident[:])
                    last.then_inc(s("turned"), 1)


class Attention:

    def __init__(self, k, heads, dh, nk, scale, causal=False, aug=1, segs=((0, None),), clip=False, vrep=1,
                 jobs=(), bo=None, wo=None, src=None, dst=None, static=()):
        self.k, self.H, self.dh, self.nk, self.scale, self.causal, self.aug = k, heads, dh, nk, scale, causal, aug
        self.segs, self.clip, self.vrep, self.jobs, self.bo, self.wo = segs, clip, vrep, jobs, bo, wo
        self.src, self.dst, self.static = src, dst, static
        self.narrow = dh == 8
        self.ns = len(segs)
        self.gs = 2 if self.narrow else 1
        self.pg = GROUP if self.narrow else 1
        self.kt = -(-nk // 128)
        self.kp = min(nk, 128)
        self.units = QT if nk == N else 1
        self.s_banks = (0, 1, 5) if self.narrow and nk == N else (0, 1) if nk == N else (0,)
        self.s_ring = len(self.s_banks)
        self.vc = dh + 1
        self.tr_units = self.ns
        self.tr_banks = (BANK_A, BANK_A) if clip or 5 in self.s_banks else (1 if self.ns == 2 else 5, BANK_A)
        self.groups = heads // self.gs
        self.n_tr = heads // self.pg * self.tr_units
        self.nf = heads * dh // 128
        self.lag = self.gs + 1
        self.ot_ch = ["VA"[c % 2] for c in range(self.nf)]
        self.n_v = sum(j["ch"] == "V" for j in jobs) + self.groups + self.ot_ch.count("V") + 1
        self.n_a = sum(j["ch"] == "A" for j in jobs) + self.ot_ch.count("A")
        self.n_rope = sum(j["ch"] == "R" for j in jobs)
        self.n_own = sum({"rope_split": 5, "split": 3}.get(j["kind"], 0) for j in jobs) + \
            (self.groups * (2 if clip else 1) if self.narrow else 0)

    def operand(self, t, h, rows):
        p = 64 * (h % 2) if self.narrow and rows < 64 else 0
        return t[p:p + rows, h // self.gs if t is self.k.QA else h, :]

    def width(self, t):
        return N - 128 * t if self.causal else N

    def pe_start(self, pe, s):
        pe.sem_inc(s("value"), 2 * self.ns)

    def pe(self, pe, s, b):
        k, H, nk, kp = self.k, self.H, self.nk, self.kp
        P, QA, KA, VA, PT = k.P, k.QA, k.KA, k.VA, k.PT
        cnt = {"V": 0, "A": 0}
        per = {"V": self.n_v, "A": self.n_a}
        free = {"V": "v_free", "A": "a_free"}
        bank = {"V": BANK_V, "A": BANK_A}

        def evacuated(ch):
            pe.wait_ge(s(free[ch]), b * per[ch] + cnt[ch] + 1)

        def done(ins, ch):
            cnt[ch] += 1
            ins.then_inc(s("v_full" if ch == "V" else "a_full"), 1)

        pe.wait_ge(s("static"), (b + 1) * len(self.static))
        for j in self.jobs:
            if j["ch"] == "R":
                continue
            if "needs" in j:
                pe.wait_ge(s("v_free"), b * self.n_v + j["needs"] + 1)
            ch = j["ch"]
            ring = RING[ch]
            pe.wait_ge(s(free[ch]), b * per[ch] + max(cnt[ch] - len(ring) + 1, 0) + 1)
            mms = j["mms"](b)
            for n, (l, r) in enumerate(mms):
                last = pe.matmul(P[0:j["m"], ring[cnt[ch] % len(ring)], 0:j["n"]], l, r, start=n == 0, stop=n == len(mms) - 1)
            done(last, ch)
        evacuated("V")
        evacuated("A")
        if self.n_rope:
            pe.wait_ge(s("rope_taken"), (b + 1) * self.n_rope + 2)
        R0 = 128 if self.narrow else 64 if self.aug == self.ns else 65
        R = 128
        sb, tb = [0], [0]

        def scores(h, u):
            pe.wait_ge(s("max_done"), b * H * self.units + sb[0] + 1)
            bk = self.s_banks[sb[0] % self.s_ring]
            sb[0] += 1
            q, kk = self.operand(QA, h, R0), self.operand(KA, h, R0)
            if self.units == 1:
                for t in range(QT):
                    last = pe.matmul(P[:, bk, nk * t:nk * (t + 1)], q[:, 128 * t:128 * (t + 1)], kk[:, 0:nk],
                                     start=True, stop=True)
            else:
                w = 128 * (u + 1) if self.causal else nk
                last = pe.matmul(P[:, bk, 0:w], q[:, 128 * u:128 * (u + 1)], kk[:, 0:w], start=True, stop=not self.causal)
                if self.causal:
                    last = pe.matmul(P[:, bk, w - 128:w], k.identb[:], k.maskq[:], start=False, stop=True)
            last.then_inc(s("score"), 1)

        def transposed(h, t):
            n = b * H * self.kt + tb[0]
            bk = BANK_ST + tb[0] % 2
            q, kk = self.operand(QA, h, R), self.operand(KA, h, R)
            if self.clip:
                pe.wait_ge(s("clipped"), n + 1)
                pe.matmul(P[0:kp, bk, :], self.operand(KA, h, MAX_ROW)[:, 0:nk], self.operand(QA, h, MAX_ROW), start=True, stop=True)
                p = 64 * (h % 2)
                last = pe.matmul(P[0:kp, (1, 5)[h % 2], :], k.pick[p:p + 64, 0:nk], QA[p:p + 64, h // 2, :], start=True, stop=True)
            else:
                pe.wait_ge(s("exp_done"), n + 1)
                w = self.width(t)
                last = pe.matmul(P[0:kp, bk, 0:w], kk[:, 128 * t:128 * t + kp], q[:, N - w:N], start=True, stop=not self.causal)
                if self.causal:
                    last = pe.matmul(P[0:kp, bk, 0:128], k.identb[:], k.maskk[:], start=False, stop=True)
            tb[0] += 1
            last.then_inc(s("score_t"), 1)

        def turn_max(g):
            if self.narrow:
                pe.wait_ge(s("max_ready"), b * self.groups + g + 1)
            else:
                pe.wait_ge(s("max_done"), b * H * self.units + (g + 1) * self.units + self.s_ring)
            evacuated("V")
            for t in range(QT):
                if self.narrow:
                    last = pe.transpose(P[:, BANK_V, 0:256].bitcast(BF16)[:, 128 * t:128 * (t + 1)], k.MB[:, t, g, :], k.identb[:])
                else:
                    last = pe.transpose(P[0:self.aug, BANK_V, 128 * t:128 * (t + 1)], k.M64[:, t, g, 0:self.aug], k.ident[:])
            done(last, "V")

        def values(h, tiles):
            if tiles[0] == 0:
                pe.wait_ge(s("exp_done"), (b * H + h + 1) * self.kt + 2)
            for g in range(self.ns):
                if tiles[0] == 0 and h % self.pg == 0:
                    pe.wait_ge(s("pv_read"), (b * (H // self.pg) + h // self.pg) * self.ns + g + 1)
                p = 32 * (h % self.pg) if self.narrow else 0
                m = 32 if self.narrow else self.vc
                for t in tiles:
                    w = self.width(t)
                    last = pe.matmul(P[p:p + m, BANK_PV + g, N - w:N], VA[:, t, h // self.vrep, m * g:m * (g + 1)],
                                     PT[:, h % 2, t, N - w:N], start=t == 0, stop=t == self.kt - 1)
                if tiles[-1] == self.kt - 1:
                    last.then_inc(s("value"), 1)

        def turn_out(h):
            u0 = h // self.pg
            pe.wait_ge(s("pv_read"), (b * (H // self.pg) + u0 + 1) * self.ns + self.ns)
            for u in range(self.tr_units):
                idx = u0 * self.tr_units + u
                tr = self.tr_banks[idx % 2]
                pe.wait_ge(s("norm_done"), b * self.n_tr + idx + (2 if self.tr_banks[0] == BANK_A else 1))
                nt = QT // self.tr_units
                for ti in range(nt):
                    t = u * nt + ti
                    if self.narrow:
                        last = pe.transpose(P[:, tr, 128 * t:128 * (t + 1)], k.OA[:, u0 % 2, 128 * t:128 * (t + 1)], k.ident[:])
                        continue
                    for g in range(self.ns):
                        c = self.vc * (self.ns * ti + g)
                        src = k.OA[0:self.vc, g if self.ns == 2 else u0 % 2, 128 * t:128 * (t + 1)]
                        last = pe.transpose(P[:, tr, c:c + self.vc], src, k.ident[0:self.vc, 0:self.vc])
                last.then_inc(s("turned_out"), 1)

        for i in range(H + self.lag + 2):
            for u in range(QT):
                if i < H and u < self.units:
                    scores(i, u)
                if 0 <= i - self.lag < H:
                    if (i - self.lag) % self.gs == 0 and u == 0:
                        evacuated("V")
                    if u < self.kt:
                        transposed(i - self.lag, u)
                if self.narrow and self.kt == QT and 0 <= i - self.lag - 1 < H:
                    values(i - self.lag - 1, [u])
            if i and i % self.gs == 0 and i // self.gs <= self.groups:
                turn_max(i // self.gs - 1)
            h = i - self.lag - 2
            if h >= 0 and h % self.pg == self.pg - 1:
                turn_out(h)
            if not (self.narrow and self.kt == QT) and 0 <= h + 1 < H:
                values(h + 1, range(self.kt))
        pe.wait_ge(s("norm_done"), (b + 1) * self.n_tr + 2)
        first = dict(cnt)
        for c in range(self.nf):
            ch = self.ot_ch[c]
            ring = RING[ch]
            pe.wait_ge(s(free[ch]), b * per[ch] + first[ch] + max(c // 2 - len(ring) + 1, 0) + 1)
            for t in range(QT):
                last = pe.transpose(P[:, ring[c // 2 % len(ring)], 128 * t:128 * (t + 1)], k.O[:, t, 128 * c:128 * (c + 1)], k.ident[:])
            done(last, ch)
        evacuated("V")
        evacuated("A")
        for t in range(QT):
            mms = [(k.OT[:, c, 128 * t:128 * (t + 1)], self.wo[:, 128 * c:128 * (c + 1)]) for c in range(self.nf)]
            if self.bo is not None:
                mms.append((k.ones[0:1, 0:128], self.bo))
            for n, (l, r) in enumerate(mms):
                last = pe.matmul(P[:, BANK_V, 128 * t:128 * (t + 1)], l, r, start=n == 0, stop=n == len(mms) - 1)
        done(last, "V")
        assert cnt == per, (cnt, per)

    def dve_start(self, v, s):
        v.sem_inc(s("v_free"), 1)
        v.sem_inc(s("max_done"), self.s_ring)
        v.sem_inc(s("norm_done"), 2)
        if self.clip:
            v.sem_inc(s("clipped"), 2)

    def dve(self, v, s, b):
        k, H = self.k, self.H
        P = k.P
        cnt, own, sb = [0], [0], [0]

        def full():
            cnt[0] += 1
            v.wait_ge(s("v_full"), b * self.n_v + cnt[0])

        def step(ins):
            own[0] += 1
            ins.then_inc(s("own"), 1)
            v.wait_ge(s("own"), b * self.n_own + own[0])

        def split(src, parts):
            step(v.tensor_copy(parts[:, 0, :], src))
            step(v.tensor_tensor(src, src, parts[:, 0, :], ALU.subtract))
            step(v.tensor_copy(parts[:, 1, :], src))
            v.tensor_tensor(parts[:, 2, :], src, parts[:, 1, :], ALU.subtract).then_inc(s("v_free"), 1)

        for j in self.jobs:
            if j["ch"] != "V":
                continue
            bk = RING["V"][cnt[0] % len(RING["V"])]
            full()
            ps = P[0:j["m"], bk, 0:j["n"]]
            if j["kind"] == "half1":
                v.wait_ge(s("rope_taken"), b * self.n_rope + j["n_pair"] + 1)
            elif j["kind"] in ("split", "rope1"):
                v.wait_ge(s("v_free"), b * self.n_v + cnt[0])
            kind = j["kind"]
            if kind == "cols":
                v.tensor_scalar(j["dst"], ps, j["bias"], None, ALU.add).then_inc(s("v_free"), 1)
            elif kind == "pair":
                v.tensor_copy(j["dst"][0], P[0:64, bk, 0:j["n"]])
                v.tensor_copy(j["dst"][1], P[64:128, bk, 0:j["n"]]).then_inc(s("v_free"), 1)
            elif kind == "halves":
                v.tensor_scalar(j["dst"][0], ps[0:64, :], j["bias"][0:64, :], None, ALU.add)
                v.tensor_scalar(j["dst"][1], ps[64:128, :], j["bias"][64:128, :], None, ALU.add).then_inc(s("v_free"), 1)
            elif kind == "rows":
                v.tensor_copy(j["dst"], ps.rearrange("p (h d) -> p h d", d=self.dh)).then_inc(s("v_free"), 1)
            elif kind == "split":
                parts, bias = j["dst"], 0.0 if j["bias"] is None else j["bias"]
                step(v.tensor_scalar(parts[:, 0, :], ps, bias, None, ALU.add))
                step(v.scalar_tensor_tensor(j["tmp"], ps, bias, parts[:, 0, :], ALU.add, ALU.subtract))
                step(v.tensor_copy(parts[:, 1, :], j["tmp"]))
                v.tensor_tensor(parts[:, 2, :], j["tmp"], parts[:, 1, :], ALU.subtract).then_inc(s("v_free"), 1)
            elif kind == "rope1":
                v.scalar_tensor_tensor(k.R1, ps, j["bias"], j["tab"], ALU.add, ALU.mult).then_inc(s("v_free"), 1)
            elif kind in ("half1", "half2"):
                r = k.PT[:, j["n_pair"] % 2, 0 if kind == "half1" else 1, :]
                v.scalar_tensor_tensor(r, ps, j["bias"], j["tab"], ALU.add, ALU.mult).then_inc(s("v_free"), 1)
                if kind == "half2":
                    v.wait_ge(s("v_free"), b * self.n_v + cnt[0] + 1)
                    r0 = k.PT[:, j["n_pair"] % 2, 0, :]
                    v.tensor_tensor(r0, r0, r, ALU.add).then_inc(s("roped"), 1)
            else:
                step(v.scalar_tensor_tensor(k.R2, ps, j["bias"], j["tab"], ALU.add, ALU.mult))
                step(v.tensor_tensor(k.R1, k.R1, k.R2, ALU.add))
                split(k.R1, j["dst"])

        def maxima(h, u):
            sb[0] += 1
            v.wait_ge(s("score"), b * H * self.units + sb[0])
            bk = self.s_banks[(sb[0] - 1) % self.s_ring]
            ts = slice(0, QT) if self.units == 1 else slice(u, u + 1)
            w = self.nk if self.units == 1 or not self.causal else 128 * (u + 1)
            for n, (k0, k1) in enumerate(self.segs):
                k1 = w if k1 is None else k1
                src = P[:, bk, 0:w * (ts.stop - ts.start)].rearrange("p (t k) -> p t k", k=w)[:, :, k0:k1]
                col = k.MF[:, ts, h] if self.narrow else k.M64[:, ts, h, self.aug - self.ns + n]
                last = v.tensor_reduce(col, src, AX.X, ALU.max, negate=True)
            last.then_inc(s("max_done"), 1)
            if self.narrow and h % 2 == 1 and u == self.units - 1:
                v.wait_ge(s("max_done"), b * H * self.units + sb[0] + self.s_ring)
                g = h // 2
                m = k.MF[:, :, 2 * g:2 * g + 2]
                if self.clip:
                    step(v.tensor_scalar(m, m, k.clip_at, -k.clip_at, ALU.min, ALU.max))
                rows = k.MB[:, :, g, :].rearrange("p t (j r) -> p t j r", j=2)
                step(v.tensor_copy(rows[:, :, :, MAX_ROW], m))
                v.tensor_tensor(rows[:, :, :, MAX_ROW + 1], m, rows[:, :, :, MAX_ROW], ALU.subtract).then_inc(s("max_ready"), 1)

        def place_max(g):
            full()
            if self.narrow:
                v.tensor_tensor(k.QA[:, g, :], k.QA[:, g, :], P[:, BANK_V, 0:256].bitcast(BF16), ALU.add).then_inc(s("v_free"), 1)
            else:
                v.tensor_copy(k.QA[64:64 + self.aug, g, :], P[0:self.aug, BANK_V, :]).then_inc(s("v_free"), 1)

        def clip_scores(h):
            n = b * H + h
            kp = self.kp
            v.wait_ge(s("score_t"), n + 1)
            lim = k.clip_at
            v.wait_ge(s("clipped"), n + 2)
            v.tensor_scalar(k.C1[0:kp, :], P[0:kp, BANK_ST + h % 2, :], lim, -lim, ALU.min, ALU.max).then_inc(s("raw_clip"), 1)
            v.wait_ge(s("raw_clip"), n + 1)
            v.wait_ge(s("exp_done"), n + 1)
            v.tensor_tensor(k.C2[0:kp, h % 2, :], k.C1[0:kp, :], P[0:kp, (1, 5)[h % 2], :], ALU.add).then_inc(s("clipped"), 1)

        def divide(h):
            dh, vc = self.dh, self.vc
            for u in range(self.tr_units):
                n = b * self.n_tr + h // self.pg * self.tr_units + u
                v.wait_ge(s("turned_out"), n + 1)
                v.wait_ge(s("norm_done"), n + 2)
                tr = self.tr_banks[(h // self.pg * self.tr_units + u) % 2]
                if self.narrow:
                    ps = P[:, tr, :].rearrange("p (t h c) -> p t h c", h=GROUP, c=32)
                    g = h // GROUP
                    v.reciprocal(k.rc[:], ps[:, :, :, dh]).then_inc(s("recip"), 1)
                    v.wait_ge(s("recip"), n + 1)
                    v.tensor_tensor(k.O[:, :, 32 * g:32 * g + 32].rearrange("p t (h d) -> p t h d", d=8), ps[:, :, :, 0:dh],
                                    k.rc[:].unsqueeze(3).to_broadcast([128, QT, GROUP, dh]), ALU.mult).then_inc(s("norm_done"), 1)
                    continue
                nt = QT // self.tr_units
                ps = P[:, tr, 0:nt * vc * self.ns].rearrange("p (t c) -> p t c", c=vc * self.ns)
                o = k.O[:, u * nt:(u + 1) * nt, dh * h:dh * (h + 1)]
                if self.ns == 1:
                    r = k.rc[:, 0:nt, 0]
                    v.reciprocal(r, ps[:, :, dh]).then_inc(s("recip"), 1)
                    v.wait_ge(s("recip"), n + 1)
                    v.tensor_tensor(o, ps[:, :, 0:dh], r.unsqueeze(2).to_broadcast([128, nt, dh]), ALU.mult).then_inc(s("norm_done"), 1)
                else:
                    r0, r1 = k.rc[:, 0:nt, 0], k.rc[:, 0:nt, 1]
                    v.reciprocal(r0, ps[:, :, dh])
                    v.reciprocal(r1, ps[:, :, 2 * vc - 1]).then_inc(s("recip"), 1)
                    v.wait_ge(s("recip"), 2 * n + 1)
                    t2 = k.seg2[:, 0:nt, :]
                    v.tensor_tensor(o, ps[:, :, 0:dh], r0.unsqueeze(2).to_broadcast([128, nt, dh]), ALU.mult)
                    v.tensor_tensor(t2, ps[:, :, vc:2 * vc - 1], r1.unsqueeze(2).to_broadcast([128, nt, dh]), ALU.mult).then_inc(s("recip"), 1)
                    v.wait_ge(s("recip"), 2 * n + 2)
                    v.tensor_tensor(o, o, t2, ALU.add).then_inc(s("norm_done"), 1)

        for i in range(H + self.lag + 2):
            if i < H:
                for u in range(self.units):
                    maxima(i, u)
            if self.clip and 0 <= i - self.lag < H:
                clip_scores(i - self.lag)
            if i and i % self.gs == 0 and i // self.gs <= self.groups:
                place_max(i // self.gs - 1)
            h = i - self.lag - 2
            if h >= 0 and h % self.pg == self.pg - 1:
                divide(h)
        for c in range(self.nf):
            if self.ot_ch[c] == "V":
                full()
                v.tensor_copy(k.OT[:, c, :], P[:, RING["V"][c // 2 % 4], :]).then_inc(s("v_free"), 1)
        full()
        y = P[:, BANK_V, :].rearrange("p (t d) -> p t d", d=D)
        v.tensor_tensor(self.dst[:, bass.ds(b * QT, QT), :], self.src[:, bass.ds(b * QT, QT), :], y, ALU.add).then_inc(s("v_free"), 1)
        assert cnt[0] == self.n_v and own[0] == self.n_own, (cnt, self.n_v, own, self.n_own)

    def act_start(self, a, s):
        a.sem_inc(s("a_free"), 1)
        a.sem_inc(s("exp_done"), 2)
        a.sem_inc(s("pv_read"), self.ns)
        if self.n_rope:
            a.sem_inc(s("rope_taken"), 2)

    def act(self, a, s, b):
        k, H = self.k, self.H
        P = k.P
        cnt = [0]

        def full():
            cnt[0] += 1
            a.wait_ge(s("a_full"), b * self.n_a + cnt[0])

        for j in self.jobs:
            if j["ch"] == "R":
                n = j["n_pair"]
                a.wait_ge(s("roped"), b * self.n_rope + n + 1)
                a.activation(j["dst"][0], k.PT[0:64, n % 2, 0, :], ACT.Copy)
                a.activation(j["dst"][1], k.PT[64:128, n % 2, 0, :], ACT.Copy).then_inc(s("rope_taken"), 1)
            if j["ch"] != "A":
                continue
            bk = RING["A"][cnt[0] % len(RING["A"])]
            full()
            ps = P[0:j["m"], bk, 0:j["n"]]
            if j["kind"] == "cols":
                a.activation(j["dst"], ps, ACT.Identity, bias=j["bias"]).then_inc(s("a_free"), 1)
            elif j["kind"] == "cast":
                a.activation(j["dst"], ps, ACT.Copy).then_inc(s("a_free"), 1)
            elif j["kind"] == "halves":
                a.activation(j["dst"][0], ps[0:64, :], ACT.Identity, bias=j["bias"][0:64, :])
                a.activation(j["dst"][1], ps[64:128, :], ACT.Identity, bias=j["bias"][64:128, :]).then_inc(s("a_free"), 1)
            elif j["kind"] == "pair":
                a.activation(j["dst"][0], P[0:64, bk, 0:j["n"]], ACT.Copy)
                a.activation(j["dst"][1], P[64:128, bk, 0:j["n"]], ACT.Copy).then_inc(s("a_free"), 1)
            else:
                a.activation(j["dst"], ps.rearrange("p (h d) -> p h d", d=self.dh), ACT.Copy).then_inc(s("a_free"), 1)
        tb = [0]

        def exponentials(h):
            for t in range(self.kt):
                tb[0] += 1
                w = self.width(t)
                a.wait_ge(s("clipped" if self.clip else "score_t"), b * H * self.kt + tb[0] + (2 if self.clip else 0))
                if t == 0:
                    a.wait_ge(s("value"), (b * H + h + 1) * self.ns)
                src = k.C2[0:self.kp, h % 2, :] if self.clip else P[0:self.kp, BANK_ST + (tb[0] - 1) % 2, 0:w]
                a.activation(k.PT[0:self.kp, h % 2, t, N - w:N], src, ACT.Exp, scale=self.scale).then_inc(s("exp_done"), 1)

        def copy_out(h):
            m = 128 if self.narrow else self.vc
            for g in range(self.ns):
                a.wait_ge(s("value"), (b * H + h) * self.ns + g + 1 + 2 * self.ns)
                slot = g if self.ns == 2 else h // self.pg % 2
                a.activation(k.OA[0:m, slot, :], P[0:m, BANK_PV + g, :], ACT.Copy).then_inc(s("pv_read"), 1)

        for i in range(self.lag, H + self.lag + 1):
            if i - self.lag < H:
                exponentials(i - self.lag)
            h = i - self.lag - 1
            if h >= 0 and h % self.pg == self.pg - 1:
                copy_out(h)
        for c in range(self.nf):
            if self.ot_ch[c] == "A":
                full()
                a.activation(k.OT[:, c, :], P[:, RING["A"][c // 2 % 4], :], ACT.Copy).then_inc(s("a_free"), 1)
        assert cnt[0] == self.n_a

    def pool(self, g, s, b):
        for dst, src in self.static:
            g.tensor_copy(dst, src(b)).then_inc(s("static"), 1)
        g.wait_ge(s("value"), (b * self.H + 2) * self.ns + 1)

    def run(self, i, prefetch=None, once=None, kaug=None):
        k, nc = self.k, self.k.nc
        w, w_ready = weights(k, i)
        ctx = self.nk < 128
        n_consts = self.ns + 1 + (1 if ctx or self.narrow else 0)
        with phase(k) as (block, s):
            @block.sync
            def _(sp):
                if self.narrow:
                    sp.dma_start(k.SEL[:, 0], k.sel_in[0]).then_inc(s("select"), 16)
                    sp.dma_start(k.SEL[:, 1], k.sel_in[1]).then_inc(s("select"), 16)
                if prefetch is not None:
                    load_weights(k, prefetch)
                if kaug is not None:
                    sp.wait_ge(s("keys_zero"), 1)
                    sp.dma_start(k.KA[64:64 + self.aug, 0:self.H, 0:self.nk], kaug).then_inc(s("kaug"), 16)

            @block.gpsimd
            def _(g):
                w_ready(g)
                g.memset(k.KA[:] if self.narrow else k.KA[64:128, :, :], 0.0).then_inc(s("keys_zero"), 1)
                g.wait_ge(s("keys_zero"), 1)
                g.memset(k.MB[:] if self.narrow else k.M64[:], 0.0 if self.narrow else 1.0).then_inc(s("consts"), 1)
                if ctx or self.narrow:
                    g.memset(k.VA[:], 0.0).then_inc(s("consts"), 1)
                    g.wait_ge(s("consts"), 2)
                if self.ns == 1:
                    g.memset(k.VA[:, :, :, self.dh:self.dh + 1], 1.0).then_inc(s("consts"), 1)
                else:
                    for n in range(2):
                        g.tensor_copy(k.VA[0:self.nk, 0, :, (self.dh + 1) * (n + 1) - 1],
                                      w["seg"][:, n:n + 1].to_broadcast([self.nk, self.H])).then_inc(s("consts"), 1)
                with g.Fori(0, B) as b:
                    self.pool(g, s, b)

            @block.vector
            def _(v):
                w_ready(v)
                self.dve_start(v, s)
                if ctx:
                    v.memset(k.PT[64:128, :, :, :], 0.0).then_inc(s("zeros"), 1)
                if not self.narrow:
                    v.memset(k.QA[64:128, :, :], 0.0).then_inc(s("zeros"), 1)
                n_zeros = ctx + (not self.narrow)
                if n_zeros:
                    v.wait_ge(s("zeros"), n_zeros)
                if once:
                    once(v, s)
                if self.narrow:
                    v.wait_ge(s("keys_zero"), 1)
                v.wait_ge(s("consts"), n_consts)
                with v.Fori(0, B) as b:
                    self.dve(v, s, b)

            @block.scalar
            def _(a):
                w_ready(a)
                self.act_start(a, s)
                if ctx:
                    a.wait_ge(s("zeros"), 1)
                if once:
                    a.wait_ge(s("once"), 1)
                if self.narrow:
                    a.wait_ge(s("keys_zero"), 1)
                a.wait_ge(s("consts"), n_consts)
                a.activation(k.warm[:], k.ones[0:1, 0:1], ACT.Exp)
                with a.Fori(0, B) as b:
                    self.act(a, s, b)

            @block.tensor
            def _(pe):
                w_ready(pe)
                self.pe_start(pe, s)
                pe.wait_ge(s("consts"), n_consts)
                if self.narrow:
                    pe.wait_ge(s("select"), 32)
                if kaug is not None:
                    pe.wait_ge(s("kaug"), 16)
                    pe.wait_ge(s("zeros"), 1)
                with pe.Fori(0, B) as b:
                    self.pe(pe, s, b)


def batch_cols(t, b, n=N):
    return t[:, bass.ds(b * n, n)]


def narrow_jobs(k, w, kv, nk, vcols, rope=False):
    jobs = []
    for name, n, parts in (("q", N, k.PQ), ("k", nk, k.PK[:, :, 0:nk])):
        if kv == "x":
            x = lambda b: k.XB[:]
        else:
            x = (lambda b: batch_cols(k.XT, b)) if name == "q" else (lambda b: k.CB[:, :])
        mk = lambda wt, x=x: (lambda b: [(w[wt], x(b))])
        if rope:
            jobs.append(dict(ch="V", kind="rope1", m=128, n=n, mms=mk("w" + name), bias=0.0, tab=w["cos"]))
            jobs.append(dict(ch="V", kind="rope_split", m=128, n=n, mms=mk("w" + name + "t"), bias=0.0, tab=w["sin"], dst=parts))
        else:
            jobs.append(dict(ch="V", kind="split", m=128, n=n, mms=mk("w" + name), bias=w.get("b" + name), tmp=k.R1[:, 0:n], dst=parts))
    kp = min(nk, 128)
    for t in range(-(-nk // 128)):
        x = k.XB if kv == "x" else k.CB
        def mms(b, t=t, x=x):
            r = [(x[:, kp * t:kp * (t + 1)], w["wv"])]
            if "bv" in w:
                r.append((k.ones[0:1, 0:kp], w["bv"]))
            return r
        jobs.append(dict(ch="A", kind="rows", m=kp, n=vcols, mms=mms, dst=k.VA[0:kp, t, 0:vcols // 8, 0:8]))
    for side, dst, parts, n in ((0, k.QA, k.PQ, N), (1, k.KA, k.PK, nk)):
        for p in range(NH // 2):
            d = dst[:, p, 0:n] if side == 0 else (dst[0:64, 2 * p, 0:n], dst[64:128, 2 * p + 1, 0:n])
            jobs.append(dict(ch="A" if side == 0 else "VA"[p % 2], kind="cast" if side == 0 else "halves", m=128, n=n, dst=d, bias=k.max_rows,
                             needs=(side + 1) * (2 if rope else 1),
                             mms=lambda b, side=side, p=p, parts=parts, n=n: [
                                 (k.SEL[:, side, 128 * (3 * p + c):128 * (3 * p + c + 1)], parts[:, c, 0:n]) for c in range(3)]))
    return jobs


@contextmanager
def attention_buffers(k, narrow, nk, heads, vheads, vc, clip=False, rope=False, segments=False):
    kt = -(-nk // 128)
    with ExitStack() as st:
        k.serial += 1
        def sb(name, shape, dt=F32):
            return st.enter_context(k.nc.sbuf_tensor(f"{name}_{k.serial}", shape, dt))
        tiles, dt = (heads // 2, BF16) if narrow else (heads, F32)
        k.QA = sb("QA", [128, tiles, N], dt)
        k.KA = sb("KA", [128, heads, nk], dt)
        k.VA = sb("VA", [128, kt, vheads, vc])
        k.PT = sb("PT", [128, 2, kt, N])
        nf = heads * (8 if narrow else 64) // 128
        k.O = sb("O", [128, QT, nf * 128])
        k.OT = k.PT[:].rearrange("p a t n -> p (a t) n") if nf == 2 * kt else sb("OT", [128, nf, N])
        if narrow:
            k.MB, k.MF = sb("MB", [128, QT, NH // 2, 128], BF16), sb("MF", [128, QT, NH])
            k.SEL = sb("SEL", [128, 2, NH // 2 * 3 * 128], BF16)
            k.PQ, k.PK = sb("PQ", [128, 3, N], BF16), sb("PK", [128, 3, nk], BF16)
            k.R1 = sb("R1", [128, N])[:]
            k.R2 = sb("R2", [128, N])[:] if rope else None
            k.OA = sb("OA", [128, 2, N])
            k.rc = sb("rc", [128, QT, GROUP])
        else:
            k.M64 = sb("M64", [128, QT, heads, 2])
            k.rc = sb("rc", [128, QT, 2])
            k.OA = sb("OA", [65, 2, N])
        if clip:
            k.C1, k.C2 = sb("C1", [128, N]), sb("C2", [128, 2, N])
        if segments:
            k.seg2 = sb("seg2", [128, QT, 64])
        yield sb


def self_static(k):
    return [(k.XB[:], lambda b: batch_cols(k.XT, b))]


def ctx_static(k):
    return [(k.CB[:, :], lambda b: k.CT[:, 0, bass.ds(b * CTX, CTX)])]


def l0_xattn(k, i):
    w, _ = weights(k, i)
    with attention_buffers(k, True, CTX, NH, NH, 32):
        Attention(k, NH, 8, CTX, 8 ** -0.5, jobs=narrow_jobs(k, w, "c", CTX, 128), bo=w["bo"], wo=w["wo"],
                  src=k.X, dst=k.X, static=ctx_static(k)).run(i, prefetch=i + 1)


def l1_xattn(k, i):
    w, _ = weights(k, i)
    k.clip_at = 10000.0 * math.sqrt(8.0)
    with attention_buffers(k, True, CTX, NH, NH, 32, clip=True):
        Attention(k, NH, 8, CTX, 8 ** -0.5, clip=True, jobs=narrow_jobs(k, w, "c", CTX, 128), bo=w["bo"], wo=w["wo"],
                  src=k.X, dst=k.X, static=ctx_static(k)).run(i, prefetch=i + 1)


def ffn_attention(k, i, causal, rope, vrep):
    w, _ = weights(k, i)
    vh = NH // vrep
    with attention_buffers(k, True, N, NH, vh, 32, rope=rope):
        Attention(k, NH, 8, N, 8 ** -0.5, causal=causal, vrep=vrep, jobs=narrow_jobs(k, w, "x", N, vh * 8, rope=rope),
                  wo=w["wo"], src=k.X, dst=k.Hs, static=self_static(k)).run(i, prefetch=i + 1)


def l2_attn(k, i):
    w, _ = weights(k, i)
    jobs = []
    with attention_buffers(k, False, N, NH, NH, 65):
        for n in range(16):
            (name, dst), g = (("q", k.QA), ("k", k.KA))[n // 8], n % 8
            cols = slice(128 * g, 128 * (g + 1))
            mk = lambda wt, cols=cols: (lambda b: [(w[wt][:, cols], k.XB[:])])
            jobs.append(dict(ch="V", kind="half1", n_pair=n, m=128, n=N, mms=mk("w" + name), bias=w["b" + name][:, g:g + 1], tab=w["cos"]))
            jobs.append(dict(ch="V", kind="half2", n_pair=n, m=128, n=N, mms=mk("w" + name + "t"), bias=w["b" + name + "t"][:, g:g + 1],
                             tab=w["sin"]))
            jobs.append(dict(ch="R", kind="pair", n_pair=n, dst=(dst[0:64, 2 * g, :], dst[0:64, 2 * g + 1, :])))
            if n % 2:
                t, u = n // 4, n // 2 % 2
                jobs.append(dict(ch="A", kind="rows", m=128, n=512, dst=k.VA[:, t, 8 * u:8 * u + 8, 0:64],
                                 mms=lambda b, t=t, u=u: [(k.XB[:, 128 * t:128 * (t + 1)], w["wv"][:, 512 * u:512 * (u + 1)]),
                                                          (k.ones[0:1, 0:128], w["bv"][:, 512 * u:512 * (u + 1)])]))
        once = lambda v, s: (v.memset(k.QA[64:66, :, :], 1.0).then_inc(s("once"), 1), v.wait_ge(s("once"), 1))
        Attention(k, NH, 64, N, 192 ** -0.5, causal=True, aug=2, jobs=jobs, bo=w["bo"], wo=w["wo"], src=k.X, dst=k.X,
                  static=self_static(k)).run(i, prefetch=i + 1, once=once, kaug=k.kaug[0])


def l2_xattn(k, i):
    w, _ = weights(k, i)
    jobs = []
    with attention_buffers(k, False, CTX, 8, 8, 65):
        for name, dst, n in (("wq", k.QA, N), ("wk", k.KA, CTX)):
            for g in range(4):
                jobs.append(dict(ch="VA"[g % 2], kind="pair", m=128, n=n, dst=[dst[0:64, 2 * g, 0:n], dst[0:64, 2 * g + 1, 0:n]],
                                 mms=lambda b, g=g, name=name: [(w[name][:, 128 * g:128 * (g + 1)],
                                                                 batch_cols(k.XT, b) if name == "wq" else k.CB[:, :])]))
        jobs.append(dict(ch="A", kind="rows", m=CTX, n=512, dst=k.VA[0:CTX, 0, :, 0:64], mms=lambda b: [(k.CB[:, :], w["wv"])]))
        Attention(k, 8, 64, CTX, 64 ** -0.5, jobs=jobs, bo=w["bo"], wo=w["wo"], src=k.X, dst=k.X,
                  static=ctx_static(k)).run(i, prefetch=i + 1, kaug=k.kaug[1])


def merge_low_rank(k, i):
    w, w_ready = weights(k, i)
    P = k.P
    full = (("wq", 128), ("wk", CD), ("wv", CD))
    with k.nc.sbuf_tensor("al", [128, 4], F32) as al, phase(k) as (block, s):
        @block.tensor
        def _(pe):
            w_ready(pe)
            for n, (_, rows) in enumerate(full):
                r = slice(RANK * n, RANK * (n + 1))
                for u in range(2):
                    pe.matmul(P[0:rows, 2 * n + u, :], w["downs"][r, 0:rows], w["ups"][r, 512 * u:512 * (u + 1)],
                              start=True, stop=True).then_inc(s("product"), 1)
            for c in range(8):
                last = pe.matmul(P[:, 6 + c // 4, 128 * (c % 4):128 * (c % 4 + 1)], w["odt"][:, 128 * c:128 * (c + 1)], w["ou"],
                                 start=True, stop=True)
                if c % 4 == 3:
                    last.then_inc(s("product"), 1)

        @block.vector
        def _(v):
            w_ready(v)
            v.tensor_scalar(al[:], w["alpha"], 1.0 / RANK, None, ALU.mult).then_inc(s("al"), 1)
            v.wait_ge(s("al"), 1)
            for n in range(8):
                name, rows = full[n // 2] if n < 6 else ("wo", 128)
                v.wait_ge(s("product"), n + 1)
                d = w[name][0:rows, 512 * (n % 2):512 * (n % 2 + 1)]
                v.scalar_tensor_tensor(d, P[0:rows, n, :], al[0:rows, n // 2:n // 2 + 1], d, ALU.mult, ALU.add)


def l3_xattn(k, i):
    w, _ = weights(k, i)
    merge_low_rank(k, i)
    with attention_buffers(k, False, CTX, NH, NH, 130, segments=True):
        x = lambda b: batch_cols(k.XT, b)
        jobs = []
        for g in range(8):
            c = slice(128 * g, 128 * (g + 1))
            jobs.append(dict(ch="VA"[g % 2], kind="pair", m=128, n=N, dst=[k.QA[0:64, 2 * g, :], k.QA[0:64, 2 * g + 1, :]],
                             mms=lambda b, c=c: [(w["wq"][:, c], x(b))]))
            jobs.append(dict(ch="AV"[g % 2], kind="pair", m=128, n=CTX, dst=[k.KA[0:64, 2 * g, :], k.KA[0:64, 2 * g + 1, :]],
                             mms=lambda b, c=c: [(w["wk"][:, c], k.CB[:, :]), (w["wki"][:, c], k.CI[:, :])]))
        for u in range(2):
            c = slice(512 * u, 512 * (u + 1))
            jobs.append(dict(ch="VA"[u], kind="rows", m=CTX, n=512, dst=k.VA[0:CTX, 0, 8 * u:8 * u + 8, 0:64],
                             mms=lambda b, c=c: [(k.CB[:, :], w["wv"][:, c])]))
            jobs.append(dict(ch="AV"[u], kind="rows", m=CTX, n=512, dst=k.VA[0:CTX, 0, 8 * u:8 * u + 8, 65:129],
                             mms=lambda b, c=c: [(k.CI[:, :], w["wvi"][:, c])]))
        Attention(k, NH, 64, CTX, 64 ** -0.5, aug=2, segs=((0, CTX - IPA), (CTX - IPA, CTX)), jobs=jobs, bo=w["bo"], wo=w["wo"],
                  src=k.X, dst=k.X,
                  static=[(k.CB[:, :], lambda b: k.CT[:, 1, bass.ds(b * CTX, CTX)]), (k.CI[:, :], lambda b: k.CT[:, 2, bass.ds(b * CTX, CTX)])]
                  ).run(i, prefetch=i + 1, kaug=k.kaug[2])


def l0_attn(k, i):
    nc, P = k.nc, k.P
    w, w_ready = weights(k, i)
    with ExitStack() as st, phase(k) as (block, s):
        sb = lambda n, sh: st.enter_context(nc.sbuf_tensor(n, sh, F32))
        S = [sb(f"l0_{n}", [128, TOK]) for n in "qkv"]
        VT, G, M = sb("l0_vt", [128, TILES, 128]), sb("l0_g", [128, B, 128]), sb("l0_m", [128, B, 128])
        stats, mv, col = sb("l0_st", [128, 3, 4, 6]), sb("l0_mv", [128, 3, 2]), sb("l0_col", [128, 3, 6])
        bank0 = (0, 4, 0)

        @block.sync
        def _(sp):
            load_weights(k, i + 1)

        @block.tensor
        def _(pe):
            w_ready(pe)
            for j, n in enumerate(("wq", "wk", "wv")):
                if j == 2:
                    pe.wait_ge(s("sig"), 4)
                for c in range(4):
                    pe.matmul(P[:, bank0[j] + c, :], w[n], k.XT[:, N * c:N * (c + 1)], start=True, stop=True).then_inc(s("proj"), 1)
            pe.wait_ge(s("sig"), 12)
            for b in range(B):
                for t in range(QT):
                    last = pe.transpose(P[:, 4 + b, 128 * t:128 * (t + 1)], S[2][:, N * b + 128 * t:N * b + 128 * (t + 1)], k.ident[:])
                last.then_inc(s("vt"), 1)
            for b in range(B):
                pe.wait_ge(s("vt_copied"), b + 1)
                for t in range(QT):
                    last = pe.matmul(P[:, 0, 128 * b:128 * (b + 1)], VT[:, QT * b + t, :], VT[:, QT * b + t, :], start=t == 0, stop=t == QT - 1)
            last.then_inc(s("gram"), 1)
            pe.wait_ge(s("gram_masked"), 1)
            for b in range(B):
                last = pe.matmul(P[:, 1, 128 * b:128 * (b + 1)], G[:, b, :], w["wp"], start=True, stop=True)
            last.then_inc(s("m"), 1)
            pe.wait_ge(s("m_copied"), 1)
            pe.wait_ge(s("qk"), 4)
            for b in range(B):
                for t in range(QT):
                    o = P[:, 4 + b, 128 * t:128 * (t + 1)]
                    pe.matmul(o, S[0][:, N * b + 128 * t:N * b + 128 * (t + 1)], M[:, b, :], start=True, stop=False)
                    last = pe.matmul(o, k.ones[0:1, 0:128], w["bp"], start=False, stop=True)
                last.then_inc(s("y"), 1)

        @block.vector
        def _(v):
            w_ready(v)
            for j in range(3):
                for c in range(4):
                    v.wait_ge(s("proj"), 4 * j + c + 1)
                    v.bn_stats(stats[:, j, c, :], P[:, bank0[j] + c, :]).then_inc(s("stats"), 1)
                v.wait_ge(s("stats"), 4 * j + 4)
                v.bn_aggr(mv[:, j, :], stats[:, j, :, :].rearrange("p c s -> p (c s)")).then_inc(s("small"), 1)
                v.wait_ge(s("small"), 5 * j + 1)
                v.tensor_scalar(col[:, j, 0:1], mv[:, j, 1:2], 1e-5, None, ALU.add).then_inc(s("small"), 1)
                v.wait_ge(s("small"), 5 * j + 2)
                v.reciprocal(col[:, j, 1:2], col[:, j, 0:1]).then_inc(s("inv"), 1)
                v.wait_ge(s("root"), j + 1)
                v.tensor_scalar(col[:, j, 3:4], col[:, j, 2:3], w["gam"][:, j:j + 1], 4.0, ALU.mult, ALU.mult).then_inc(s("small"), 1)
                v.wait_ge(s("small"), 5 * j + 3)
                v.tensor_scalar(col[:, j, 4:5], mv[:, j, 0:1], col[:, j, 3:4], -1.0, ALU.mult, ALU.mult).then_inc(s("small"), 1)
                v.wait_ge(s("small"), 5 * j + 4)
                v.scalar_tensor_tensor(col[:, j, 5:6], w["bet"][:, j:j + 1], 4.0, col[:, j, 4:5], ALU.mult, ALU.add).then_inc(s("small"), 1)
                v.wait_ge(s("small"), 5 * j + 5)
                v.tensor_scalar(col[:, j, 5:6], col[:, j, 5:6], -4.0, None, ALU.add).then_inc(s("affine"), 1)
            for c in range(4):
                v.wait_ge(s("sig"), 8)
                cs = slice(N * c, N * (c + 1))
                v.scalar_tensor_tensor(S[0][:, cs], S[0][:, cs], 8 ** -0.5, S[1][:, cs], ALU.mult, ALU.mult).then_inc(s("qk"), 1)
            for b in range(B):
                v.wait_ge(s("vt"), b + 1)
                v.tensor_copy(VT[:, QT * b:QT * (b + 1), :].rearrange("p t d -> p (t d)"), P[:, 4 + b, :]).then_inc(s("vt_copied"), 1)
            v.wait_ge(s("gram"), 1)
            v.tensor_tensor(G[:], P[:, 0, :].rearrange("p (b d) -> p b d", b=B), w["blocks"].unsqueeze(1).to_broadcast([128, B, 128]),
                            ALU.mult).then_inc(s("gram_masked"), 1)
            v.wait_ge(s("m"), 1)
            v.tensor_copy(M[:].rearrange("p b d -> p (b d)"), P[:, 1, :]).then_inc(s("m_copied"), 1)
            for b in range(B):
                v.wait_ge(s("y"), b + 1)
                x = k.X[:, QT * b:QT * (b + 1), :].rearrange("p t d -> p (t d)")
                v.tensor_tensor(x, x, P[:, 4 + b, :], ALU.add)

        @block.scalar
        def _(a):
            for j in range(3):
                a.wait_ge(s("inv"), j + 1)
                a.activation(col[:, j, 2:3], col[:, j, 1:2], ACT.Sqrt).then_inc(s("root"), 1)
                a.wait_ge(s("affine"), j + 1)
                for c in range(4):
                    a.activation(S[j][:, N * c:N * (c + 1)], P[:, bank0[j] + c, :], ACT.Sigmoid, scale=col[:, j, 3:4],
                                 bias=col[:, j, 5:6]).then_inc(s("sig"), 1)


def l0_ffn_attention(k, i):
    nc, P = k.nc, k.P
    w, w_ready = weights(k, i)
    pairs = [(q, t) for q in range(B) for t in range(q + 1)]
    first = [q * (q + 1) // 2 for q in range(B + 1)]
    with ExitStack() as st, phase(k) as (block, s):
        sb = lambda n, sh: st.enter_context(nc.sbuf_tensor(n, sh, F32))
        QKV = sb("f_qkv", [128, 2, B, 384])
        PR, SC, RD = sb("f_pr", [128, len(pairs), 128]), sb("f_sc", [128, len(pairs), NH]), sb("f_rd", [128, B, NH])
        MX, O, OT = sb("f_mx", [128, B, NH]), sb("f_o", [128, 2, B, 128]), sb("f_ot", [128, 2, N])

        @block.sync
        def _(sp):
            load_weights(k, i + 1)

        @block.tensor
        def _(pe):
            w_ready(pe)

            def qkv(r):
                if r >= 1:
                    pe.wait_ge(s("qkv_copied"), 4 * r)
                for q in range(B):
                    t = QT * q + r
                    pe.matmul(P[:, q, 0:384], k.XT[:, 128 * t:128 * (t + 1)], w["wqkv"], start=True, stop=True).then_inc(s("qkv"), 1)

            qkv(0)
            for r in range(QT):
                if r + 1 < QT:
                    qkv(r + 1)
                pe.wait_ge(s("o"), r + 1)
                for q in range(B):
                    last = pe.transpose(P[:, 4, 128 * q:128 * (q + 1)], O[:, r % 2, q, :], k.ident[:])
                last.then_inc(s("ot"), 1)
                pe.wait_ge(s("ot_copied"), r + 1)
                if r >= 1:
                    pe.wait_ge(s("added"), r)
                for q in range(B):
                    last = pe.matmul(P[:, 5, 128 * q:128 * (q + 1)], OT[:, r % 2, 128 * q:128 * (q + 1)], w["wo"], start=True, stop=True)
                last.then_inc(s("y"), 1)

        @block.scalar
        def _(a):
            def copies(r):
                if r >= 2:
                    a.wait_ge(s("o"), r - 1)
                for q in range(B):
                    a.wait_ge(s("qkv"), 4 * r + q + 1)
                    a.activation(QKV[:, r % 2, q, :], P[:, q, 0:384], ACT.Copy).then_inc(s("qkv_copied"), 1)

            copies(0)
            for r in range(QT):
                if r + 1 < QT:
                    copies(r + 1)
                a.wait_ge(s("shifted"), r + 1)
                a.activation(SC[:], SC[:], ACT.Exp, scale=8 ** -0.5).then_inc(s("exp"), 1)
                a.wait_ge(s("ot"), r + 1)
                a.activation(OT[:, r % 2, :], P[:, 4, :], ACT.Copy).then_inc(s("ot_copied"), 1)

        @block.vector
        def _(v):
            n = [0]

            def step(ins):
                n[0] += 1
                ins.then_inc(s("step"), 1)
                v.wait_ge(s("step"), n[0])

            for r in range(QT):
                v.wait_ge(s("qkv_copied"), 4 * r + 4)
                for q in range(B):
                    m = q + 1
                    last = v.tensor_tensor(PR[:, first[q]:first[q + 1], :],
                                           QKV[:, r % 2, q:q + 1, 0:128].to_broadcast([128, m, 128]),
                                           QKV[:, r % 2, 0:m, 128:256], ALU.mult)
                step(last)
                step(v.tensor_reduce(SC[:], PR[:].rearrange("p n (h d) -> p n h d", d=8), AX.X, ALU.add))
                for q in range(B):
                    last = v.tensor_reduce(MX[:, q, :], SC[:, first[q]:first[q + 1], :].rearrange("p t h -> p h t"), AX.X, ALU.max)
                step(last)
                for q in range(B):
                    m = q + 1
                    sc = SC[:, first[q]:first[q + 1], :]
                    last = v.tensor_tensor(sc, sc, MX[:, q:q + 1, :].to_broadcast([128, m, NH]), ALU.subtract)
                last.then_inc(s("shifted"), 1)
                v.wait_ge(s("exp"), r + 1)
                for q in range(B):
                    last = v.tensor_reduce(RD[:, q, :], SC[:, first[q]:first[q + 1], :].rearrange("p t h -> p h t"), AX.X, ALU.add)
                step(last)
                v.reciprocal(RD[:], RD[:])
                for q in range(B):
                    m = q + 1
                    o = PR[:, first[q]:first[q + 1], :].rearrange("p t (h d) -> p t h d", d=8)
                    last = v.tensor_tensor(o, SC[:, first[q]:first[q + 1], :].unsqueeze(3).to_broadcast([128, m, NH, 8]),
                                           QKV[:, r % 2, 0:m, 256:384].rearrange("p t (h d) -> p t h d", d=8), ALU.mult)
                step(last)
                if r >= 2:
                    v.wait_ge(s("ot"), r - 1)
                for q in range(B):
                    last = v.tensor_reduce(O[:, r % 2, q, :], PR[:, first[q]:first[q + 1], :].rearrange("p t x -> p x t"), AX.X, ALU.add)
                step(last)
                o = O[:, r % 2, :, :].rearrange("p q (h d) -> p (q h) d", d=8)
                v.tensor_tensor(o, o, RD[:].rearrange("p q h -> p (q h)").unsqueeze(2).to_broadcast([128, B * NH, 8]), ALU.mult).then_inc(s("o"), 1)
                v.wait_ge(s("y"), r + 1)
                tiles = lambda t: t[:, r::QT, :]
                v.tensor_tensor(tiles(k.Hs), tiles(k.X), P[:, 5, :].rearrange("p (q d) -> p q d", d=128), ALU.add).then_inc(s("added"), 1)


def l1_attn(k, i):
    nc, P = k.nc, k.P
    w, w_ready = weights(k, i)
    NS = 16
    with ExitStack() as st, phase(k) as (block, s):
        sb = lambda n, sh: st.enter_context(nc.sbuf_tensor(n, sh, F32))
        XC, C1, C2, XS = sb("m_xc", [128, N + 2]), sb("m_c1", [128, N]), sb("m_c2", [128, N]), sb("m_xs", [128, N])
        AB, RE, DT, DTX, Z = (sb(f"m_{n}", [128, N]) for n in ("ab", "re", "dt", "dtx", "z"))
        DA, BX, H, HC = (sb(f"m_{n}", [128, 2, N]) for n in ("da", "bxx", "h", "hc"))
        YZ = sb("m_yz", [128, N])
        BC, MID = sb("m_bc", [32, N]), st.enter_context(nc.sbuf_tensor("m_mid", [32, N], BF16))
        PARTS_BC, PICK = (st.enter_context(nc.sbuf_tensor(n, sh, BF16)) for n, sh in (("m_parts", [96, N]), ("m_pick", [96, 32])))
        PB, PC, PY, PM = 0, 2, 4, 5

        @block.sync
        def _(sp):
            load_weights(k, i + 1)

        @block.gpsimd
        def _(g):
            g.memset(XC[:], 0.0).then_inc(s("edges"), 1)

        @block.tensor
        def _(pe):
            w_ready(pe)
            with pe.Fori(0, B) as b:
                x = k.XT[:, bass.ds(b * N, N)]
                pe.wait_ge(s("m_free"), 3 * b + 1)
                pe.matmul(P[:, PM, :], w["win"], x, start=True, stop=True).then_inc(s("m_full"), 1)
                pe.wait_ge(s("z_free"), b + 1)
                pe.matmul(P[:, PM + 1, :], w["wg"], x, start=True, stop=True).then_inc(s("z_full"), 1)
                pe.wait_ge(s("xs"), b + 1)
                pe.wait_ge(s("m_free"), 3 * b + 2)
                pe.matmul(P[:, PM, :], w["wdt"], XS[:], start=True, stop=True).then_inc(s("m_full"), 1)

                pe.matmul(P[0:32, 7, :], w["wbc"], XS[:], start=True, stop=True).then_inc(s("bc_full"), 1)
                pe.wait_ge(s("parts"), 5 * (b + 1) + 2)

                def b_row(n):
                    pe.wait_ge(s("bx"), NS * b + n + 1)
                    pe.matmul(P[:, PB + n % 2, :], PICK[:, n:n + 1].to_broadcast([96, 128]), PARTS_BC[:], start=True, stop=True).then_inc(s("b_full"), 1)

                b_row(0)
                for n in range(NS + 2):
                    if n + 1 < NS:
                        b_row(n + 1)
                    if n < NS:
                        pe.wait_ge(s("hc"), NS * b + n + 1)
                        pe.matmul(P[:, PC + n % 2, :], PICK[:, NS + n:NS + n + 1].to_broadcast([96, 128]), PARTS_BC[:], start=True, stop=True).then_inc(s("c_full"), 1)
                    if n >= 2:
                        m = n - 2
                        pe.wait_ge(s("hc"), NS * b + m + 3)
                        pe.matmul(P[:, PY, :], k.ident[:], HC[:, m % 2, :], start=m == 0, stop=m == NS - 1).then_inc(s("summed"), 1)
                pe.wait_ge(s("yz"), b + 1)
                pe.wait_ge(s("m_free"), 3 * b + 3)
                for t in range(QT):
                    o = P[:, PM, 128 * t:128 * (t + 1)]
                    pe.matmul(o, YZ[:, 128 * t:128 * (t + 1)], w["wout"], start=True, stop=False)
                    last = pe.matmul(o, k.ones[0:1, 0:128], w["bout"], start=False, stop=True)
                last.then_inc(s("m_full"), 1)

        @block.scalar
        def _(a):
            w_ready(a)
            a.sem_inc(s("z_free"), 1)
            with a.Fori(0, B) as b:
                a.wait_ge(s("conv"), b + 1)
                a.activation(XS[:], C1[:], ACT.Silu, bias=w["convb"]).then_inc(s("xs"), 1)
                a.wait_ge(s("z_full"), b + 1)
                a.activation(Z[:], P[:, PM + 1, :], ACT.Silu, bias=w["bg"]).then_inc(s("z_free"), 1)
                a.wait_ge(s("m_full"), 3 * b + 2)
                a.activation(AB[:], P[:, PM, :], ACT.Abs, bias=w["bdt"]).then_inc(s("abs"), 1)
                a.wait_ge(s("abs"), b + 1)
                a.activation(AB[:], AB[:], ACT.Exp, scale=-1.0).then_inc(s("ab"), 1)
                a.wait_ge(s("ab"), 2 * b + 1)
                a.activation(AB[:], AB[:], ACT.Ln, bias=1.0).then_inc(s("ab"), 1)
                a.wait_ge(s("dt"), b + 1)
                for n in range(NS):
                    a.wait_ge(s("scan"), NS * b + n + 1)
                    a.activation(DA[:, n % 2, :], DT[:], ACT.Exp, scale=w["a"][:, n:n + 1]).then_inc(s("da"), 1)

        @block.vector
        def _(v):
            w_ready(v)
            v.sem_inc(s("m_free"), 1)
            v.sem_inc(s("bx"), 2)
            v.sem_inc(s("hc"), 2)
            v.sem_inc(s("scan"), 2)
            v.sem_inc(s("summed"), 2)
            v.tensor_tensor(PICK[:], k.identb[0:96, 0:32], k.identb[0:96, 32:64], ALU.add).then_inc(s("parts"), 1)
            v.wait_ge(s("parts"), 1)
            v.tensor_tensor(PICK[:], PICK[:], k.identb[0:96, 64:96], ALU.add).then_inc(s("parts"), 1)
            v.wait_ge(s("edges"), 1)
            with v.Fori(0, B) as b:
                v.wait_ge(s("m_full"), 3 * b + 1)
                v.tensor_scalar(XC[:, 1:N + 1], P[:, PM, :], w["bin"], None, ALU.add).then_inc(s("m_free"), 1)
                v.wait_ge(s("m_free"), 3 * b + 2)
                cw = w["convw"]
                v.tensor_scalar(C1[:], XC[:, 0:N], cw[:, 0:1], None, ALU.mult).then_inc(s("own"), 1)
                v.wait_ge(s("own"), 3 * b + 1)
                v.scalar_tensor_tensor(C2[:], XC[:, 1:N + 1], cw[:, 1:2], C1[:], ALU.mult, ALU.add).then_inc(s("own"), 1)
                v.wait_ge(s("own"), 3 * b + 2)
                v.scalar_tensor_tensor(C1[:], XC[:, 2:N + 2], cw[:, 2:3], C2[:], ALU.mult, ALU.add).then_inc(s("conv"), 1)
                v.wait_ge(s("m_full"), 3 * b + 2)
                v.wait_ge(s("abs"), b + 1)
                v.tensor_scalar(RE[:], P[:, PM, :], w["bdt"], 0.0, ALU.add, ALU.max).then_inc(s("m_free"), 1)
                v.wait_ge(s("m_free"), 3 * b + 3)
                v.wait_ge(s("bc_full"), b + 1)
                bc = P[0:32, 7, :]
                v.tensor_copy(PARTS_BC[0:32, :], bc).then_inc(s("parts"), 1)
                v.wait_ge(s("parts"), 5 * b + 3)
                v.tensor_tensor(BC[:], bc, PARTS_BC[0:32, :], ALU.subtract).then_inc(s("parts"), 1)
                v.wait_ge(s("parts"), 5 * b + 4)
                v.tensor_copy(MID[:], BC[:]).then_inc(s("parts"), 1)
                v.wait_ge(s("parts"), 5 * b + 5)
                v.tensor_copy(PARTS_BC[32:64, :], MID[:]).then_inc(s("parts"), 1)
                v.tensor_tensor(PARTS_BC[64:96, :], BC[:], MID[:], ALU.subtract).then_inc(s("parts"), 1)
                v.wait_ge(s("ab"), 2 * b + 2)
                v.tensor_tensor(DT[:], RE[:], AB[:], ALU.add).then_inc(s("dt"), 1)
                v.wait_ge(s("dt"), b + 1)
                v.tensor_tensor(DTX[:], DT[:], XS[:], ALU.mult).then_inc(s("own"), 1)
                v.wait_ge(s("own"), 3 * b + 3)

                def inp(n):
                    v.wait_ge(s("b_full"), NS * b + n + 1)
                    v.scalar_tensor_tensor(BX[:, n % 2, :], P[:, PB + n % 2, :], w["bb"][:, n:n + 1], DTX[:], ALU.add, ALU.mult).then_inc(s("bx"), 1)

                def out(n):
                    v.wait_ge(s("c_full"), NS * b + n + 1)
                    v.wait_ge(s("scan"), NS * b + n + 3)
                    v.wait_ge(s("summed"), NS * b + n + 1)
                    v.scalar_tensor_tensor(HC[:, n % 2, :], P[:, PC + n % 2, :], w["bc"][:, n:n + 1], H[:, n % 2, :], ALU.add, ALU.mult).then_inc(s("hc"), 1)

                inp(0)
                for n in range(NS):
                    v.wait_ge(s("da"), NS * b + n + 1)
                    v.wait_ge(s("bx"), NS * b + n + 3)
                    v.wait_ge(s("hc"), NS * b + n + 1)
                    v.tensor_tensor_scan(H[:, n % 2, :], DA[:, n % 2, :], BX[:, n % 2, :], 0.0, ALU.mult, ALU.add).then_inc(s("scan"), 1)
                    if n + 1 < NS:
                        inp(n + 1)
                    if n >= 1:
                        out(n - 1)
                out(NS - 1)
                v.wait_ge(s("summed"), NS * (b + 1) + 2)
                v.tensor_tensor(YZ[:], P[:, PY, :], Z[:], ALU.mult).then_inc(s("yz"), 1)
                v.wait_ge(s("m_full"), 3 * b + 3)
                x = k.X[:, bass.ds(b * QT, QT), :]
                v.tensor_tensor(x, x, P[:, PM, :].rearrange("p (t d) -> p t d", d=D), ALU.add).then_inc(s("m_free"), 1)


def l3_attn(k, i):
    nc, P = k.nc, k.P
    w, w_ready = weights(k, i)
    SC = 128 ** -0.5
    with ExitStack() as st, phase(k) as (block, s):
        sb = lambda n, sh: st.enter_context(nc.sbuf_tensor(n, sh, F32))
        PK, E, WT = (sb(f"a_{n}", [128, B, QT, 128]) for n in ("pk", "e", "wt"))
        MX, SM, GQ, GK, WR, WM = sb("a_mx", [128, 2, B, QT]), sb("a_sm", [128, 2, B, QT]), sb("a_gq", [128, B, 128]), \
            sb("a_gk", [128, B]), sb("a_wr", [128, B, 128]), sb("a_wm", [128, B, 128])

        @block.sync
        def _(sp):
            load_weights(k, i + 1)

        @block.tensor
        def _(pe):
            w_ready(pe)
            for n, bank in (("wq", 0), ("wk", 4)):
                for b in range(B):
                    for t in range(QT):
                        last = pe.matmul(P[:, bank + b, 128 * t:128 * (t + 1)], k.XT[:, N * b + 128 * t:N * b + 128 * (t + 1)], w[n], start=True, stop=True)
                    last.then_inc(s("proj"), 1)
            for b in range(B):
                pe.wait_ge(s("weighted"), b + 1)
                for t in range(QT):
                    last = pe.matmul(P[:, b, 0:128], k.ones[:, 0:128], WT[:, b, t, :], start=t == 0, stop=t == QT - 1)
                last.then_inc(s("gq"), 1)
            for b in range(B):
                pe.wait_ge(s("weighted"), B + b + 1)
                for t in range(QT):
                    last = pe.matmul(P[:, b, 128:129], WT[:, b, t, :], k.ones[:, 0:1], start=t == 0, stop=t == QT - 1)
                last.then_inc(s("gk"), 1)
            for b in range(B):
                pe.wait_ge(s("wr"), b + 1)
                pe.matmul(P[:, b, 256:384], w["wvt"], WR[:, b, :], start=True, stop=True).then_inc(s("m"), 1)
            for b in range(B):
                pe.wait_ge(s("wm"), b + 1)
                for t in range(QT):
                    last = pe.matmul(P[:, 4 + b, 128 * t:128 * (t + 1)], k.XT[:, N * b + 128 * t:N * b + 128 * (t + 1)], WM[:, b, :], start=True, stop=True)
                last.then_inc(s("y"), 1)

        @block.scalar
        def _(a):
            for n in range(2 * B):
                a.wait_ge(s("shifted"), n + 1)
                a.activation(E[:, n % B, :, :], E[:, n % B, :, :], ACT.Exp, scale=SC).then_inc(s("exp"), 1)

        @block.vector
        def _(v):
            w_ready(v)
            own = [0]

            def step(ins):
                own[0] += 1
                ins.then_inc(s("step"), 1)
                v.wait_ge(s("step"), own[0])

            over = lambda c: c.unsqueeze(2).to_broadcast([128, QT, 128])
            for j in range(2):
                for b in range(B):
                    if j == 0:
                        v.wait_ge(s("proj"), b + 1)
                        x = P[:, b, :].rearrange("p (t d) -> p t d", d=128)
                    else:
                        v.wait_ge(s("proj"), B + b + 1)
                        v.wait_ge(s("gq"), b + 1)
                        step(v.tensor_copy(GQ[:, b, :], P[:, b, 0:128]))
                        x = PK[:, b, :, :]
                        step(v.tensor_tensor(x, P[:, 4 + b, :].rearrange("p (t d) -> p t d", d=128),
                                             GQ[:, b:b + 1, :].to_broadcast([128, QT, 128]), ALU.mult))
                    step(v.tensor_reduce(MX[:, j, b, :], x, AX.X, ALU.max, negate=True))
                    v.tensor_tensor(E[:, b, :, :], x, over(MX[:, j, b, :]), ALU.add).then_inc(s("shifted"), 1)
                for b in range(B):
                    x = P[:, b, :].rearrange("p (t d) -> p t d", d=128) if j == 0 else PK[:, b, :, :]
                    v.wait_ge(s("exp"), B * j + b + 1)
                    step(v.tensor_reduce(SM[:, j, b, :], E[:, b, :, :], AX.X, ALU.add))
                    step(v.reciprocal(SM[:, j, b, :], SM[:, j, b, :]))
                    step(v.tensor_tensor(WT[:, b, :, :], x, over(SM[:, j, b, :]), ALU.mult))
                    v.tensor_tensor(WT[:, b, :, :], WT[:, b, :, :], E[:, b, :, :], ALU.mult).then_inc(s("weighted"), 1)
            for b in range(B):
                v.wait_ge(s("gk"), b + 1)
                step(v.tensor_copy(GK[:, b:b + 1], P[:, b, 128:129]))
                v.tensor_scalar(WR[:, b, :], w["wr"], GK[:, b:b + 1], None, ALU.mult).then_inc(s("wr"), 1)
            for b in range(B):
                v.wait_ge(s("m"), b + 1)
                v.tensor_tensor(WM[:, b, :], P[:, b, 256:384], w["wq"], ALU.add).then_inc(s("wm"), 1)
            for b in range(B):
                v.wait_ge(s("y"), b + 1)
                x = k.X[:, QT * b:QT * (b + 1), :].rearrange("p t d -> p (t d)")
                v.tensor_tensor(x, x, P[:, 4 + b, :], ALU.add)


def route(k, i, E, mode):
    nc, P = k.nc, k.P
    w, w_ready = weights(k, i)
    with ExitStack() as st, phase(k) as (block, s):
        sb = lambda n, sh: st.enter_context(nc.sbuf_tensor(n, sh, F32))
        k.serial += 1
        q = k.serial
        L, SCO, SEL = (sb(f"r_{n}_{q}", [128, TILES, E]) for n in ("l", "sco", "sel"))
        c1, c2 = (sb(f"r_{n}_{q}", [128, TILES, 1]) for n in ("c1", "c2"))
        T1, T2 = (sb(f"r_{n}_{q}", [128, TILES * E * max(E, 8)]) for n in ("t1", "t2"))
        GS, GM = (sb(f"r_{n}_{q}", [128, TILES, 4]) for n in ("gs", "gm"))
        WE = k.WE[:, :, 0:E]

        @block.tensor
        def _(pe):
            w_ready(pe)
            for t in range(TILES):
                last = pe.matmul(P[:, 0, E * t:E * (t + 1)], k.XT[:, 128 * t:128 * (t + 1)], w["router"], start=True, stop=True)
            last.then_inc(s("logits"), 1)

        @block.scalar
        def _(a):
            a.wait_ge(s("shifted"), 1)
            a.activation(SCO[:], L[:], ACT.Sigmoid if mode == "groups" else ACT.Exp).then_inc(s("exp"), 1)

        @block.vector
        def _(v):
            own = [0]

            def step(ins):
                own[0] += 1
                ins.then_inc(s("step"), 1)
                v.wait_ge(s("step"), own[0])

            def choose(x, m, n, top, out):
                t1 = T1[:, 0:m * n * n].rearrange("p (m i j) -> p m i j", i=n, j=n)
                t2 = T2[:, 0:m * n * n].rearrange("p (m i j) -> p m i j", i=n, j=n)
                xj = x.unsqueeze(2).to_broadcast([128, m, n, n])
                xi = x.unsqueeze(3).to_broadcast([128, m, n, n])
                earlier = k.before[:, 0:n, 0:n].unsqueeze(1).to_broadcast([128, m, n, n])
                v.tensor_tensor(t2, xj, xi, ALU.is_gt)
                step(v.tensor_tensor(t1, xj, xi, ALU.is_ge))
                step(v.tensor_tensor(t1, t1, earlier, ALU.mult))
                step(v.tensor_tensor(t1, t1, t2, ALU.max))
                step(v.tensor_reduce(out, t1, AX.X, ALU.add))
                step(v.tensor_scalar(out, out, top - 0.5, None, ALU.is_lt))

            def per(c, n=E):
                return c.to_broadcast([128, TILES, n])

            v.wait_ge(s("logits"), 1)
            lg = P[:, 0, 0:TILES * E].rearrange("p (t e) -> p t e", e=E)
            if mode == "groups":
                v.tensor_copy(L[:], lg).then_inc(s("shifted"), 1)
                v.wait_ge(s("exp"), 1)
                w_ready(v)
                step(v.tensor_tensor(L[:], SCO[:], w["ebias"].unsqueeze(1).to_broadcast([128, TILES, E]), ALU.add))
                x4 = L[:].rearrange("p t (g e) -> p (t g) e", e=4)
                sel4 = SEL[:].rearrange("p t (g e) -> p (t g) e", e=4)
                choose(x4, TILES * 4, 4, 2, sel4)
                step(v.tensor_tensor(sel4, sel4, x4, ALU.mult))
                step(v.tensor_reduce(GS[:].rearrange("p t g -> p (t g)"), sel4, AX.X, ALU.add))
                choose(GS[:], TILES, 4, 2, GM[:])
                step(v.tensor_tensor(x4, x4, GM[:].rearrange("p t g -> p (t g)").unsqueeze(2).to_broadcast([128, TILES * 4, 4]), ALU.mult))
                choose(L[:], TILES, E, 4, SEL[:])
                step(v.tensor_tensor(SEL[:], SEL[:], SCO[:], ALU.mult))
                step(v.tensor_reduce(c1[:, :, 0], SEL[:], AX.X, ALU.add))
                step(v.tensor_scalar(c1[:], c1[:], 1e-20, None, ALU.add))
                step(v.reciprocal(c1[:], c1[:]))
                step(v.tensor_scalar(c1[:], c1[:], 2.5, None, ALU.mult))
                v.tensor_tensor(WE, SEL[:], per(c1[:]), ALU.mult)
                return
            step(v.tensor_reduce(c1[:, :, 0], lg, AX.X, ALU.max))
            v.tensor_tensor(L[:], lg, per(c1[:]), ALU.subtract).then_inc(s("shifted"), 1)
            v.wait_ge(s("exp"), 1)
            if mode == "plain":
                step(v.tensor_reduce(c1[:, :, 0], SCO[:], AX.X, ALU.add))
                choose(SCO[:], TILES, E, 2, SEL[:])
                step(v.tensor_tensor(SEL[:], SEL[:], SCO[:], ALU.mult))
            else:
                v.wait_ge(s("shifted"), 1)
                choose(L[:], TILES, E, 2, SEL[:])
                step(v.tensor_tensor(SEL[:], SEL[:], SCO[:], ALU.mult))
                step(v.tensor_reduce(c1[:, :, 0], SEL[:], AX.X, ALU.add))
            step(v.reciprocal(c2[:], c1[:]))
            v.tensor_tensor(WE, SEL[:], per(c2[:]), ALU.mult)


def experts(k, i, units, gated, func, hidden_in=None):
    nc, P = k.nc, k.P
    w, w_ready = weights(k, i)
    nb = len(units[0][0])
    n_up = sum(len(u[0]) for u in units)
    n_out = sum(len(u[1]) for u in units)
    with ExitStack() as st, phase(k) as (block, s):
        k.serial += 1
        sb = lambda n, sh: st.enter_context(nc.sbuf_tensor(f"{n}_{k.serial}", sh, F32))
        HT = sb("e_h", [128, 2, nb, N])
        SG = sb("e_g", [128, 2, N])
        PG, PU, PY = 0, 2, 4

        @block.tensor
        def _(pe):
            w_ready(pe)
            pe.sem_inc(s("down"), 2)
            with pe.Fori(0, 4) as c:
                x = k.XT[:, bass.ds(c * N, N)]
                nu, no, nh = [0], [0], [0]

                def up(u):
                    for col in units[u][0]:
                        j = nu[0]
                        nu[0] += 1
                        pe.wait_ge(s("act"), n_up * c + j + 1)
                        pe.matmul(P[:, PG + j % 2, :], w["w1"][:, col:col + 128], x, start=True, stop=True).then_inc(s("gate"), 1)
                        if gated:
                            pe.wait_ge(s("hidden"), n_up * c + j + 1)
                            pe.matmul(P[:, PU + j % 2, :], w["w3"][:, col:col + 128], x, start=True, stop=True).then_inc(s("up"), 1)

                def down(u):
                    nh[0] += len(units[u][0])
                    if gated:
                        pe.wait_ge(s("hidden"), n_up * c + nh[0] + 2)
                    else:
                        pe.wait_ge(s("act"), n_up * c + nh[0] + 2)
                    for m, (_, parts) in enumerate(units[u][1]):
                        j = no[0]
                        no[0] += 1
                        pe.wait_ge(s("added"), n_out * c + j + 1)
                        for t in range(4):
                            for n, (blk, rows, w2) in enumerate(parts):
                                last = pe.matmul(P[:, PY + j % 2, 128 * t:128 * (t + 1)], HT[rows, u % 2, blk, 128 * t:128 * (t + 1)], w2,
                                                 start=n == 0, stop=n == len(parts) - 1)
                        last.then_inc(s("y"), 1)
                    pe.sem_inc(s("down"), 1)

                for u in range(len(units) + 1):
                    if u < len(units):
                        up(u)
                    if u >= 1:
                        down(u - 1)

        def half_free(eng, c, u):
            eng.wait_ge(s("down"), len(units) * c + u + 1)

        @block.scalar
        def _(a):
            a.sem_inc(s("act"), 2)
            with a.Fori(0, 4) as c:
                j = 0
                for u in range(len(units)):
                    if not gated:
                        half_free(a, c, u)
                    for blk in range(len(units[u][0])):
                        a.wait_ge(s("gate"), n_up * c + j + 1)
                        if gated:
                            a.wait_ge(s("hidden"), n_up * c + j + 1)
                        dst = SG[:, j % 2, :] if gated else HT[:, u % 2, blk, :]
                        a.activation(dst, P[:, PG + j % 2, :], func).then_inc(s("act"), 1)
                        j += 1

        @block.vector
        def _(v):
            v.sem_inc(s("hidden"), 2)
            if hidden_in is not None:
                v.tensor_tensor(k.X[:], k.X[:], hidden_in[:], ALU.add).then_inc(s("added"), 2)
            else:
                v.sem_inc(s("added"), 2)
            with v.Fori(0, 4) as c:
                j, jo = [0], [0]

                def hidden(u):
                    half_free(v, c, u)
                    for blk in range(len(units[u][0])):
                        v.wait_ge(s("act"), n_up * c + j[0] + 3)
                        v.wait_ge(s("up"), n_up * c + j[0] + 1)
                        v.tensor_tensor(HT[:, u % 2, blk, :], SG[:, j[0] % 2, :], P[:, PU + j[0] % 2, :], ALU.mult).then_inc(s("hidden"), 1)
                        j[0] += 1

                def out(u):
                    for e, _ in units[u][1]:
                        v.wait_ge(s("y"), n_out * c + jo[0] + 1)
                        v.wait_ge(s("added"), n_out * c + jo[0] + 2)
                        for t in range(4):
                            x = k.X[:, bass.ds(c * 4 + t, 1), :].rearrange("p a d -> p (a d)")
                            y = P[:, PY + jo[0] % 2, 128 * t:128 * (t + 1)]
                            if e is None:
                                last = v.tensor_tensor(x, x, y, ALU.add)
                            else:
                                last = v.scalar_tensor_tensor(x, y, k.WE[:, bass.ds(c * 4 + t, 1), e], x, ALU.mult, ALU.add)
                        last.then_inc(s("added"), 1)
                        jo[0] += 1

                for u in range(len(units) + 1):
                    if gated and u < len(units):
                        hidden(u)
                    if u >= 1:
                        out(u - 1)


ALL = slice(0, 128)


def expert_units(k, i, n, blocks):
    w, _ = weights(k, i)
    return [([128 * (blocks * e + f) for f in range(blocks)],
             [(e, [(f, ALL, w["w2"][:, 128 * (blocks * e + f):128 * (blocks * e + f + 1)]) for f in range(blocks)])]) for e in range(n)]


def l3_units(k, i):
    w, _ = weights(k, i)
    units = [([128 * p], [(2 * p + h, [(0, slice(64 * h, 64 * h + 64), w["w2"][64 * h:64 * h + 64, 128 * p:128 * (p + 1)])]) for h in range(2)])
             for p in range(8)]
    return units + [([1024], [(None, [(0, ALL, w["w2"][:, 1024:1152])])])]


def begin(k, i):
    nc, P = k.nc, k.P
    with phase(k) as (block, s):
        @block.sync
        def _(sp):
            sp.dma_start(k.X[:], k.x_in).then_inc(s("x"), 16)
            load_weights(k, i)

        @block.scalar
        def _(a):
            a.dma_start(k.cst[:], k.const_in).then_inc(s("const"), 16)
            a.dma_start(k.CT[:], k.ctx_in).then_inc(s("ctx"), 16)
            a.wait_ge(s("ctx"), 16)

        @block.gpsimd
        def _(g):
            g.memset(k.ones[:], 1.0)

        @block.tensor
        def _(pe):
            pe.wait_ge(s("x"), 16)
            pe.wait_ge(s("const"), 16)
            for c in range(4):
                for t in range(4):
                    last = pe.transpose(P[:, c, 128 * t:128 * (t + 1)], k.X[:, 4 * c + t, :], k.ident[:])
                last.then_inc(s("turned"), 1)

        @block.vector
        def _(v):
            v.wait_ge(s("const"), 16)
            v.tensor_copy(k.identb[:], k.ident[:])
            v.tensor_copy(k.maskq[:], k.cst[:, 128:256])
            v.tensor_copy(k.maskk[:], k.cst[:, 256:384])
            v.tensor_copy(k.pick[:], k.max_rows.to_broadcast([128, CTX]))
            for c in range(4):
                v.wait_ge(s("turned"), c + 1)
                v.tensor_copy(k.XT[:, N * c:N * (c + 1)], P[:, c, :])


def build(nc, x, const, ctx, kaug, sel, wd, where, out):
    k = Ctx()
    k.sel_in = sel
    k.nc, k.x_in, k.const_in, k.ctx_in, k.kaug, k.wd, k.where, k.out, k.serial = nc, x, const, ctx, kaug, wd, where, out, 0
    sb = lambda n, sh, dt=F32: nc.alloc_sbuf_tensor(n, sh, dt)
    k.X, k.XT = sb("X", [128, TILES, D]), sb("XT", [128, TOK])
    k.W = [sb(f"W{n}", [128, max([w.shape[1] for j, w in enumerate(wd) if j % 2 == n])]) for n in range(2)]
    k.XB, k.CB, k.CI, k.CT = sb("XB", [128, N]), sb("CB", [CD, CTX]), sb("CI", [CD, CTX]), sb("CT", [CD, 3, B * CTX])
    k.cst = sb("cst", [128, 641])
    k.ident, k.before = k.cst[:, 0:128], k.cst[:, 384:640].rearrange("p (i j) -> p i j", j=16)
    k.max_rows, k.pick = k.cst[:, 640:641], sb("pick", [128, CTX], BF16)
    k.identb, k.maskq, k.maskk = sb("identb", [128, 128], BF16), sb("maskq", [128, 128], BF16), sb("maskk", [128, 128], BF16)
    k.ones, k.warm = sb("ones", [128, 128]), sb("warm", [1, 1])
    k.P = nc.alloc_psum_tensor("P", [128, 8, 512], F32)
    k.pool = [nc.alloc_semaphore(f"count{n}") for n in range(24)]
    k.w_loaded = [nc.alloc_semaphore(f"weights_{n}") for n in STAGES]

    k.stored = nc.alloc_semaphore("stored")

    begin(k, FIRST)
    for i in range(FIRST, LAST):
        with ExitStack() as st:
            if STAGES[i] in ("L0_ffn", "L1_ffn", "L2_ffn"):
                k.Hs = st.enter_context(nc.sbuf_tensor(f"Hs{i}", [128, TILES, D], F32))
            if "ffn" in STAGES[i]:
                k.WE = st.enter_context(nc.sbuf_tensor(f"WE{i}", [128, TILES, 16], F32))
            run_stage(k, i, STAGES[i])
            normalise(k, i, k.X, k.X, 1e-5, store=i == LAST - 1)


def run_stage(k, i, name):
    nc = k.nc
    if name == "L0_attn":
        l0_attn(k, i)
    elif name == "L0_xattn":
        l0_xattn(k, i)
    elif name == "L0_ffn":
        with nc.sbuf_tensor("NX0", [128, TILES, D], F32) as nx:
            normalise(k, i, k.X, nx, 1e-5, scale="n1w", shift="n1b")
            l0_ffn_attention(k, i)
            normalise(k, i, k.Hs, nx, 1e-5, scale="n2w", shift="n2b")
        route(k, i, 8, "plain")
        experts(k, i, expert_units(k, i, 8, 2), False, ACT.Gelu_apprx_tanh, hidden_in=k.Hs)
    elif name == "L1_attn":
        l1_attn(k, i)
    elif name == "L1_xattn":
        l1_xattn(k, i)
    elif name == "L1_ffn":
        with nc.sbuf_tensor("NX1", [128, TILES, D], F32) as nx:
            normalise(k, i, k.X, nx, 1e-5, rms=True, scale="n1w")
        ffn_attention(k, i, False, False, 1)
        with nc.sbuf_tensor("NX2", [128, TILES, D], F32) as nx:
            normalise(k, i, k.Hs, nx, 1e-5, rms=True, scale="n2w")
        route(k, i, 8, "shares")
        experts(k, i, expert_units(k, i, 8, 2), True, ACT.Silu, hidden_in=k.Hs)
    elif name == "L2_attn":
        l2_attn(k, i)
    elif name == "L2_xattn":
        l2_xattn(k, i)
    elif name == "L2_ffn":
        eps = 1.1920928955078125e-07
        with nc.sbuf_tensor("NX3", [128, TILES, D], F32) as nx:
            normalise(k, i, k.X, nx, eps, rms=True, scale="n1w")
        ffn_attention(k, i, True, True, 4)
        with nc.sbuf_tensor("NX4", [128, TILES, D], F32) as nx:
            normalise(k, i, k.Hs, nx, eps, rms=True, scale="n2w")
        route(k, i, 4, "shares")
        experts(k, i, expert_units(k, i, 4, 3), True, ACT.Silu, hidden_in=k.Hs)
    elif name == "L3_attn":
        l3_attn(k, i)
    elif name == "L3_xattn":
        l3_xattn(k, i)
    else:
        route(k, i, 16, "groups")
        experts(k, i, l3_units(k, i), True, ACT.Silu)


def tokens_down(x):
    return np.ascontiguousarray(x.reshape(TILES, 128, D).transpose(1, 0, 2).reshape(128, TILES * D))


def kernel(**inputs):
    import concourse.bacc as _bacc
    from concourse.bass_utils import run_bass_kernel_spmd as _run

    a = {n: np.asarray(v) for n, v in inputs.items()}
    nc = _bacc.Bacc("TRN2", target_bir_lowering=False, num_devices=1)
    ctx = a["ctx_768"].transpose(2, 0, 1)
    org, ipa = np.zeros_like(ctx), np.zeros_like(ctx)
    org[:, :, :CTX - IPA] = ctx[:, :, :CTX - IPA]
    ipa[:, :, CTX - IPA:] = ctx[:, :, CTX - IPA:]
    arrays = {"x": tokens_down(a["x"]), "const": constants(), "ctx": np.concatenate([t.reshape(CD, B * CTX) for t in (ctx, org, ipa)], 1)}
    where = []
    for n in STAGES:
        arrays[f"w_{n}"], wh = pack(n, a)
        where.append(wh)
    for n, v in zip(("kaug_l2a", "kaug_l2x", "kaug_l3x"), key_rows()):
        arrays[n] = v
    arrays = {n: np.ascontiguousarray(v) for n, v in arrays.items()}
    for n, side in (("select_q", 0), ("select_k", 1)):
        arrays[n] = stacking(side)
    d = {n: nc.dram_tensor(f"in_{n}", v.shape, mybir.dt.uint16 if n.startswith("select") else F32, kind="ExternalInput").ap() for n, v in arrays.items()}
    out = nc.dram_tensor("out_0", (128, TILES * D), F32, kind="ExternalOutput").ap()
    tiled = lambda p: p.rearrange("p (t d) -> p t d", d=D)
    kaug = [d["kaug_l2a"].rearrange("a (h k) -> a h k", k=N), d["kaug_l2x"].rearrange("a (h k) -> a h k", k=CTX),
            d["kaug_l3x"].rearrange("a (h k) -> a h k", k=CTX)]
    build(nc, tiled(d["x"]), d["const"], d["ctx"].rearrange("c (s k) -> c s k", s=3), kaug, [d["select_q"].bitcast(BF16), d["select_k"].bitcast(BF16)], [d[f"w_{n}"] for n in STAGES], where, tiled(out))
    r = _run(nc, [{f"in_{n}": v for n, v in arrays.items()}], core_ids=[0])
    o = r.results[0]["out_0"]
    return o.reshape(128, TILES, D).transpose(1, 0, 2).reshape(B, N, D)
```
